# Optimizing a Trainium2 kernel written in Bass

```python
import numpy as np
import jax
import jax.numpy as jnp

def _softmax(x, axis=-1):
    return jax.nn.softmax(x, axis=axis)

def _gelu(x):
    return jax.nn.gelu(x, approximate=True)

def _silu(x):
    return jax.nn.silu(x)

def _sigmoid(x):
    return jax.nn.sigmoid(x)

def _layernorm(x, axis=-1, eps=1e-05):
    m = jnp.mean(x, axis=axis, keepdims=True)
    v = jnp.var(x, axis=axis, keepdims=True)
    return (x - m) / jnp.sqrt(v + eps)

def _scatter_add(tgt, idx, src, axis=0):
    return tgt.at[idx].add(src)

def _segment_sum(src, seg, n):
    return jax.ops.segment_sum(src, seg, n)
kernel_name = 'mk_adaln_d2_jaxref_r8_d8c63c'

def setup_inputs(seed: int=0):
    np.random.seed(seed)
    _w = jnp.asarray

    def _L0_attn_setup():
        import math
        import jax, jax.numpy as jnp
        import numpy as np
        B, T, C, H = (8, 128, 128, 16)
        HD = C // H
        key = jax.random.key(seed)
        ks = jax.random.split(key, 7)
        return {'x': jax.random.normal(ks[0], (B, T, C), dtype=jnp.float32), 'Wattn': jax.random.normal(ks[1], (C, 3 * C), dtype=jnp.float32) * 0.02, 'battn': jax.random.normal(ks[2], (3 * C,), dtype=jnp.float32) * 0.02, 'Wproj': jax.random.normal(ks[3], (C, C), dtype=jnp.float32) * 0.02, 'bproj': jax.random.normal(ks[4], (C,), dtype=jnp.float32) * 0.02, 'embk': jax.random.normal(ks[5], (T, HD), dtype=jnp.float32) * 0.02, 'embv': jax.random.normal(ks[6], (T, HD), dtype=jnp.float32) * 0.02}
    _L0_attn_in = _L0_attn_setup()

    def _L0_ffn_setup():
        import jax, jax.numpy as jnp
        import numpy as np
        N_EXP = 8
        TOP_K = 2
        CAPACITY_FACTOR = 1.25
        key = jax.random.key(seed)
        ks = jax.random.split(key, 5)
        B, T, D = (4, 128, 128)
        H = 4 * D
        E = N_EXP
        x = jax.random.normal(ks[0], (B, T, D), jnp.float32)
        gate_w = jax.random.normal(ks[1], (D, E), jnp.float32) * 0.02
        c_fc = jax.random.normal(ks[2], (E, D, H), jnp.float32) * 0.02
        fc_bias = jnp.zeros((E, 1, H), jnp.float32)
        c_proj = jax.random.normal(ks[3], (E, H, D), jnp.float32) * 0.02
        proj_bias = jnp.zeros((E, 1, D), jnp.float32)
        return dict(x=x, gate_w=gate_w, c_fc=c_fc, fc_bias=fc_bias, c_proj=c_proj, proj_bias=proj_bias)
    _L0_ffn_in = _L0_ffn_setup()
    _L0_c = _w((lambda *s: np.random.randn(*s).astype(np.float32) * 0.05)(16, 128))
    _L0_wmod = _w((lambda *s: np.random.randn(*s).astype(np.float32) * 0.05)(128, 6 * 128) * 128 ** (-0.5))

    def _L1_attn_setup():
        import jax, jax.numpy as jnp
        import numpy as np
        import math
        D_MODEL = 128
        N_HEADS = 16
        SPARSITY = 0.3
        key = jax.random.key(seed)
        ks = jax.random.split(key, 12)
        B, S, D = (4, 256, D_MODEL)
        Dh = D // 2
        sc = 0.02
        inp = {'x': jax.random.normal(ks[0], (B, S, D), dtype=jnp.float32), 'wq': jax.random.normal(ks[1], (D, D), dtype=jnp.float32) * sc, 'bq': jnp.zeros((D,), jnp.float32), 'wk': jax.random.normal(ks[2], (D, D), dtype=jnp.float32) * sc, 'bk': jnp.zeros((D,), jnp.float32), 'wv': jax.random.normal(ks[3], (D, D), dtype=jnp.float32) * sc, 'bv': jnp.zeros((D,), jnp.float32), 'wo': jax.random.normal(ks[4], (D, D), dtype=jnp.float32) * sc, 'bo': jnp.zeros((D,), jnp.float32), 'wi1': jax.random.normal(ks[5], (Dh, D), dtype=jnp.float32) * sc, 'bi1': jnp.zeros((Dh,), jnp.float32), 'wi2': jax.random.normal(ks[6], (1, Dh), dtype=jnp.float32) * sc, 'bi2': jnp.zeros((1,), jnp.float32)}
        return inp
    _L1_attn_in = _L1_attn_setup()

    def _L1_ffn_setup():
        import jax, jax.numpy as jnp
        import numpy as np
        E, K = (8, 2)
        B, S, H, F = (2, 256, 128, 512)
        EPS = 1e-12

        def _expert_ffn(xf, Wi_e, bi_e, Wg_e, bg_e, Wo_e, bo_e, g_e, b_e):
            h = jax.nn.gelu(xf @ Wi_e + bi_e, approximate=False) * jax.nn.sigmoid(xf @ Wg_e + bg_e)
            r = xf + (h @ Wo_e + bo_e)
            mu = jnp.mean(r, axis=-1, keepdims=True)
            var = jnp.mean(jnp.square(r - mu), axis=-1, keepdims=True)
            return (r - mu) * jax.lax.rsqrt(var + EPS) * g_e + b_e
        key = jax.random.key(seed)
        ks = jax.random.split(key, 8)
        s = 0.02
        return {'x': jax.random.normal(ks[0], (B, S, H), jnp.float32), 'Wr': jax.random.normal(ks[1], (H, E), jnp.float32) * s, 'br': jnp.zeros((E,), jnp.float32), 'Wi': jax.random.normal(ks[2], (E, H, F), jnp.float32) * s, 'bi': jnp.zeros((E, F), jnp.float32), 'Wg': jax.random.normal(ks[3], (E, H, F), jnp.float32) * s, 'bg': jnp.zeros((E, F), jnp.float32), 'Wo': jax.random.normal(ks[4], (E, F, H), jnp.float32) * s, 'bo': jnp.zeros((E, H), jnp.float32), 'gamma': jnp.ones((E, H), jnp.float32), 'beta': jnp.zeros((E, H), jnp.float32)}
    _L1_ffn_in = _L1_ffn_setup()
    _L1_c = _w((lambda *s: np.random.randn(*s).astype(np.float32) * 0.05)(16, 128))
    _L1_wmod = _w((lambda *s: np.random.randn(*s).astype(np.float32) * 0.05)(128, 6 * 128) * 128 ** (-0.5))
    _d = {'L0_attn_x': _L0_attn_in['x'], 'L0_attn_Wattn': _L0_attn_in['Wattn'], 'L0_attn_battn': _L0_attn_in['battn'], 'L0_attn_Wproj': _L0_attn_in['Wproj'], 'L0_attn_bproj': _L0_attn_in['bproj'], 'L0_attn_embk': _L0_attn_in['embk'], 'L0_attn_embv': _L0_attn_in['embv'], 'L0_ffn_gate_w': _L0_ffn_in['gate_w'], 'L0_ffn_c_fc': _L0_ffn_in['c_fc'], 'L0_ffn_fc_bias': _L0_ffn_in['fc_bias'], 'L0_ffn_c_proj': _L0_ffn_in['c_proj'], 'L0_ffn_proj_bias': _L0_ffn_in['proj_bias'], 'L0_c': _L0_c, 'L0_wmod': _L0_wmod, 'L1_attn_wq': _L1_attn_in['wq'], 'L1_attn_bq': _L1_attn_in['bq'], 'L1_attn_wk': _L1_attn_in['wk'], 'L1_attn_bk': _L1_attn_in['bk'], 'L1_attn_wv': _L1_attn_in['wv'], 'L1_attn_bv': _L1_attn_in['bv'], 'L1_attn_wo': _L1_attn_in['wo'], 'L1_attn_bo': _L1_attn_in['bo'], 'L1_attn_wi1': _L1_attn_in['wi1'], 'L1_attn_bi1': _L1_attn_in['bi1'], 'L1_attn_wi2': _L1_attn_in['wi2'], 'L1_attn_bi2': _L1_attn_in['bi2'], 'L1_ffn_Wr': _L1_ffn_in['Wr'], 'L1_ffn_br': _L1_ffn_in['br'], 'L1_ffn_Wi': _L1_ffn_in['Wi'], 'L1_ffn_bi': _L1_ffn_in['bi'], 'L1_ffn_Wg': _L1_ffn_in['Wg'], 'L1_ffn_bg': _L1_ffn_in['bg'], 'L1_ffn_Wo': _L1_ffn_in['Wo'], 'L1_ffn_bo': _L1_ffn_in['bo'], 'L1_ffn_gamma': _L1_ffn_in['gamma'], 'L1_ffn_beta': _L1_ffn_in['beta'], 'L1_c': _L1_c, 'L1_wmod': _L1_wmod}
    _x0 = _d['L0_attn_x']
    _d['L0_attn_x'] = jax.random.normal(jax.random.fold_in(jax.random.key(seed), 1), (16, 256, 128), dtype=_x0.dtype)
    del _x0
    return _d

def reference(L0_attn_x, L0_attn_Wattn, L0_attn_battn, L0_attn_Wproj, L0_attn_bproj, L0_attn_embk, L0_attn_embv, L0_ffn_gate_w, L0_ffn_c_fc, L0_ffn_fc_bias, L0_ffn_c_proj, L0_ffn_proj_bias, L0_c, L0_wmod, L1_attn_wq, L1_attn_bq, L1_attn_wk, L1_attn_bk, L1_attn_wv, L1_attn_bv, L1_attn_wo, L1_attn_bo, L1_attn_wi1, L1_attn_bi1, L1_attn_wi2, L1_attn_bi2, L1_ffn_Wr, L1_ffn_br, L1_ffn_Wi, L1_ffn_bi, L1_ffn_Wg, L1_ffn_bg, L1_ffn_Wo, L1_ffn_bo, L1_ffn_gamma, L1_ffn_beta, L1_c, L1_wmod):

    def _L0_attn_ref(x, Wattn, battn, Wproj, bproj, embk, embv):
        import math
        import jax, jax.numpy as jnp
        import numpy as np
        B, T, C, H = (8, 128, 128, 16)
        HD = C // H
        b, t, c = x.shape
        qkv = x @ Wattn + battn
        q, k, v = jnp.split(qkv, 3, axis=-1)
        q = q.reshape(b, t, H, HD).transpose(0, 2, 1, 3)
        k = k.reshape(b, t, H, HD).transpose(0, 2, 1, 3)
        v = v.reshape(b, t, H, HD).transpose(0, 2, 1, 3)
        idx = jnp.arange(t)
        rel = jnp.tril(idx[:, None] - idx[None, :])
        rk = embk[rel]
        rv = embv[rel]
        scale = 1.0 / math.sqrt(HD)
        att1 = jnp.einsum('bhtd,bhsd->bhts', q, k) * scale
        att2 = jnp.einsum('bhtd,tsd->bhts', q, rk)
        att = att1 + att2
        causal = idx[None, :] <= idx[:, None]
        att = jnp.where(causal[None, None], att, -jnp.inf)
        att = jax.nn.softmax(att, axis=-1)
        y1 = jnp.einsum('bhts,bhsd->bhtd', att, v)
        y2 = jnp.einsum('bhts,tsd->bhtd', att, rv)
        y = (y1 + y2).transpose(0, 2, 1, 3).reshape(b, t, c)
        return y @ Wproj + bproj

    def _L0_ffn_ref(x, gate_w, c_fc, fc_bias, c_proj, proj_bias):
        import jax, jax.numpy as jnp
        import numpy as np
        N_EXP = 8
        TOP_K = 2
        CAPACITY_FACTOR = 1.25
        B, T, D = x.shape
        n = B * T
        E, k = (N_EXP, TOP_K)
        cap = int(CAPACITY_FACTOR * n * k / E)
        xt = x.reshape(n, D)
        logits = xt @ gate_w
        top_logits, top_idx = jax.lax.top_k(logits, k)
        masked = jnp.full_like(logits, -jnp.inf)
        masked = masked.at[jnp.arange(n)[:, None], top_idx].set(top_logits)
        router_probs = jax.nn.softmax(masked, axis=-1)
        exp_mask = jax.nn.one_hot(top_idx, E, dtype=jnp.int32)
        exp_mask = jnp.transpose(exp_mask, (1, 0, 2))
        exp_rank = jnp.cumsum(exp_mask.reshape(k * n, E), axis=0) - 1
        exp_rank = exp_rank.reshape(k, n, E)
        exp_mask = exp_mask * (exp_rank < cap).astype(jnp.int32)
        used_capacity = jnp.sum(exp_mask, axis=(0, 1))
        exp_rank = jnp.sum(exp_mask * exp_rank, axis=-1)
        exp_weights = exp_mask.astype(x.dtype) * router_probs[None]
        rank_oh = jax.nn.one_hot(exp_rank, cap, dtype=x.dtype)
        cb_weight = jnp.einsum('kne,knc->nec', exp_weights, rank_oh)
        sec_mask = (cb_weight != 0).astype(x.dtype)
        exp_batches = jnp.einsum('nec,nd->ecd', sec_mask, xt)
        h = jnp.einsum('ecd,edh->ech', exp_batches, c_fc) + fc_bias
        h = jax.nn.gelu(h, approximate=False)
        exp_out = jnp.einsum('ech,ehd->ecd', h, c_proj) + proj_bias
        out = jnp.einsum('nec,ecd->nd', cb_weight, exp_out)
        return out.reshape(B, T, D)

    def _L1_attn_ref(x, wq, bq, wk, bk, wv, bv, wo, bo, wi1, bi1, wi2, bi2):
        import jax, jax.numpy as jnp
        import numpy as np
        import math
        D_MODEL = 128
        N_HEADS = 16
        SPARSITY = 0.3
        B, S, D = x.shape
        H = N_HEADS
        hd = D // H
        k = max(1, int(S * SPARSITY))
        Q = (x @ wq.T + bq).reshape(B, S, H, hd).transpose(0, 2, 1, 3)
        K = (x @ wk.T + bk).reshape(B, S, H, hd).transpose(0, 2, 1, 3)
        V = (x @ wv.T + bv).reshape(B, S, H, hd).transpose(0, 2, 1, 3)
        h = jnp.maximum(x @ wi1.T + bi1, 0.0)
        importance = (h @ wi2.T + bi2)[..., 0]
        _, top_idx = jax.lax.top_k(importance, k)
        sparse_mask = jnp.zeros((B, S), dtype=x.dtype).at[jnp.arange(B)[:, None], top_idx].set(1.0)
        scores = jnp.einsum('bhqd,bhkd->bhqk', Q, K) / math.sqrt(hd)
        scores = jnp.where(sparse_mask[:, None, None, :] == 0, -jnp.inf, scores)
        attn = jax.nn.softmax(scores, axis=-1)
        out = jnp.einsum('bhqk,bhkd->bhqd', attn, V)
        out = out.transpose(0, 2, 1, 3).reshape(B, S, D)
        return out @ wo.T + bo

    def _L1_ffn_ref(x, Wr, br, Wi, bi, Wg, bg, Wo, bo, gamma, beta):
        import jax, jax.numpy as jnp
        import numpy as np
        E, K = (8, 2)
        B, S, H, F = (2, 256, 128, 512)
        EPS = 1e-12

        def _expert_ffn(xf, Wi_e, bi_e, Wg_e, bg_e, Wo_e, bo_e, g_e, b_e):
            h = jax.nn.gelu(xf @ Wi_e + bi_e, approximate=False) * jax.nn.sigmoid(xf @ Wg_e + bg_e)
            r = xf + (h @ Wo_e + bo_e)
            mu = jnp.mean(r, axis=-1, keepdims=True)
            var = jnp.mean(jnp.square(r - mu), axis=-1, keepdims=True)
            return (r - mu) * jax.lax.rsqrt(var + EPS) * g_e + b_e
        b, s, h = x.shape
        T = b * s
        xf = x.reshape(T, h)
        probs = jax.nn.softmax(xf @ Wr + br, axis=-1)
        topw, topi = jax.lax.top_k(probs, K)
        topw = topw / jnp.sum(topw, axis=-1, keepdims=True)
        c = jnp.zeros((T, E), x.dtype).at[jnp.arange(T)[:, None], topi].set(topw)
        y = jax.vmap(_expert_ffn, in_axes=(None, 0, 0, 0, 0, 0, 0, 0, 0))(xf, Wi, bi, Wg, bg, Wo, bo, gamma, beta)
        out = jnp.einsum('te,eth->th', c, y)
        return out.reshape(b, s, h)
    x = L0_attn_x
    mod = (_silu(L0_c) @ L0_wmod).reshape(L0_c.shape[0], 6, 1, -1)
    sa, ca, ga, sb, cb, gb = (mod[:, 0], mod[:, 1], mod[:, 2], mod[:, 3], mod[:, 4], mod[:, 5])
    ga = (2 * (ga >= 0) - 1) * jnp.maximum(jnp.abs(ga), 0.25)
    gb = (2 * (gb >= 0) - 1) * jnp.maximum(jnp.abs(gb), 0.25)
    h = _layernorm(x, axis=-1) * (1 + ca) + sa
    x = x + ga * _L0_attn_ref(h, L0_attn_Wattn, L0_attn_battn, L0_attn_Wproj, L0_attn_bproj, L0_attn_embk, L0_attn_embv)
    h = _layernorm(x, axis=-1) * (1 + cb) + sb
    x = x + gb * _L0_ffn_ref(h, L0_ffn_gate_w, L0_ffn_c_fc, L0_ffn_fc_bias, L0_ffn_c_proj, L0_ffn_proj_bias)
    mod = (_silu(L1_c) @ L1_wmod).reshape(L1_c.shape[0], 6, 1, -1)
    sa, ca, ga, sb, cb, gb = (mod[:, 0], mod[:, 1], mod[:, 2], mod[:, 3], mod[:, 4], mod[:, 5])
    ga = (2 * (ga >= 0) - 1) * jnp.maximum(jnp.abs(ga), 0.25)
    gb = (2 * (gb >= 0) - 1) * jnp.maximum(jnp.abs(gb), 0.25)
    h = _layernorm(x, axis=-1) * (1 + ca) + sa
    x = x + ga * _L1_attn_ref(h, L1_attn_wq, L1_attn_bq, L1_attn_wk, L1_attn_bk, L1_attn_wv, L1_attn_bv, L1_attn_wo, L1_attn_bo, L1_attn_wi1, L1_attn_bi1, L1_attn_wi2, L1_attn_bi2)
    h = _layernorm(x, axis=-1) * (1 + cb) + sb
    x = x + gb * _L1_ffn_ref(h, L1_ffn_Wr, L1_ffn_br, L1_ffn_Wi, L1_ffn_bi, L1_ffn_Wg, L1_ffn_bg, L1_ffn_Wo, L1_ffn_bo, L1_ffn_gamma, L1_ffn_beta)
    return x

_drawn_inputs = setup_inputs


def setup_inputs(seed=0):
    import zlib

    import numpy as np

    out = dict(_drawn_inputs(seed))
    spreads = {'L0_ffn_fc_bias': (0.0, 0.8),
     'L0_ffn_proj_bias': (0.0, 0.43),
     'L1_attn_bq': (0.0, 0.8),
     'L1_attn_bk': (0.0, 2.0),
     'L1_attn_bv': (0.0, 0.8),
     'L1_attn_bo': (0.0, 0.333),
     'L1_attn_bi1': (0.0, 0.8),
     'L1_ffn_br': (0.0, 0.322),
     'L1_ffn_bi': (0.0, 0.8),
     'L1_ffn_bg': (0.0, 2.0),
     'L1_ffn_bo': (0.0, 1.904),
     'L1_ffn_gamma': (1.0, 0.592),
     'L1_ffn_beta': (0.0, 0.495)}
    factors = {'L0_attn_Wattn': 8.0,
     'L0_attn_battn': 8.0,
     'L0_attn_Wproj': 8.0,
     'L0_attn_bproj': 8.0,
     'L0_attn_embk': 8.0,
     'L0_attn_embv': 8.0,
     'L0_ffn_gate_w': 3.121,
     'L0_ffn_c_fc': 5.633,
     'L0_ffn_c_proj': 5.136,
     'L1_attn_wq': 8.0,
     'L1_attn_wk': 8.0,
     'L1_attn_wv': 8.0,
     'L1_attn_wo': 8.0,
     'L1_attn_wi1': 8.0,
     'L1_attn_wi2': 8.0,
     'L1_ffn_Wi': 8.0,
     'L1_ffn_Wg': 8.0,
     'L1_ffn_Wo': 8.0}
    for name, (base, spread) in spreads.items():
        noise = np.random.default_rng([zlib.crc32(name.encode()), seed]).standard_normal(out[name].shape)
        drawn = base * np.exp(spread * noise) if base else spread * noise
        out[name] = jnp.asarray(drawn.astype(out[name].dtype))
    for name, factor in factors.items():
        out[name] = (out[name] * factor).astype(out[name].dtype)
    return out
```

```python
from contextlib import ExitStack

import concourse.bass as bass
from concourse import mybir

ALU = mybir.AluOpType
ACT = mybir.ActivationFunctionType
AX = mybir.AxisListType
F32 = mybir.dt.float32
I32 = mybir.dt.int32
U32 = mybir.dt.uint32

P = 128
B, T, C, H = 16, 256, 128, 16
HD = C // H
NTOK = B * T
NT = NTOK // P
CH = 512
NCH = NTOK // CH
NREL = 128
LN_EPS = 1e-5
NEG = -1e30
QK_SCALE = HD ** -0.5
GATE_FLOOR = 0.25

TB = 8
TILES = T // TB
QUAD = 4
NQ = TILES // QUAD
HALF_TILES = P // TB
NG = H // 4
HALVES = 2 * B


def view(ap, offset, dims):
    return bass.AP(ap.tensor, ap.offset + offset, [list(ap.ap[0])] + dims)


def wait(eng, sem, value):
    if isinstance(value, int) and value <= 0:
        return
    eng.wait_ge(sem, value)


def phase_semaphore(nc, k, name):
    sem = nc.alloc_semaphore(name)
    k.semaphores.append(sem)
    return sem


def clear_semaphores(nc, k):
    nc.all_engine_barrier()
    nc.clear_and_free_semaphores(k.semaphores)
    nc.all_engine_barrier()
    k.semaphores = []


class Chain:

    def __init__(self, eng, sem):
        self.eng, self.sem, self.n = eng, sem, 0

    def __call__(self, ins):
        self.n += 1
        ins.then_inc(self.sem, 1)
        self.eng.wait_ge(self.sem, self.n)


def setup_phase(nc, d, k):
    with ExitStack() as ctx:
        def sb(n, s, dt=F32):
            return ctx.enter_context(nc.sbuf_tensor(n, s, dt))

        def sem(n):
            return phase_semaphore(nc, k, n)

        x_rows = sb("x_rows", [P, NT, C])
        cond = sb("cond", [B, 2, C])
        cond_exp = sb("cond_exp", [B, 2, C])
        cond_T = sb("cond_T", [P, 2, B])
        wmod = sb("wmod", [P, 2, 6 * C])
        gate_abs = sb("gate_abs", [P, 2, 2, B])
        gate_sign = sb("gate_sign", [P, 2, 2, B])
        ps = ctx.enter_context(nc.psum_tensor("ps_setup", [P, 8, CH], F32))
        x_in = [sem(f"x_in{i}") for i in range(4)]
        cond_in, wmod_in = sem("cond_in"), sem("wmod_in")
        ident_ready = sem("ident_ready")
        pool_step, dve_step = sem("pool_step0"), sem("dve_step0")
        x_turned, x_copied = sem("x_turned"), sem("x_copied")
        exp_ready, silu_ready, cond_turned, cond_copied = sem("exp_ready"), sem("silu_ready"), sem("cond_turned"), sem("cond_copied")
        mod_ready, zeros_ready = sem("mod_ready"), sem("zeros_ready")
        block = ctx.enter_context(nc.Block())

        @block.sync
        def _(sp):
            for l in range(2):
                sp.dma_start(cond[:, l, :], d[f"L{l}_c"]).then_inc(cond_in, 16)
            for i in range(4):
                r = slice(i * NT // 4, (i + 1) * NT // 4)
                sp.dma_start(x_rows[:, r, :], d["x"].rearrange("(n p) c -> p n c", p=P)[:, r, :]).then_inc(x_in[i], 16)
            for l in range(2):
                sp.dma_start(wmod[:, l, :], d[f"L{l}_wmod"]).then_inc(wmod_in, 16)
            sp.wait_ge(zeros_ready, 1)
            n = XTILES * XS * C // P
            sp.dma_start(bass.AP(k.x_slots.tensor, 0, [[n, P], [CH * 2, n // (2 * CH)], [1, CH * 2]]),
                         view(k.zeros[:, :], 0, [[0, n // (2 * CH)], [1, CH * 2]])).then_inc(k.slots_zeroed, 16)

        @block.gpsimd
        def _(pool):
            step = Chain(pool, pool_step)
            step(pool.memset(k.ident[:, :], 0.0))
            pool.affine_select(out=k.ident[:, :], in_=k.ident[:, :], compare_op=ALU.not_equal, fill=1.0, base=0,
                               pattern=[[-1, P]], channel_multiplier=1).then_inc(ident_ready, 1)
            pool.memset(k.zeros[:, :], 0.0).then_inc(zeros_ready, 1)
            pool.memset(k.mean_w[:, :], 1.0 / C)
            pool.memset(k.ones[:, :], 1.0)
            pool.memset(k.eps[:, :], LN_EPS)

        @block.tensor
        def _(pe):
            pe.wait_ge(ident_ready, 1)
            pe.wait_ge(silu_ready, 1)
            for l in range(2):
                m = pe.transpose(ps[:, 6, l * B:(l + 1) * B], cond[:, l, :], k.ident[0:B, 0:B])
            m.then_inc(cond_turned, 1)
            for n in range(NCH):
                pe.wait_ge(x_in[n // 2], 16)
                wait(pe, x_copied, n - 3)
                for j in range(4):
                    m = pe.transpose(ps[:, n % 4, j * P:(j + 1) * P], x_rows[:, 4 * n + j, :], k.ident[:, :])
                m.then_inc(x_turned, 1)
            pe.wait_ge(cond_copied, 1)
            pe.wait_ge(wmod_in, 32)
            for l in range(2):
                for j in range(6):
                    m = pe.matmul(ps[:, 7, (6 * l + j) * B:(6 * l + j + 1) * B], wmod[:, l, j * C:(j + 1) * C],
                                  cond_T[:, l, :], start=True, stop=True)
            m.then_inc(mod_ready, 1)

        @block.scalar
        def _(act):
            act.wait_ge(cond_in, 32)
            act.activation(cond_exp[:, :, :], cond[:, :, :], ACT.Exp, scale=-1.0).then_inc(exp_ready, 1)

        @block.vector
        def _(dve):
            step = Chain(dve, dve_step)
            dve.wait_ge(exp_ready, 1)
            step(dve.tensor_scalar(cond_exp[:, :, :], cond_exp[:, :, :], 1.0, None, ALU.add))
            step(dve.reciprocal(cond_exp[:, :, :], cond_exp[:, :, :]))
            dve.tensor_tensor(cond[:, :, :], cond[:, :, :], cond_exp[:, :, :], ALU.mult).then_inc(silu_ready, 1)
            dve.wait_ge(cond_turned, 1)
            dve.tensor_copy(cond_T[:, :, :], ps[:, 6, 0:2 * B]).then_inc(cond_copied, 1)
            for n in range(NCH):
                dve.wait_ge(x_turned, n + 1)
                dve.tensor_copy(k.xT[:, n * CH:(n + 1) * CH], ps[:, n % 4, :]).then_inc(x_copied, 1)
            dve.wait_ge(mod_ready, 1)
            step(dve.tensor_copy(k.mod[:, :, :, :], ps[:, 7, 0:12 * B]))
            scales = k.mod[:, :, 1::3, :]
            gates = k.mod[:, :, 2::3, :]
            for l in range(2):
                sc, ga, ab, sg = scales[:, l], gates[:, l], gate_abs[:, l], gate_sign[:, l]
                step(dve.tensor_scalar(sc, sc, 1.0, None, ALU.add))
                step(dve.tensor_scalar(ab, ga, -1.0, None, ALU.mult))
                step(dve.tensor_tensor(ab, ab, ga, ALU.max))
                step(dve.tensor_scalar(ab, ab, GATE_FLOOR, None, ALU.max))
                step(dve.tensor_scalar(sg, ga, 0.0, 2.0, ALU.is_ge, ALU.mult))
                step(dve.scalar_tensor_tensor(out=ga, in0=sg, scalar=-1.0, in1=ab, op0=ALU.add, op1=ALU.mult))


def norm_phase(nc, k, name, layer, which):
    shift_i, scale_i = 3 * which, 3 * which + 1
    with ExitStack() as ctx:
        def sb(n, s, dt=F32):
            return ctx.enter_context(nc.sbuf_tensor(n + name, s, dt))

        def sem(n):
            return phase_semaphore(nc, k, n + name)

        cen = sb("cen", [P, 3, CH])
        sq = sb("sq", [P, 2, CH])
        std = sb("std", [P, 2, CH])
        rstd = sb("rstd", [P, 2, CH])
        ps = ctx.enter_context(nc.psum_tensor("ps" + name, [P, 8, CH], F32))
        mean_ready, cen_ready, sq_ready, var_ready = sem("mean_ready"), sem("cen_ready"), sem("sq_ready"), sem("var_ready")
        std_ready, rstd_ready, norm_ready, h_ready = sem("std_ready"), sem("rstd_ready"), sem("norm_ready"), sem("h_ready")
        block = ctx.enter_context(nc.Block())

        @block.tensor
        def _(pe):
            for n in range(NCH + 1):
                if n < NCH:
                    wait(pe, cen_ready, n - 1)
                    pe.matmul(ps[:, n % 2, :], k.mean_w[:, :], k.xT[:, n * CH:(n + 1) * CH],
                              start=True, stop=True).then_inc(mean_ready, 1)
                if n >= 1:
                    m = n - 1
                    pe.wait_ge(sq_ready, m + 1)
                    wait(pe, std_ready, m - 1)
                    pe.matmul(ps[:, 2 + m % 2, :], k.mean_w[:, :], sq[:, m % 2, :],
                              start=True, stop=True).then_inc(var_ready, 1)

        @block.scalar
        def _(act):
            for n in range(NCH + 2):
                if n < NCH:
                    act.wait_ge(cen_ready, n + 1)
                    wait(act, var_ready, n - 1)
                    act.activation(sq[:, n % 2, :], cen[:, n % 3, :], ACT.Square).then_inc(sq_ready, 1)
                if 1 <= n <= NCH:
                    m = n - 1
                    act.wait_ge(var_ready, m + 1)
                    wait(act, rstd_ready, m - 1)
                    act.activation(std[:, m % 2, :], ps[:, 2 + m % 2, :], ACT.Sqrt, bias=k.eps[:, 0:1]).then_inc(std_ready, 1)
                if n >= 2:
                    m = n - 2
                    act.wait_ge(norm_ready, m + 1)
                    for s in range(CH // T):
                        b = m * (CH // T) + s
                        act.activation(k.hT[:, b * T:(b + 1) * T], cen[:, m % 3, s * T:(s + 1) * T], ACT.Identity,
                                       scale=k.mod[:, layer, scale_i, b:b + 1],
                                       bias=k.mod[:, layer, shift_i, b:b + 1]).then_inc(h_ready, 1)

        @block.vector
        def _(dve):
            for n in range(NCH + 1):
                if n < NCH:
                    dve.wait_ge(mean_ready, n + 1)
                    wait(dve, h_ready, 2 * (n - 2))
                    dve.tensor_tensor(cen[:, n % 3, :], k.xT[:, n * CH:(n + 1) * CH], ps[:, n % 2, :],
                                      ALU.subtract).then_inc(cen_ready, 1)
                if n >= 1:
                    m = n - 1
                    dve.wait_ge(std_ready, m + 1)
                    dve.reciprocal(rstd[:, m % 2, :], std[:, m % 2, :]).then_inc(rstd_ready, 1)
                    dve.wait_ge(rstd_ready, m + 1)
                    dve.wait_ge(sq_ready, m + 1)
                    dve.tensor_tensor(cen[:, m % 3, :], cen[:, m % 3, :], rstd[:, m % 2, :],
                                      ALU.mult).then_inc(norm_ready, 1)


REL_W = NREL + T + TB
VE_W = C + TB * HD
VE_BLOCKS = TILES + TILES // 2
TABLES = 4 + 2 + 2 * TB

SKEW_W = REL_W * HD


def ve_block(i, ch):
    return i if ch == 0 else TILES + i - TILES // 2


def rel_tables_phase(nc, d, k, a):
    with ExitStack() as ctx:
        def sb(n, s, dt=F32):
            return ctx.enter_context(nc.sbuf_tensor(n, s, dt))

        def sem(n):
            return phase_semaphore(nc, k, n)

        wqkv = sb("wqkv0", [P, 3 * C])
        bqk = sb("bqk0", [P, 2])
        bv = sb("bv0", [P, C])
        ek_wide = sb("ek_wide", [P, (T + TB) * HD])
        ps = ctx.enter_context(nc.psum_tensor("ps_qkv0", [P, 8, CH], F32))
        w_in, line_out, skew_out, table_in = sem("w_in0"), sem("line_out"), sem("skew_out"), sem("table_in")
        pool_step = sem("pool_step1")
        q_ready, k_ready, v_ready = sem("q_ready0"), sem("k_ready0"), sem("v_ready0")
        q_copied, k_copied, v_copied = sem("q_copied0"), sem("k_copied0"), sem("v_copied0")
        ek_turned, ek_copied = sem("ek_turned"), sem("ek_copied")
        block = ctx.enter_context(nc.Block())

        @block.sync
        def _(sp):
            sp.dma_start(wqkv[:, :], d["L0_attn_Wattn"]).then_inc(w_in, 16)
            sp.dma_start(bqk[:, :], d["L0_attn_battn"][0:2 * C].rearrange("(j p) -> p j", p=P),
                         allow_slow_non_contiguous=True).then_inc(w_in, 16)
            sp.dma_start(bv[:, :], bass.AP(d["L0_attn_battn"].tensor, 2 * C, [[0, P], [1, C]])).then_inc(w_in, 16)
            for line, emb in ((a.ek_line, d["L0_attn_embk"]), (a.ev_line, d["L0_attn_embv"])):
                sp.dma_start(line[0:NREL, :], bass.AP(emb.tensor, 0, [[0, NREL], [1, HD]])).then_inc(line_out, 16)
                sp.dma_start(line[NREL:2 * NREL, :], emb[:, :]).then_inc(line_out, 16)
                sp.dma_start(line[2 * NREL:REL_W, :],
                             bass.AP(emb.tensor, (NREL - 1) * HD, [[0, REL_W - 2 * NREL], [1, HD]])).then_inc(line_out, 16)
            sp.wait_ge(line_out, 16 * 6)
            for line, skew in ((a.ek_line, a.ek_skew), (a.ev_line, a.ev_skew)):
                sp.dma_start(bass.AP(skew.tensor, 0, [[SKEW_W + HD, P], [1, SKEW_W]]),
                             bass.AP(line.tensor, 0, [[0, P], [1, SKEW_W]])).then_inc(skew_out, 16)
            sp.wait_ge(skew_out, 32)
            sp.dma_start(ek_wide[:, :], bass.AP(a.ek_skew.tensor, NREL * HD, [[SKEW_W, P], [1, (T + TB) * HD]])).then_inc(table_in, 16)
            for ch in range(2):
                first, count = ve_block(ch * TILES // 2, ch), TILES // (1 + ch)
                sp.dma_start(view(a.ve[:, :], first * VE_W + 64, [[VE_W, count], [1, TB * HD]]),
                             bass.AP(a.ev_skew.tensor, NREL * HD, [[SKEW_W, P], [TB * HD, count], [1, TB * HD]])).then_inc(table_in, 16)
            wp = d["L0_attn_Wproj"]
            for hh in range(2):
                sp.dma_start(a.wproj[64 * hh:64 * hh + 64, 8 * hh:8 * hh + 8, :],
                             bass.AP(wp.tensor, hh * 64 * C, [[C, 64], [0, 8], [1, C]])).then_inc(table_in, 16)
                for t in range(TB):
                    row = 64 * (1 - hh) + t * HD
                    sp.dma_start(a.wproj[row:row + HD, 8 * hh:8 * hh + 8, :],
                                 bass.AP(wp.tensor, hh * 64 * C, [[C, HD], [HD * C, 8], [1, C]])).then_inc(table_in, 16)
            sp.dma_start(a.bproj[:, :], d["L0_attn_bproj"].rearrange("(p o) -> p o", o=1),
                         allow_slow_non_contiguous=True).then_inc(table_in, 16)
            sp.wait_ge(table_in, 16 * TABLES)

        @block.gpsimd
        def _(pool):
            step = Chain(pool, pool_step)

            def band(out, base, pattern, width, rows_mult=1):
                step(pool.memset(out, 1.0))
                step(pool.affine_select(out=out, in_=out, compare_op=ALU.is_ge, fill=0.0, base=base,
                                        pattern=pattern, channel_multiplier=rows_mult))
                step(pool.affine_select(out=out, in_=out, compare_op=ALU.is_ge, fill=0.0, base=width - 1 - base,
                                        pattern=[[-s, n] for s, n in pattern], channel_multiplier=-rows_mult))

            band(a.head_mask[:, :], 0, [[-HD, H]], HD)
            for hh in range(2):
                r = slice(64 * hh, 64 * hh + 64)
                band(a.y_mask[r, hh, :], 0, [[-HD, 8], [0, TB]], HD)
                band(a.y_mask[r, 1 - hh, :], 0, [[0, 8], [-HD, TB]], HD)
            band(a.t_mask[:, :], 0, [[-HD, TB]], HD)
            band(a.spread[:, :], 0, [[-HD, H], [0, TB], [-1, HD]], 1)
            for slot in range(2):
                out = a.q_rel[64:64 + TB, slot, :]
                band(out, 0, [[0, HALF_TILES * H], [-1, TB]], 1)
            m = a.e_rel[64:64 + TB, :]
            step(pool.memset(m, 0.0))
            step(pool.affine_select(out=m, in_=m, compare_op=ALU.is_ge, fill=NEG, base=T, pattern=[[-1, T + P]],
                                    channel_multiplier=1))

        @block.tensor
        def _(pe):
            pe.wait_ge(w_in, 48)
            for n in range(NCH):
                h = k.hT[:, n * CH:(n + 1) * CH]
                wait(pe, q_copied, n - 1)
                pe.matmul(ps[:, n % 2, :], wqkv[:, 0:C], h, start=True, stop=True).then_inc(q_ready, 1)
                wait(pe, k_copied, n - 1)
                pe.matmul(ps[:, 2 + n % 2, :], wqkv[:, C:2 * C], h, start=True, stop=True).then_inc(k_ready, 1)
                wait(pe, v_copied, n - 1)
                for j in range(4):
                    m = pe.matmul(ps[:, 4 + n % 2, j * P:(j + 1) * P], k.hT[:, n * CH + j * P:n * CH + (j + 1) * P],
                                  wqkv[:, 2 * C:3 * C], start=True, stop=True)
                m.then_inc(v_ready, 1)
            pe.wait_ge(table_in, 16 * TABLES)
            for i, u in enumerate((T, P, 0)):
                m = pe.transpose(ps[0:64, 6, i * P:(i + 1) * P], ek_wide[:, u * HD:(u + TB) * HD], k.ident[:, :])
            m.then_inc(ek_turned, 1)

        @block.scalar
        def _(act):
            act.wait_ge(w_in, 48)
            for n in range(NCH):
                act.wait_ge(q_ready, n + 1)
                act.activation(a.qT[:, n * CH:(n + 1) * CH], ps[:, n % 2, :], ACT.Identity,
                               bias=bqk[:, 0:1]).then_inc(q_copied, 1)
            act.wait_ge(ek_turned, 1)
            act.activation(a.e_rel[0:64, :], ps[0:64, 6, 0:3 * P], ACT.Copy).then_inc(ek_copied, 1)

        @block.vector
        def _(dve):
            dve.wait_ge(w_in, 48)
            dve.wait_ge(table_in, 16 * TABLES)
            dve.tensor_scalar(a.gate_bias[:, :], k.mod[:, 0, 2, :], a.bproj[:, 0:1], None, ALU.mult)
            for n in range(NCH):
                dve.wait_ge(k_ready, n + 1)
                dve.tensor_scalar(a.kT[:, n * CH:(n + 1) * CH], ps[:, 2 + n % 2, :], bqk[:, 1:2], QK_SCALE,
                                  ALU.add, ALU.mult).then_inc(k_copied, 1)
                dve.wait_ge(v_ready, n + 1)
                out = a.v[:, 4 * n * C:4 * (n + 1) * C]
                dve.tensor_tensor(view(out, 0, [[C, 4], [1, C]]), ps[:, 4 + n % 2, :].rearrange("p (j c) -> p j c", j=4),
                                  view(bv[:, :], 0, [[0, 4], [1, C]]), ALU.add).then_inc(v_copied, 1)


def rel_attention_phase(nc, k, a):
    with ExitStack() as ctx:
        def sb(n, s, dt=F32):
            return ctx.enter_context(nc.sbuf_tensor(n, s, dt))

        def sem(n):
            return phase_semaphore(nc, k, n)

        prob = sb("prob", [P, 4, QUAD, T])
        neg_max = sb("neg_max", [P, 4, QUAD])
        den = sb("den", [P, 4, QUAD])
        rden = sb("rden", [P, 4, QUAD])
        probT = sb("probT", [P, 2, 2, CH])
        ym = sb("ym", [P, 2, HALF_TILES * P])
        upd = sb("upd", [P, 2, P])
        ps_s = ctx.enter_context(nc.psum_tensor("ps_s", [P, 2, QUAD, T], F32))
        ps_t = ctx.enter_context(nc.psum_tensor("ps_t", [P, 2, CH], F32))
        ps_y = ctx.enter_context(nc.psum_tensor("ps_y", [P, CH], F32))
        ps_m = ctx.enter_context(nc.psum_tensor("ps_m", [P, CH], F32))
        score, maxed, expd, rden_ready, probs = sem("score"), sem("maxed"), sem("expd"), sem("rden_ready"), sem("probs")
        turned, turned_out, pv, masked = sem("turned"), sem("turned_out"), sem("pv"), sem("masked")
        spread, q_rel_ready, q_diag_ready, v_ready = sem("spread_s"), sem("q_rel_ready"), sem("q_diag_ready"), sem("v_ready")
        projd, gated, added = sem("projd"), sem("gated"), sem("added")
        block = ctx.enter_context(nc.Block())

        def turns(b, q):
            return 12 * b + (q if q < 4 else 4 + 2 * (q - 4))

        def quad(b, q):
            return b + q // NQ, q % NQ

        def exists(b, q=0):
            return not isinstance(b, int) or 0 <= b < B

        def sequences(eng, body):
            body(-1)
            body(0)
            with eng.Fori(1, B - 1) as b:
                body(b)
            body(B - 1)

        def spread_group(b, q):
            if q < 2:
                return b, 1, q + 2
            if q < 6:
                return b + 1, 0, q - 2
            return b + 1, 1, q - 6

        @block.tensor
        def _(pe):
            def body(b):
                for q in range(NQ):
                    n = NQ * b + q
                    sb_, sq_ = quad(b, q + 2)
                    if exists(sb_):
                        sn = n + 2
                        half, slot, r = sq_ // 4, sq_ // 4, q % 2
                        if sq_ % 4 == 0:
                            c = 2 * sb_ + half
                            pe.wait_ge(q_diag_ready, c + 1)
                            pe.wait_ge(q_rel_ready, NG * c + NG)
                        wait(pe, expd, sn - 1)
                        keys = 4 * TB * (sq_ + 1)
                        for j in range(QUAD):
                            i = QUAD * sq_ + j
                            rows = slice((i % HALF_TILES) * P, (i % HALF_TILES + 1) * P)
                            pe.matmul(ps_s[:, r, j, 0:keys], a.q_diag[:, slot, rows], a.kT[:, bass.ds(sb_ * T, keys)],
                                      start=True, stop=False)
                            m = pe.matmul(ps_s[:, r, j, 0:keys], a.q_rel[0:64 + TB, slot, rows],
                                          a.e_rel[0:64 + TB, T - TB * i:T - TB * i + keys], start=False, stop=True)
                        m.then_inc(score, 1)
                    gb, half, g = spread_group(b, q)
                    if exists(gb):
                        c = 2 * gb + half
                        wait(pe, q_rel_ready, NG * c + g)
                        wait(pe, gated, 2 * b + (-1 if q < 2 else 0 if q < 6 else 1))
                        pe.nop(nofuse=True)
                        for h in range(4):
                            w = (4 * g + h) * TB * HD
                            m = pe.matmul(ps_m[0:64, h * P:(h + 1) * P], a.spread[:, w:w + TB * HD],
                                          a.qT[:, bass.ds(gb * T + half * P, P)], start=True, stop=True)
                        m.then_inc(spread, 1)
                    if exists(b):
                        pe.wait_ge(probs, n + 1)
                        wait(pe, turned_out, turns(b, q))
                        pe.nop(nofuse=True)
                        keys = 4 * TB * (q + 1)
                        for ch in range(1 if q < 4 else 2):
                            ks = min(P, keys - ch * P)
                            for j in range(QUAD):
                                m = pe.transpose(ps_t[0:ks, ch, j * P:(j + 1) * P],
                                                 prob[:, q % 4, j, ch * P:ch * P + ks], k.ident[:, :])
                            m.then_inc(turned, 1)
                    if q == 1 or q == 5:
                        c = 2 * b + (0 if q == 5 else -1)
                        if exists(b) and not (isinstance(c, int) and c < 0):
                            project(b, q, c)
                    pb, pq = quad(b, q - 1)
                    if exists(pb):
                        values(pb, pq, n - 1)

            def values(b, q, n):
                pe.wait_ge(turned_out, turns(b, q) + (1 if q < 4 else 2))
                pe.wait_ge(v_ready, n + 1)
                wait(pe, masked, n)
                keys = 4 * TB * (q + 1)
                for j in range(QUAD):
                    for hh in range(2):
                        col = j * P + hh * 64
                        chunks = range(1 if q < 4 else 2)
                        for ch in chunks:
                            ks = min(P, keys - ch * P)
                            at = ve_block(QUAD * q + j, ch) * VE_W + hh * 64
                            m = pe.matmul(ps_y[:, col:col + 64], a.ve[0:ks, at:at + P], probT[0:ks, q % 2, ch, col:col + 64],
                                          start=ch == 0, stop=ch == chunks[-1])
                m.then_inc(pv, 1)

            def project(b, q, c):
                pe.wait_ge(masked, 4 * c + 4)
                wait(pe, gated, c)
                gb, half, g = spread_group(b, q)
                pe.wait_ge(q_rel_ready, NG * (2 * gb + half) + g + 1 if exists(gb) else NG * HALVES)
                for h in range(H):
                    rhs = view(ym[:, 1 if q == 1 else 0, :], h * TB, [[P, HALF_TILES], [1, TB]])
                    m = pe.matmul(ps_m[:, 0:P], a.wproj[:, h, :], rhs, start=h == 0, stop=h == H - 1)
                m.then_inc(projd, 1)

            sequences(pe, body)
            values(B - 1, NQ - 1, NQ * B - 1)
            project(B, 1, HALVES - 1)

        @block.vector
        def _(dve):
            def body(b):
                for q in range(NQ):
                    n = NQ * b + q
                    sb_, sq_ = quad(b, q + 2)
                    sn = n + 2
                    keys = 4 * TB * (sq_ + 1)
                    if exists(sb_):
                        dve.wait_ge(score, sn + 1)
                        dve.tensor_reduce(neg_max[:, sq_ % 4, :], ps_s[:, q % 2, :, 0:keys], AX.X, ALU.max,
                                          negate=True).then_inc(maxed, 1)
                    gb, half, g = spread_group(b, q)
                    if exists(gb):
                        c = 2 * gb + half
                        dve.wait_ge(spread, NG * c + g + 1)
                        wait(dve, score, 4 * c - 4)
                        out = view(a.q_rel[0:64, half, :], 4 * g * TB, [[TB, 4], [P, HALF_TILES], [1, TB]])
                        dve.tensor_tensor(out, view(ps_m[0:64, :], 0, [[P, 4], [TB, HALF_TILES], [1, TB]]),
                                          view(a.t_mask[0:64, :], 0, [[0, 4], [0, HALF_TILES], [1, TB]]),
                                          ALU.mult).then_inc(q_rel_ready, 1)
                    pb, pq = quad(b, q - 1)
                    if exists(pb):
                        mask(pb, pq, n - 1)
                    vb, vq = quad(b, q + 6)
                    if exists(vb):
                        place_values(vb, vq, n + 6)
                    if exists(sb_):
                        dve.wait_ge(expd, sn + 1)
                        dve.reciprocal(rden[:, sq_ % 4, :], den[:, sq_ % 4, :]).then_inc(rden_ready, 1)
                    if (q == 2 or q == 6) and exists(b):
                        c = 2 * b + (0 if q == 6 else -1)
                        if not (isinstance(c, int) and c < 0):
                            add(c, 1 if q == 2 else 0)

            def mask(b, q, n):
                dve.wait_ge(pv, n + 1)
                if q % 4 == 0:
                    wait(dve, projd, 2 * b + q // 4 - 1)
                out = ym[:, q // 4, (q % 4) * CH:(q % 4 + 1) * CH].rearrange("p (r c) -> p r c", c=P)
                dve.tensor_tensor(out, ps_y[:, :].rearrange("p (r c) -> p r c", c=P),
                                  view(a.y_mask[:, 0, :], 0, [[0, QUAD], [1, P]]), ALU.mult).then_inc(masked, 1)

            def place_values(b, q, n):
                wait(dve, pv, n - 7)
                dve.nop(nofuse=True)
                for ch in range(1 if q < 4 else 2):
                    at = ve_block(QUAD * q, ch) * VE_W
                    m = dve.tensor_copy(view(a.ve[:, :], at, [[VE_W, QUAD], [P, 2], [1, 64]]),
                                        view(a.v[:, bass.ds(b * 2 * C + ch * C, C)], 0, [[0, QUAD], [64, 2], [1, 64]]))
                m.then_inc(v_ready, 1)

            def add(c, half):
                dve.wait_ge(gated, c + 1)
                xs = k.xT[:, bass.ds(c * P, P)]
                dve.tensor_tensor(xs, xs, upd[:, half, :], ALU.add).then_inc(added, 1)

            sequences(dve, body)
            mask(B - 1, NQ - 1, NQ * B - 1)
            add(HALVES - 1, 1)

        @block.scalar
        def _(act):
            def body(b):
                for q in range(NQ):
                    n = NQ * b + q
                    sb_, sq_ = quad(b, q + 2)
                    sn = n + 2
                    keys = 4 * TB * (sq_ + 1)
                    if exists(sb_):
                        act.wait_ge(maxed, sn + 1)
                        ob, oq = quad(sb_, sq_ - 3)
                        wait(act, turned, turns(ob, oq))
                        for j in range(QUAD):
                            m = act.activation(prob[:, sq_ % 4, j, 0:keys], ps_s[:, q % 2, j, 0:keys], ACT.Exp,
                                               bias=neg_max[:, sq_ % 4, j:j + 1], accum_out=den[:, sq_ % 4, j:j + 1])
                        m.then_inc(expd, 1)
                    if exists(b):
                        keys = 4 * TB * (q + 1)
                        wait(act, pv, n - 1)
                        for ch in range(1 if q < 4 else 2):
                            ks = min(P, keys - ch * P)
                            act.wait_ge(turned, turns(b, q) + ch + 1)
                            act.activation(probT[0:ks, q % 2, ch, :], ps_t[0:ks, ch, :], ACT.Copy).then_inc(turned_out, 1)
                        if q == 1 or q == 5:
                            c = 2 * b + (0 if q == 5 else -1)
                            if not (isinstance(c, int) and c < 0):
                                gate(b if q == 5 else b - 1, 0 if q == 5 else 1, c)

            def gate(b, half, c):
                act.wait_ge(projd, c + 1)
                wait(act, added, c - 1)
                act.activation(upd[:, half, :], ps_m[:, 0:P], ACT.Identity, scale=k.mod[:, 0, 2, bass.ds(b, 1)],
                               bias=a.gate_bias[:, bass.ds(b, 1)]).then_inc(gated, 1)

            sequences(act, body)
            gate(B - 1, 1, HALVES - 1)

        @block.gpsimd
        def _(pool):
            def body(b):
                for q in range(NQ):
                    n = NQ * b + q
                    if q == 2 or q == 6:
                        half = 0 if q == 2 else 1
                        if exists(b + 1):
                            c = 2 * (b + 1) + half
                            wait(pool, score, 4 * c - 4)
                            out = a.q_diag[:, half, :]
                            q_in = a.qT[:, bass.ds((b + 1) * T + half * P, P)]
                            pool.tensor_tensor(view(out, 0, [[P, HALF_TILES], [TB, H], [1, TB]]),
                                               view(q_in, 0, [[TB, HALF_TILES], [0, H], [1, TB]]),
                                               view(a.head_mask[:, :], 0, [[0, HALF_TILES], [1, H], [0, TB]]),
                                               ALU.mult).then_inc(q_diag_ready, 1)
                    sb_, sq_ = quad(b, q + 2)
                    if exists(sb_):
                        keys = 4 * TB * (sq_ + 1)
                        pool.wait_ge(rden_ready, n + 3)
                        ps_ = prob[:, sq_ % 4, :, 0:keys]
                        pool.tensor_tensor(ps_, ps_, view(rden[:, sq_ % 4, :], 0, [[1, QUAD], [0, keys]]),
                                           ALU.mult).then_inc(probs, 1)

            sequences(pool, body)


KEPT = max(1, int(T * 0.3))
PARTS = ((0, 6), (6, 6), (12, 4))


def sparse_project_phase(nc, d, k, a):
    with ExitStack() as ctx:
        def sb(n, s, dt=F32):
            return ctx.enter_context(nc.sbuf_tensor(n, s, dt))

        def sem(n):
            return phase_semaphore(nc, k, n)

        w_rows = sb("w_rows1", [P, 4, C])
        wi1_rows = sb("wi1_rows", [C // 2, C])
        w_T = sb("w_T1", [P, 3 * C])
        wi1_T = sb("wi1_T", [P, C // 2])
        bq, bi1, bi2, wi2 = sb("bq1", [P, 1]), sb("bi1", [C // 2, 1]), sb("bi2", [P, 1]), sb("wi2", [C // 2, 1])
        wi2_rep = sb("wi2_rep", [C // 2, P])
        bkv = sb("bkv1", [P, 2 * C])
        hid = sb("hid1", [C // 2, 2, CH])
        imp_row = sb("imp_row", [P, NTOK])
        imp_col = sb("imp_col", [P, NT])
        picked = sb("picked", [P, P])
        compared = sb("compared", [P, 2, T])
        before = sb("before", [P, 2, T])
        above = sb("above", [P, NT])
        tied = sb("tied", [P, NT])
        ps = ctx.enter_context(nc.psum_tensor("ps_proj1", [P, 8, CH], F32))
        w_in, w_turned, w_copied = sem("w_in1"), sem("w_turned1"), sem("w_copied1")
        pool_step, const_ready, wi2_ready = sem("pool_step3"), sem("const_ready3"), sem("wi2_ready")
        q_ready, kv_ready, hid_ready, imp_ready = sem("q_ready1"), sem("kv_ready1"), sem("hid_ready1"), sem("imp_ready1")
        q_copied, kv_copied, hid_copied, imp_copied = sem("q_copied1"), sem("kv_copied1"), sem("hid_copied1"), sem("imp_copied1")
        col_ready, ranked = sem("col_ready"), sem("ranked")
        block = ctx.enter_context(nc.Block())

        def column(name, n):
            return d[name].rearrange("(p o) -> p o", o=1)[0:n, :]

        @block.sync
        def _(sp):
            for i, name in enumerate(("wq", "wk", "wv", "wo")):
                sp.dma_start(w_rows[:, i, :], d["L1_attn_" + name]).then_inc(w_in, 16)
            sp.dma_start(wi1_rows[:, :], d["L1_attn_wi1"]).then_inc(w_in, 16)
            sp.dma_start(bq[:, :], column("L1_attn_bq", P), allow_slow_non_contiguous=True).then_inc(w_in, 16)
            sp.dma_start(a.bo[:, :], column("L1_attn_bo", P), allow_slow_non_contiguous=True).then_inc(w_in, 16)
            sp.dma_start(bi1[:, :], column("L1_attn_bi1", C // 2), allow_slow_non_contiguous=True).then_inc(w_in, 16)
            sp.dma_start(wi2[:, :], d["L1_attn_wi2"].rearrange("o p -> p o"), allow_slow_non_contiguous=True).then_inc(w_in, 16)
            sp.dma_start(bi2[:, :], bass.AP(d["L1_attn_bi2"].tensor, 0, [[0, P], [1, 1]]),
                         allow_slow_non_contiguous=True).then_inc(w_in, 16)
            for i, name in enumerate(("bk", "bv")):
                sp.dma_start(bkv[:, i * C:(i + 1) * C],
                             bass.AP(d["L1_attn_" + name].tensor, 0, [[0, P], [1, C]])).then_inc(w_in, 16)

        @block.gpsimd
        def _(pool):
            step = Chain(pool, pool_step)
            step(pool.memset(before[:, :, :], 1.0))
            step(pool.affine_select(out=before[:, :, :], in_=before[:, :, :], compare_op=ALU.is_gt, fill=0.0, base=0,
                                    pattern=[[P, 2], [-1, T]], channel_multiplier=1))
            m = a.group_mask[:, :, :]
            step(pool.memset(m, 1.0))
            step(pool.affine_select(out=m, in_=m, compare_op=ALU.is_ge, fill=0.0, base=0,
                                    pattern=[[-HD, 4], [1, 4 * HD]], channel_multiplier=0))
            step(pool.affine_select(out=m, in_=m, compare_op=ALU.is_ge, fill=0.0, base=HD - 1,
                                    pattern=[[HD, 4], [-1, 4 * HD]], channel_multiplier=0))
            m = a.head_mask[:, :]
            step(pool.memset(m, 1.0))
            step(pool.affine_select(out=m, in_=m, compare_op=ALU.is_ge, fill=0.0, base=0,
                                    pattern=[[-HD, H]], channel_multiplier=1))
            step(pool.affine_select(out=m, in_=m, compare_op=ALU.is_ge, fill=0.0, base=HD - 1,
                                    pattern=[[HD, H]], channel_multiplier=-1))
            pool.iota(a.places[:, :], [[1, KEPT]], base=0, channel_multiplier=0,
                      allow_small_or_imprecise_dtypes=True).then_inc(const_ready, 1)

        @block.tensor
        def _(pe):
            pe.wait_ge(w_in, 16 * 12)
            for i in range(4):
                pe.transpose(ps[:, 0, i * C:(i + 1) * C], w_rows[:, i, :], k.ident[:, :])
            pe.transpose(ps[:, 1, 0:C // 2], wi1_rows[:, :], k.ident[0:C // 2, 0:C // 2]).then_inc(w_turned, 1)
            pe.wait_ge(w_copied, 3)
            pe.wait_ge(wi2_ready, 1)
            for n in range(NCH + 1):
                if n < NCH:
                    h = k.hT[:, n * CH:(n + 1) * CH]
                    wait(pe, hid_copied, n)
                    pe.matmul(ps[0:C // 2, 4, :], wi1_T[:, :], h, start=True, stop=True).then_inc(hid_ready, 1)
                    wait(pe, q_copied, n - 1)
                    pe.matmul(ps[:, n % 2, :], w_T[:, 0:C], h, start=True, stop=True).then_inc(q_ready, 1)
                if n >= 1:
                    m = n - 1
                    pe.wait_ge(hid_copied, m + 1)
                    wait(pe, imp_copied, m)
                    pe.matmul(ps[:, 5, :], wi2_rep[:, :], hid[:, m % 2, :], start=True, stop=True).then_inc(imp_ready, 1)
                if n < NCH:
                    for g in range(2):
                        u = 2 * n + g
                        wait(pe, kv_copied, u - 1)
                        for j in range(2):
                            t = 4 * n + 2 * g + j
                            m = pe.matmul(ps[:, 2 + u % 2, j * 2 * C:(j + 1) * 2 * C], k.hT[:, t * P:(t + 1) * P],
                                          w_T[:, C:3 * C], start=True, stop=True)
                        m.then_inc(kv_ready, 1)

        @block.scalar
        def _(act):
            act.wait_ge(w_turned, 1)
            act.activation(w_T[:, :], ps[:, 0, 0:3 * C], ACT.Copy).then_inc(w_copied, 1)
            act.activation(a.wo_T[:, :], ps[:, 0, 3 * C:4 * C], ACT.Copy).then_inc(w_copied, 1)
            act.activation(wi1_T[:, :], ps[:, 1, 0:C // 2], ACT.Copy).then_inc(w_copied, 1)
            for n in range(NCH + 1):
                if n < NCH:
                    act.wait_ge(hid_ready, n + 1)
                    wait(act, imp_ready, n - 1)
                    act.activation(hid[:, n % 2, :], ps[0:C // 2, 4, :], ACT.Relu, bias=bi1[:, 0:1]).then_inc(hid_copied, 1)
                if n >= 1:
                    act.wait_ge(imp_ready, n)
                    act.activation(imp_row[:, (n - 1) * CH:n * CH], ps[:, 5, :], ACT.Identity, bias=bi2[:, 0:1]).then_inc(imp_copied, 1)

        @block.vector
        def _(dve):
            dve.wait_ge(w_in, 16 * 12)
            dve.tensor_scalar(wi2_rep[:, :], k.ones[0:C // 2, :], wi2[:, 0:1], None, ALU.mult).then_inc(wi2_ready, 1)
            dve.tensor_scalar(a.gate_bias[:, :], k.mod[:, 1, 2, :], a.bo[:, 0:1], None, ALU.mult)
            for n in range(NCH):
                dve.wait_ge(q_ready, n + 1)
                dve.tensor_scalar(a.qT[:, n * CH:(n + 1) * CH], ps[:, n % 2, :], bq[:, 0:1], QK_SCALE,
                                  ALU.add, ALU.mult).then_inc(q_copied, 1)
                for g in range(2):
                    u = 2 * n + g
                    dve.wait_ge(kv_ready, u + 1)
                    dve.tensor_tensor(a.kv[:, 2 * u:2 * u + 2, :], ps[:, 2 + u % 2, :].rearrange("p (j c) -> p j c", j=2),
                                      view(bkv[:, :], 0, [[0, 2], [1, 2 * C]]), ALU.add).then_inc(kv_copied, 1)
            dve.wait_ge(const_ready, 1)
            dve.wait_ge(imp_copied, NCH)
            for t in range(NT):
                dve.scalar_tensor_tensor(out=picked[:, :], in0=imp_row[:, t * P:(t + 1) * P], scalar=1.0,
                                         in1=k.ident[:, :], op0=ALU.mult, op1=ALU.mult,
                                         accum_out=imp_col[:, t:t + 1]).then_inc(col_ready, 1)
                dve.wait_ge(col_ready, t + 1)
            for t in range(NT):
                row = imp_row[:, t // 2 * T:(t // 2 + 1) * T]
                dve.tensor_scalar(compared[:, 0, :], row, imp_col[:, t:t + 1], 0.0, ALU.is_gt, ALU.add,
                                  accum_out=above[:, t:t + 1]).then_inc(ranked, 1)
                dve.scalar_tensor_tensor(out=compared[:, 1, :], in0=row, scalar=imp_col[:, t:t + 1],
                                         in1=before[:, t % 2, :], op0=ALU.is_equal, op1=ALU.mult,
                                         accum_out=tied[:, t:t + 1]).then_inc(ranked, 1)
                dve.wait_ge(ranked, 2 * t + 2)
            dve.tensor_tensor(a.rank[:, :], above[:, :], tied[:, :], ALU.add)


def sparse_attention_phase(nc, k, a):
    with ExitStack() as ctx:
        def sb(n, s, dt=F32):
            return ctx.enter_context(nc.sbuf_tensor(n, s, dt))

        def sem(n):
            return phase_semaphore(nc, k, n)

        select = sb("select", [P, 2, 2, KEPT])
        kv_kept = sb("kv_kept", [KEPT, 2, 2 * C])
        k_diag = sb("k_diag", [P, 2, H * KEPT])
        v_diag = sb("v_diag", [KEPT, 2, H, 4 * HD])
        q_now = sb("q_now", [P, 2, T])
        prob = sb("prob1", [P, 2, H, KEPT])
        top = sb("top1", [P, 2, H])
        den = sb("den1", [P, 2, H])
        rden = sb("rden1", [P, 2, H])
        probT = sb("probT1", [KEPT, 2, CH])
        y_T = sb("y_T1", [P, 2, P])
        upd = sb("upd1", [P, 2, P])
        ps_s = ctx.enter_context(nc.psum_tensor("ps_s1", [P, 3, CH], F32))
        ps_g = ctx.enter_context(nc.psum_tensor("ps_g1", [P, CH], F32))
        ps_t = ctx.enter_context(nc.psum_tensor("ps_t1", [P, 2, CH], F32))
        ps_y = ctx.enter_context(nc.psum_tensor("ps_y1", [P, CH], F32))
        ps_o = ctx.enter_context(nc.psum_tensor("ps_o1", [P, CH], F32))
        selected, gathered, kept, k_turned = sem("selected"), sem("gathered"), sem("kept"), sem("k_turned")
        k_ready, v_ready, q_ready = sem("k_ready4"), sem("v_ready4"), sem("q_ready4")
        score, maxed, shifted, expd, summed = sem("score1"), sem("maxed1"), sem("shifted1"), sem("expd1"), sem("summed1")
        rden_ready, probs, turned, turned_out = sem("rden1_ready"), sem("probs1"), sem("turned1"), sem("turned_out1")
        pv, y_out, projd, gated, added = sem("pv1"), sem("y_out1"), sem("projd1"), sem("gated1"), sem("added1")
        block = ctx.enter_context(nc.Block())

        def exists(w):
            return not isinstance(w, int) or 0 <= w < HALVES

        def pairs(eng, step):
            def body(i):
                for s in range(4):
                    step(4 * i + s, 2 * i + s // 2, s)
            body(-1)
            body(0)
            with eng.Fori(1, B // 2 - 1) as i:
                body(i)
            body(B // 2 - 1)

        @block.tensor
        def _(pe):
            def scores(w, b, s, part):
                first, count = PARTS[part]
                if part == 0:
                    pe.wait_ge(k_ready, b + 1)
                    pe.wait_ge(q_ready, b + 1)
                wait(pe, shifted, 3 * w + part - 2)
                pe.matmul(ps_s[:, part, 0:count * KEPT], q_now[:, s // 2, (s % 2) * P:(s % 2 + 1) * P],
                          k_diag[:, s // 2, first * KEPT:(first + count) * KEPT], start=True, stop=True).then_inc(score, 1)

            def turn(w, s, g):
                pe.wait_ge(probs, 3 * w + (1, 2, 2, 3)[g])
                wait(pe, turned_out, 4 * w + g - 1)
                for h in range(4):
                    m = pe.transpose(ps_t[0:KEPT, g % 2, h * P:(h + 1) * P], prob[:, s % 2, 4 * g + h, :], k.ident[:, :])
                m.then_inc(turned, 1)

            def values(w, b, s, g):
                pe.wait_ge(turned_out, 4 * w + g + 1)
                if g == 0:
                    pe.wait_ge(v_ready, b + 1)
                    wait(pe, y_out, w - 1)
                pe.nop(nofuse=True)
                for h in range(4):
                    m = pe.matmul(ps_y[4 * HD * g:4 * HD * (g + 1), (s % 2) * P:(s % 2 + 1) * P],
                                  v_diag[:, s // 2, 4 * g + h, :], probT[:, g % 2, h * P:(h + 1) * P],
                                  start=h == 0, stop=h == 3)
                m.then_inc(pv, 1)

            def project(w, s):
                pe.wait_ge(y_out, w + 1)
                wait(pe, gated, w)
                pe.matmul(ps_o[:, 0:P], a.wo_T[:, :], y_T[:, s % 2, :], start=True, stop=True).then_inc(projd, 1)

            def step(w, b, s):
                ahead = s % 2 == 0 and exists(2 * (b + 1))
                if ahead:
                    pe.wait_ge(selected, b + 2)
                    wait(pe, kept, b + 1)
                    for ch in range(2):
                        m = pe.matmul(ps_g[0:KEPT, 0:2 * C], select[:, (s // 2 + 1) % 2, ch, :],
                                      a.kv[:, bass.ds(2 * (b + 1) + ch, 1), :], start=ch == 0, stop=ch == 1)
                    m.then_inc(gathered, 1)
                now, nxt = exists(w), exists(w + 1)
                nb, ns = b + s % 2, (s + 1) % 4
                if now:
                    turn(w, s, 0)
                if nxt:
                    scores(w + 1, nb, ns, 0)
                if now:
                    turn(w, s, 1)
                    values(w, b, s, 0)
                if nxt:
                    scores(w + 1, nb, ns, 1)
                if now:
                    turn(w, s, 2)
                    values(w, b, s, 1)
                if ahead:
                    pe.wait_ge(kept, b + 2)
                    wait(pe, k_ready, b + 1)
                    pe.transpose(ps_g[:, 2 * C:2 * C + KEPT], kv_kept[:, (s // 2 + 1) % 2, 0:C],
                                 k.ident[0:KEPT, 0:KEPT]).then_inc(k_turned, 1)
                if nxt:
                    scores(w + 1, nb, ns, 2)
                if now:
                    turn(w, s, 3)
                    values(w, b, s, 2)
                if exists(w - 1) and exists(w):
                    project(w - 1, s + 1)
                if now:
                    values(w, b, s, 3)

            pairs(pe, step)
            project(HALVES - 1, HALVES - 1)

        @block.vector
        def _(dve):
            def shift(w, s, part):
                first, count = PARTS[part]
                r = slice(first, first + count)
                scores = ps_s[:, part, 0:count * KEPT].rearrange("p (h r) -> p h r", h=count)
                dve.wait_ge(score, 3 * w + part + 1)
                dve.tensor_reduce(top[:, s % 2, r], scores, AX.X, ALU.max).then_inc(maxed, 1)
                dve.wait_ge(maxed, 3 * w + part + 1)
                wait(dve, turned, 4 * w - 4)
                dve.tensor_tensor(prob[:, s % 2, r, :], scores, view(top[:, s % 2, r], 0, [[1, count], [0, KEPT]]),
                                  ALU.subtract).then_inc(shifted, 1)

            def total(w, s, part):
                first, count = PARTS[part]
                r = slice(first, first + count)
                dve.wait_ge(expd, 3 * w + part + 1)
                dve.tensor_reduce(den[:, s % 2, r], prob[:, s % 2, r, :], AX.X, ALU.add).then_inc(summed, 1)
                dve.wait_ge(summed, 3 * w + part + 1)
                dve.reciprocal(rden[:, s % 2, r], den[:, s % 2, r]).then_inc(rden_ready, 1)

            def step(w, b, s):
                ahead = s % 2 == 0 and exists(2 * (b + 1))
                slot = (s // 2 + 1) % 2
                if ahead:
                    wait(dve, gathered, b)
                    dve.nop(nofuse=True)
                    for ch in range(2):
                        m = dve.tensor_scalar(select[:, slot, ch, :], a.places[:, :],
                                              a.rank[:, bass.ds(2 * (b + 1) + ch, 1)], None, ALU.is_equal)
                    m.then_inc(selected, 1)
                nxt, ns = exists(w + 1), (s + 1) % 4
                if nxt:
                    shift(w + 1, ns, 0)
                    shift(w + 1, ns, 1)
                    total(w + 1, ns, 0)
                if ahead:
                    dve.wait_ge(k_turned, b + 2)
                    wait(dve, score, 6 * (b + 1) - 6)
                    dve.tensor_tensor(k_diag[:, slot, :].rearrange("p (h r) -> p h r", h=H),
                                      view(ps_g[:, 2 * C:2 * C + KEPT], 0, [[0, H], [1, KEPT]]),
                                      view(a.head_mask[:, :], 0, [[1, H], [0, KEPT]]), ALU.mult).then_inc(k_ready, 1)
                if nxt:
                    shift(w + 1, ns, 2)
                    total(w + 1, ns, 1)
                    total(w + 1, ns, 2)
                if exists(w - 1) and exists(w):
                    add(w - 1, s + 1)

            def add(w, s):
                dve.wait_ge(gated, w + 1)
                xs = k.xT[:, bass.ds(w * P, P)]
                dve.tensor_tensor(xs, xs, upd[:, s % 2, :], ALU.add).then_inc(added, 1)

            pairs(dve, step)
            add(HALVES - 1, HALVES - 1)

        @block.scalar
        def _(act):
            def exp(w, s, part):
                first, count = PARTS[part]
                act.wait_ge(shifted, 3 * w + part + 1)
                p = prob[:, s % 2, first:first + count, :]
                act.activation(p, p, ACT.Exp).then_inc(expd, 1)

            def copy(w, s, g):
                act.wait_ge(turned, 4 * w + g + 1)
                wait(act, pv, 4 * w + g - 1)
                act.activation(probT[:, g % 2, :], ps_t[0:KEPT, g % 2, :], ACT.Copy).then_inc(turned_out, 1)

            def gate(w, b, s):
                act.wait_ge(projd, w + 1)
                wait(act, added, w - 1)
                act.nop(nofuse=True)
                act.activation(upd[:, s % 2, :], ps_o[:, 0:P], ACT.Identity, scale=k.mod[:, 1, 2, bass.ds(b, 1)],
                               bias=a.gate_bias[:, bass.ds(b, 1)]).then_inc(gated, 1)

            def step(w, b, s):
                if s % 2 == 0 and exists(2 * (b + 1)):
                    act.wait_ge(gathered, b + 2)
                    wait(act, v_ready, b)
                    act.activation(kv_kept[:, (s // 2 + 1) % 2, :], ps_g[0:KEPT, 0:2 * C], ACT.Copy).then_inc(kept, 1)
                now, nxt, ns = exists(w), exists(w + 1), (s + 1) % 4
                for g in range(4):
                    if now:
                        copy(w, s, g)
                    if nxt and g < 3:
                        exp(w + 1, ns, g)
                if exists(w - 1) and exists(w):
                    gate(w - 1, b - (1 - s % 2), s + 1)
                if now:
                    act.wait_ge(pv, 4 * w + 4)
                    wait(act, projd, w - 1)
                    act.activation(y_T[:, s % 2, :], ps_y[:, (s % 2) * P:(s % 2 + 1) * P], ACT.Copy).then_inc(y_out, 1)

            pairs(act, step)
            gate(HALVES - 1, B - 1, HALVES - 1)

        @block.gpsimd
        def _(pool):
            def step(w, b, s):
                if s % 2 == 0 and exists(2 * (b + 1)):
                    slot = (s // 2 + 1) % 2
                    wait(pool, score, 6 * (b + 1) - 6)
                    pool.nop(nofuse=True)
                    pool.tensor_copy(q_now[:, slot, :], a.qT[:, bass.ds((b + 1) * T, T)]).then_inc(q_ready, 1)
                    pool.wait_ge(kept, b + 2)
                    wait(pool, pv, 8 * (b + 1) - 8)
                    pool.tensor_tensor(view(v_diag[:, slot, 0, :], 0, [[16 * HD, 4], [4 * HD, 4], [1, 4 * HD]]),
                                       view(kv_kept[:, slot, C:2 * C], 0, [[4 * HD, 4], [0, 4], [1, 4 * HD]]),
                                       view(a.group_mask[:, 0, :], 0, [[0, 4], [4 * HD, 4], [1, 4 * HD]]),
                                       ALU.mult).then_inc(v_ready, 1)
                if exists(w + 1):
                    for part, (first, count) in enumerate(PARTS):
                        r = slice(first, first + count)
                        ns = (s + 1) % 2
                        pool.wait_ge(rden_ready, 3 * (w + 1) + part + 1)
                        pool.tensor_tensor(prob[:, ns, r, :], prob[:, ns, r, :],
                                           view(rden[:, ns, r], 0, [[1, count], [0, KEPT]]), ALU.mult).then_inc(probs, 1)

            pairs(pool, step)


def layer1_attention(nc, d, k):
    with ExitStack() as ctx:
        def sb(n, s, dt=F32):
            return ctx.enter_context(nc.sbuf_tensor(n, s, dt))

        a = Place()
        a.qT, a.kv = sb("qT1", [P, NTOK]), sb("kv1", [P, NT, 2 * C])
        a.wo_T, a.bo, a.gate_bias = sb("wo_T", [P, C]), sb("bo1", [P, 1]), sb("gate_bias1", [P, B])
        a.rank, a.places = sb("rank", [P, NT]), sb("places", [P, KEPT])
        a.group_mask, a.head_mask = sb("group_mask", [KEPT, 4, 4 * HD]), sb("head_mask1", [P, H])
        with nc.sbuf_tensor("hT1", [P, NTOK], F32) as hT:
            k.hT = hT
            norm_phase(nc, k, "_n10", 1, 0)
            sparse_project_phase(nc, d, k, a)
        sparse_attention_phase(nc, k, a)


E, TOPK = 8, 2
FF = 4 * C
FK = FF // P
CAPACITY = int(1.25 * NTOK * TOPK / E)
XS = 2 * P
XTILES = 40
MAXT = NTOK // XS
KT = TOPK * NT
assert NTOK * TOPK // XS + E - 1 <= XTILES and XTILES % 2 == 0


def route_phase(nc, d, k, r, name, gate_w, gate_b, capacity):
    with ExitStack() as ctx:
        def sb(n, s, dt=F32):
            return ctx.enter_context(nc.sbuf_tensor(n + name, s, dt))

        def sem(n):
            return phase_semaphore(nc, k, n + name)

        w = sb("gate_w", [P, E])
        bias = sb("gate_b", [P, E])
        rows = sb("h_rows", [P, NT, C])
        logit = sb("logit", [P, NT, E])
        hit = sb("hit", [P, TOPK, NT, E])
        eq = sb("eq", [P, NT, E])
        top = sb("top", [P, TOPK, NT])
        best = sb("best", [P, NT])
        prio = sb("prio", [P, E])
        earlier = sb("earlier", [P, P])
        gap = sb("gap", [P, NT])
        total = sb("total", [P, KT, E])
        upto = sb("upto", [P, KT, E])
        rank = sb("rank_e", [P, KT, E])
        ranked = sb("ranked_e", [P, KT, E])
        keep = sb("keep", [P, KT])
        steps = sb("steps", [P, E, MAXT])
        need = sb("need", [P, E])
        past = sb("past", [P, E])
        start = sb("start", [P, E])
        more = sb("more", [P, E, MAXT])
        slot = sb("slot_f", [P, KT])
        tile_no = sb("tile_no", [P, XTILES, E])
        tile_e = sb("tile_e", [P, XTILES])
        ps = ctx.enter_context(nc.psum_tensor("ps_route" + name, [P, 8, CH], F32))
        w_in, const_ready, pool_step, dve_step = sem("w_in"), sem("const_ready"), sem("pool_step"), sem("dve_step")
        logit_ready, turned, copied = sem("logit_ready"), sem("turned"), sem("copied")
        gap_ready, exp_ready, hit_ready, prefix_ready = sem("gap_ready"), sem("exp_ready"), sem("hit_ready"), sem("prefix_ready")
        slot_ready, scattered = sem("slot_ready"), sem("scattered")
        block = ctx.enter_context(nc.Block())

        @block.sync
        def _(sp):
            sp.dma_start(w[:, :], gate_w).then_inc(w_in, 16)
            if gate_b is not None:
                sp.dma_start(bias[:, :], bass.AP(gate_b.tensor, 0, [[0, P], [1, E]])).then_inc(w_in, 16)

        loads = 16 if gate_b is None else 32

        @block.gpsimd
        def _(pool):
            step = Chain(pool, pool_step)
            step(pool.memset(earlier[:, :], 1.0))
            step(pool.affine_select(out=earlier[:, :], in_=earlier[:, :], compare_op=ALU.is_gt, fill=0.0, base=0,
                                    pattern=[[1, P]], channel_multiplier=-1))
            step(pool.iota(prio[:, :], [[-1, E]], base=E, channel_multiplier=0, allow_small_or_imprecise_dtypes=True))
            step(pool.iota(steps[:, :, :], [[0, E], [XS, MAXT]], base=0, channel_multiplier=0,
                           allow_small_or_imprecise_dtypes=True))
            pool.iota(tile_no[:, :, :], [[1, XTILES], [0, E]], base=0, channel_multiplier=0,
                      allow_small_or_imprecise_dtypes=True).then_inc(const_ready, 1)
            pool.wait_ge(k.slots_zeroed, 16)
            pool.wait_ge(slot_ready, 1)
            pool.wait_ge(copied, NCH)
            for c in range(TOPK):
                for t in range(NT):
                    n = c * NT + t
                    pool.indirect_dma_start(out=k.x_slots, out_offset=bass.IndirectOffsetOnAxis(ap=r.slot[:, n:n + 1], axis=0),
                                            in_=rows[:, t, :], in_offset=None).then_inc(scattered, 16)
            pool.wait_ge(scattered, 16 * KT)

        @block.tensor
        def _(pe):
            pe.wait_ge(w_in, loads)
            for t in range(NT):
                m = pe.matmul(ps[:, 4, t * E:(t + 1) * E], k.hT[:, t * P:(t + 1) * P], w[:, :], start=True, stop=True)
            m.then_inc(logit_ready, 1)
            for n in range(NCH):
                wait(pe, copied, n - 3)
                for j in range(4):
                    t = 4 * n + j
                    m = pe.transpose(ps[:, n % 4, j * P:(j + 1) * P], k.hT[:, t * P:(t + 1) * P], k.ident[:, :])
                m.then_inc(turned, 1)
            pe.wait_ge(const_ready, 1)
            pe.wait_ge(hit_ready, 1)
            h = hit[:, :, :, :].rearrange("p c t e -> p (c t e)")
            pe.matmul(ps[:, 5, :], earlier[:, :], h, start=True, stop=True)
            pe.matmul(ps[:, 6, :], k.ones[:, :], h, start=True, stop=True).then_inc(prefix_ready, 1)

        @block.scalar
        def _(act):
            for n in range(NCH):
                act.wait_ge(turned, n + 1)
                act.activation(rows[:, 4 * n:4 * n + 4, :], ps[:, n % 4, :].rearrange("p (j c) -> p j c", j=4),
                               ACT.Copy).then_inc(copied, 1)
            act.wait_ge(gap_ready, 1)
            act.activation(gap[:, :], gap[:, :], ACT.Exp).then_inc(exp_ready, 1)

        @block.vector
        def _(dve):
            step = Chain(dve, dve_step)

            def over_e(v, n=NT):
                return view(v, 0, [[1, n], [0, E]])

            def for_all(v, n=NT):
                return view(v, 0, [[0, n], [1, E]])

            dve.wait_ge(logit_ready, 1)
            dve.wait_ge(const_ready, 1)
            dve.wait_ge(w_in, loads)
            logits = ps[:, 4, 0:NT * E].rearrange("p (t e) -> p t e", e=E)
            if gate_b is None:
                step(dve.tensor_copy(logit[:, :, :], logits))
            else:
                step(dve.tensor_tensor(logit[:, :, :], logits, for_all(bias[:, :]), ALU.add))
            for c in range(TOPK):
                step(dve.tensor_reduce(top[:, c, :], logit[:, :, :], AX.X, ALU.max))
                step(dve.tensor_tensor(eq[:, :, :], logit[:, :, :], over_e(top[:, c, :]), ALU.is_equal))
                step(dve.tensor_tensor(eq[:, :, :], eq[:, :, :], for_all(prio[:, :]), ALU.mult))
                step(dve.tensor_reduce(best[:, :], eq[:, :, :], AX.X, ALU.max))
                step(dve.tensor_tensor(hit[:, c, :, :], eq[:, :, :], over_e(best[:, :]), ALU.is_equal))
                if c == 0:
                    step(dve.scalar_tensor_tensor(out=logit[:, :, :], in0=hit[:, 0, :, :], scalar=NEG, in1=logit[:, :, :],
                                                  op0=ALU.mult, op1=ALU.add))
            dve.tensor_tensor(gap[:, :], top[:, 1, :], top[:, 0, :], ALU.subtract).then_inc(gap_ready, 1)
            dve.sem_inc(hit_ready, 1)
            dve.wait_ge(exp_ready, 1)
            step(dve.tensor_scalar(best[:, :], gap[:, :], 1.0, None, ALU.add))
            step(dve.reciprocal(r.weight[:, 0:NT], best[:, :]))
            step(dve.tensor_tensor(r.weight[:, NT:KT], r.weight[:, 0:NT], gap[:, :], ALU.mult))
            dve.wait_ge(prefix_ready, 1)
            within = ps[:, 5, :].rearrange("p (n e) -> p n e", e=E)
            step(dve.tensor_copy(total[:, :, :], ps[:, 6, :].rearrange("p (n e) -> p n e", e=E)))
            for e in range(E):
                m = dve.tensor_tensor_scan(view(upto[:, :, :], e, [[E, KT]]), k.ones[:, 0:KT],
                                           view(total[:, :, :], e, [[E, KT]]), 0.0, ALU.mult, ALU.add)
                step(m)
            step(dve.tensor_tensor(rank[:, :, :], upto[:, :, :], total[:, :, :], ALU.subtract))
            step(dve.tensor_tensor(rank[:, :, :], rank[:, :, :], within, ALU.add))
            step(dve.tensor_tensor(more[:, :, :], view(upto[:, KT - 1, :], 0, [[1, E], [0, MAXT]]), steps[:, :, :], ALU.is_gt))
            step(dve.tensor_reduce(need[:, :], more[:, :, :], AX.X, ALU.add))
            step(dve.tensor_tensor_scan(past[:, :], k.ones[:, 0:E], need[:, :], 0.0, ALU.mult, ALU.add))
            step(dve.tensor_tensor(start[:, :], past[:, :], need[:, :], ALU.subtract))
            step(dve.tensor_scalar(start[:, :], start[:, :], float(XS), None, ALU.mult))
            hits = hit[:, :, :, :].rearrange("p c t e -> p (c t) e")
            if capacity is not None:
                step(dve.tensor_tensor(ranked[:, :, :], rank[:, :, :], hits, ALU.mult))
                step(dve.tensor_reduce(keep[:, :], ranked[:, :, :], AX.X, ALU.add))
                step(dve.scalar_tensor_tensor(out=r.weight[:, :], in0=keep[:, :], scalar=float(capacity), in1=r.weight[:, :],
                                              op0=ALU.is_lt, op1=ALU.mult))
            step(dve.tensor_tensor(rank[:, :, :], rank[:, :, :], for_all(start[:, :], KT), ALU.add))
            step(dve.tensor_tensor(ranked[:, :, :], rank[:, :, :], hits, ALU.mult))
            step(dve.tensor_reduce(slot[:, :], ranked[:, :, :], AX.X, ALU.add))
            dve.tensor_copy(r.slot[:, :], slot[:, :]).then_inc(slot_ready, 1)
            step(dve.tensor_tensor(tile_no[:, :, :], tile_no[:, :, :], for_all(past[:, :], XTILES), ALU.is_ge))
            step(dve.tensor_reduce(tile_e[:, :], tile_no[:, :, :], AX.X, ALU.add))
            step(dve.tensor_scalar(r.expert[:, :], tile_e[:, :], float(E - 1), None, ALU.min))


def expert_phase(nc, k, r, name, weights, gated):
    fc_names = ["fc", "gate"] if gated else ["fc"]
    nf = len(fc_names)
    row_names = ["out_b", "gamma", "beta"] if gated else ["out_b"]
    nr = len(row_names)
    with ExitStack() as ctx:
        def sb(n, s, dt=F32):
            return ctx.enter_context(nc.sbuf_tensor(n + name, s, dt))

        def sem(n):
            return phase_semaphore(nc, k, n + name)

        fc = sb("fc", [P, 2, nf, FF])
        proj = sb("proj", [P, 2, FK, C])
        fc_b = sb("fc_b", [P, nf, E, FK])
        out_rows = sb("out_rows", [P, nr, E, C])
        x_rows = sb("x_rows", [P, 2, 2, C])
        x_T = sb("x_T", [P, 2, XS])
        act1 = sb("act1", [P, 2, FK, XS])
        act2 = sb("act2", [P, 2, FK, XS]) if gated else None
        y = sb("y", [P, 2, 2, C])
        ps_x = ctx.enter_context(nc.psum_tensor("ps_x" + name, [P, CH], F32))
        ps_h = ctx.enter_context(nc.psum_tensor("ps_h" + name, [P, nf, 2, 2, XS], F32))
        ps_o = ctx.enter_context(nc.psum_tensor("ps_o" + name, [P, 2, CH], F32))
        if gated:
            cen = sb("cen", [P, 2, C])
            stats = sb("stats", [P, 2, 6])
            moments = sb("moments", [P, 2, 2])
            inv_std = sb("inv_std", [P, 2])
            exponent = sb("exponent", [P, 2])
            dve_step, var_ready, inv_ready = sem("dve_step"), sem("var_ready"), sem("inv_ready")
            exponent_ready = sem("exponent_ready")
        tables_in, halved = sem("tables_in"), sem("halved")
        w_in = [sem(f"w_in{i}_") for i in range(2)]
        x_in = [sem(f"x_in{i}_") for i in range(2)]
        x_turned, x_copied, fc_ready, act_ready = sem("x_turned"), sem("x_copied"), sem("fc_ready"), sem("act_ready")
        g_ready, out_ready, y_ready = sem("g_ready"), sem("out_ready"), sem("y_ready")
        stored = [sem(f"stored{i}_") for i in range(2)]
        block = ctx.enter_context(nc.Block())

        def tiles(eng, step, ahead):
            if ahead:
                step(-1, 1)
            for s in range(2):
                step(s, s)
            with eng.Fori(1, XTILES // 2 - 1) as i:
                for s in range(2):
                    step(2 * i + s, s)
            for s in range(2):
                step(XTILES - 2 + s, s)

        def exists(j):
            return not isinstance(j, int) or 0 <= j < XTILES

        nw = nf + 1

        @block.sync
        def _(sp):
            for f, (_, b) in enumerate(weights.fc):
                sp.dma_start(fc_b[:, f, :, :], b.rearrange("e (p f) -> p e f", p=P)).then_inc(tables_in, 16)
            for i, t in enumerate(weights.rows):
                sp.dma_start(out_rows[:, i, :, :], bass.AP(t.tensor, 0, [[0, P], [1, E * C]])).then_inc(tables_in, 16)

            def step(j, s):
                if not isinstance(j, int) or j >= 2:
                    wait_free(j)
                e = sp.value_load(r.expert[0:1, bass.ds(j, 1)], min_val=0, max_val=E - 1)
                for f, (w, _) in enumerate(weights.fc):
                    sp.dma_start(fc[:, s, f, :], w[bass.ds(e, 1), :, :].rearrange("o p f -> (o p) f")).then_inc(w_in[s], 16)
                sp.dma_start(proj[:, s, :, :], weights.proj[bass.ds(e, 1), :, :].rearrange("o (p f) c -> (o p) f c", p=P)).then_inc(w_in[s], 16)
                sp.dma_start(x_rows[:, s, :, :],
                             k.x_slots[bass.ds(j * XS, XS), :].rearrange("(s p) c -> p s c", p=P)).then_inc(x_in[s], 16)

            def wait_free(j):
                sp.wait_ge(out_ready, j - 1)
                sp.wait_ge(y_ready, j - 1)

            for s in range(2):
                step(s, s)
            with sp.Fori(1, XTILES // 2) as i:
                for s in range(2):
                    step(2 * i + s, s)

        @block.tensor
        def _(pe):
            def step(j, s):
                ns = 1 - s
                if exists(j + 1):
                    n = j + 1
                    pe.wait_ge(x_in[ns], 16 * ((n + 2) // 2) if isinstance(n, int) else 8 * (n - ns) + 16)
                    wait(pe, x_copied, n)
                    for h in range(2):
                        m = pe.transpose(ps_x[:, h * P:(h + 1) * P], x_rows[:, ns, h, :], k.ident[:, :])
                    m.then_inc(x_turned, 1)
                if exists(j):
                    pe.wait_ge(g_ready if gated else act_ready, j + 1 if gated else 2 * j + 2)
                    wait(pe, y_ready, j - 1)
                    for h in range(2):
                        for f in range(FK):
                            m = pe.matmul(ps_o[:, s, h * P:(h + 1) * P], act1[:, s, f, h * P:(h + 1) * P],
                                          proj[:, s, f, :], start=f == 0, stop=f == FK - 1)
                    m.then_inc(out_ready, 1)
                if exists(j + 1):
                    pe.wait_ge(w_in[ns], 16 * nw * ((n + 2) // 2) if isinstance(n, int) else 8 * nw * (n - ns) + 16 * nw)
                    pe.wait_ge(x_copied, n + 1)
                    for g in range(2):
                        for i in range(nf):
                            wait(pe, act_ready, 2 * nf * n - 2 * nf + g * nf + i + 1)
                            for f in (2 * g, 2 * g + 1):
                                m = pe.matmul(ps_h[:, i, g, f % 2, :], fc[:, ns, i, f:FF:FK], x_T[:, ns, :],
                                              start=True, stop=True)
                            m.then_inc(fc_ready, 1)

            tiles(pe, step, True)

        @block.scalar
        def _(act):
            act.wait_ge(tables_in, 16 * (nf + nr))
            if gated:
                act.wait_ge(halved, 1)

            def step(j, s):
                ns = 1 - s
                if not exists(j + 1):
                    return
                n = j + 1
                act.wait_ge(x_turned, n + 1)
                wait(act, fc_ready, 2 * nf * (n - 1))
                act.activation(x_T[:, ns, :], ps_x[:, 0:XS], ACT.Copy).then_inc(x_copied, 1)
                e = act.value_load(r.expert[0:1, bass.ds(n, 1)], min_val=0, max_val=E - 1)
                for g in range(2):
                    for i in range(nf):
                        act.wait_ge(fc_ready, 2 * nf * n + g * nf + i + 1)
                        wait(act, out_ready, n - 1)
                        act.nop(nofuse=True)
                        out = (act1, act2)[i]
                        for f in (2 * g, 2 * g + 1):
                            m = act.activation(out[:, ns, f, :], ps_h[:, i, g, f % 2, :], ACT.Tanh if i else ACT.Gelu,
                                               scale=0.5 if i else 1.0, bias=fc_b[:, i, bass.ds(e, 1), f])
                        m.then_inc(act_ready, 1)

            tiles(act, step, True)

        @block.vector
        def _(dve):
            dve.wait_ge(tables_in, 16 * (nf + nr))
            if gated:
                dve.tensor_scalar(fc_b[:, 1, :, :], fc_b[:, 1, :, :], 0.5, None, ALU.mult).then_inc(halved, 1)

            def gate(n, ns):
                for g in range(2):
                    dve.wait_ge(act_ready, 4 * n + 2 * g + 2)
                    a1 = act1[:, ns, 2 * g:2 * g + 2, :]
                    m = dve.scalar_tensor_tensor(out=a1, in0=act2[:, ns, 2 * g:2 * g + 2, :], scalar=1.0, in1=a1,
                                                 op0=ALU.add, op1=ALU.mult)
                m.then_inc(g_ready, 1)

            def finish(j, s):
                e = dve.value_load(r.expert[0:1, bass.ds(j, 1)], min_val=0, max_val=E - 1)

                def row(i):
                    return view(out_rows[:, i, bass.ds(e, 1), :], 0, [[0, 2], [1, C]])

                dve.wait_ge(out_ready, j + 1)
                if not isinstance(j, int):
                    dve.wait_ge(stored[s], 8 * (j - s))
                elif j >= 2:
                    dve.wait_ge(stored[s], 16 * (j // 2))
                dve.nop(nofuse=True)
                out = ps_o[:, s, 0:XS].rearrange("p (h c) -> p h c", h=2)
                if not gated:
                    dve.tensor_tensor(y[:, s, :, :], out, row(0), ALU.add).then_inc(y_ready, 1)
                    return
                count = [0]
                steps = 5

                def step(ins):
                    count[0] += 1
                    ins.then_inc(dve_step, 1)
                    dve.wait_ge(dve_step, steps * j + count[0])

                step(dve.scalar_tensor_tensor(out=cen[:, :, :], in0=out, scalar=0.5, in1=x_rows[:, s, :, :],
                                              op0=ALU.mult, op1=ALU.add))
                dve.nop(nofuse=True)
                step(dve.tensor_tensor(cen[:, :, :], cen[:, :, :], row(0), ALU.add))
                for h in range(2):
                    m = dve.bn_stats(stats[:, h, :], cen[:, h, :])
                step(m)
                dve.nop(nofuse=True)
                for h in range(2):
                    m = dve.bn_aggr(moments[:, h, :], stats[:, h, :])
                m.then_inc(var_ready, 1)
                dve.wait_ge(inv_ready, j + 1)
                for h in range(2):
                    m = dve.tensor_scalar(y[:, s, h, :], cen[:, h, :], moments[:, h, 0:1], inv_std[:, h:h + 1],
                                          ALU.subtract, ALU.mult)
                step(m)
                dve.nop(nofuse=True)
                step(dve.tensor_tensor(y[:, s, :, :], y[:, s, :, :], row(1), ALU.mult))
                dve.nop(nofuse=True)
                dve.tensor_tensor(y[:, s, :, :], y[:, s, :, :], row(2), ALU.add).then_inc(y_ready, 1)

            def step(j, s):
                if gated and exists(j + 1):
                    gate(j + 1, 1 - s)
                if exists(j):
                    finish(j, s)

            tiles(dve, step, True)

        @block.gpsimd
        def _(pool):
            if gated:
                pool.memset(exponent[:, :], -0.5).then_inc(exponent_ready, 1)
                pool.wait_ge(exponent_ready, 1)

            def step(j, s):
                if gated:
                    pool.wait_ge(var_ready, j + 1)
                    pool.tensor_tensor(inv_std[:, :], moments[:, :, 1], exponent[:, :], ALU.pow).then_inc(inv_ready, 1)
                pool.wait_ge(y_ready, j + 1)
                pool.dma_start(k.y_slots[bass.ds(j * XS, XS), :].rearrange("(s p) c -> p s c", p=P),
                               y[:, s, :, :]).then_inc(stored[s], 16)

            tiles(pool, step, False)
            for s in range(2):
                pool.wait_ge(stored[s], 8 * XTILES)


def combine_phase(nc, k, r, name, layer):
    with ExitStack() as ctx:
        def sb(n, s, dt=F32):
            return ctx.enter_context(nc.sbuf_tensor(n + name, s, dt))

        def sem(n):
            return phase_semaphore(nc, k, n + name)

        got = sb("got", [P, TOPK, NT, C])
        part = sb("part", [P, 2, 4, C])
        both = sb("both", [P, 2, 4, C])
        ps = ctx.enter_context(nc.psum_tensor("ps_comb" + name, [P, 2, CH], F32))
        rows_in = [sem(f"rows_in{n}_") for n in range(NCH)]
        part_ready, both_ready, turned, added = sem("part_ready"), sem("both_ready"), sem("turned"), sem("added")
        block = ctx.enter_context(nc.Block())

        @block.gpsimd
        def _(pool):
            for t in range(NT):
                for c in range(TOPK):
                    n = c * NT + t
                    pool.indirect_dma_start(out=got[:, c, t, :], out_offset=None, in_=k.y_slots,
                                            in_offset=bass.IndirectOffsetOnAxis(ap=r.slot[:, n:n + 1], axis=0)).then_inc(rows_in[t // 4], 16)

        @block.tensor
        def _(pe):
            for n in range(NCH):
                pe.wait_ge(both_ready, 4 * (n + 1))
                wait(pe, added, 2 * (n - 1))
                for j in range(4):
                    m = pe.transpose(ps[:, n % 2, j * P:(j + 1) * P], both[:, n % 2, j, :], k.ident[:, :])
                m.then_inc(turned, 1)

        @block.scalar
        def _(act):
            for n in range(NCH):
                act.wait_ge(rows_in[n], 16 * 4 * TOPK)
                wait(act, both_ready, 4 * (n - 1))
                for j in range(4):
                    t = 4 * n + j
                    act.activation(part[:, n % 2, j, :], got[:, 0, t, :], ACT.Copy, scale=r.weight[:, t:t + 1]).then_inc(part_ready, 1)

        @block.vector
        def _(dve):
            for n in range(NCH + 1):
                if n < NCH:
                    wait(dve, turned, n - 1)
                    for j in range(4):
                        t = 4 * n + j
                        dve.wait_ge(part_ready, t + 1)
                        dve.scalar_tensor_tensor(out=both[:, n % 2, j, :], in0=got[:, 1, t, :], scalar=r.weight[:, NT + t:NT + t + 1],
                                                 in1=part[:, n % 2, j, :], op0=ALU.mult, op1=ALU.add).then_inc(both_ready, 1)
                if n >= 1:
                    m = n - 1
                    dve.wait_ge(turned, m + 1)
                    for s in range(2):
                        b = 2 * m + s
                        xs = k.xT[:, b * T:(b + 1) * T]
                        dve.scalar_tensor_tensor(out=xs, in0=ps[:, m % 2, s * T:(s + 1) * T], scalar=k.mod[:, layer, 5, b:b + 1],
                                                 in1=xs, op0=ALU.mult, op1=ALU.add).then_inc(added, 1)


def experts(nc, d, k, name, layer, gate_w, gate_b, capacity, weights, gated):
    with ExitStack() as ctx:
        def sb(n, s, dt=F32):
            return ctx.enter_context(nc.sbuf_tensor(n + name, s, dt))

        r = Place()
        r.weight, r.slot, r.expert = sb("weight", [P, KT]), sb("slot", [P, KT], I32), sb("expert", [P, XTILES], I32)
        with nc.sbuf_tensor("hT" + name, [P, NTOK], F32) as hT:
            k.hT = hT
            norm_phase(nc, k, "_n" + name, layer, 1)
            route_phase(nc, d, k, r, name, gate_w, gate_b, capacity)
        expert_phase(nc, k, r, "_x" + name, weights, gated)
        combine_phase(nc, k, r, "_c" + name, layer)


def layer0_experts(nc, d, k):
    w = Place()
    w.fc = [(d["L0_ffn_c_fc"], d["L0_ffn_fc_bias"].rearrange("e o f -> (e o) f"))]
    w.proj = d["L0_ffn_c_proj"]
    w.rows = [d["L0_ffn_proj_bias"]]
    experts(nc, d, k, "_m0", 0, d["L0_ffn_gate_w"], None, CAPACITY, w, False)


def layer1_experts(nc, d, k):
    w = Place()
    w.fc = [(d["L1_ffn_Wi"], d["L1_ffn_bi"]), (d["L1_ffn_Wg"], d["L1_ffn_bg"])]
    w.proj = d["L1_ffn_Wo"]
    w.rows = [d["L1_ffn_bo"], d["L1_ffn_gamma"], d["L1_ffn_beta"]]
    experts(nc, d, k, "_m1", 1, d["L1_ffn_Wr"], d["L1_ffn_br"], None, w, True)


class Place:
    pass


def output_phase(nc, d, k):
    with ExitStack() as ctx:
        rows = ctx.enter_context(nc.sbuf_tensor("out_rows", [P, 3, CH], F32))
        ps = ctx.enter_context(nc.psum_tensor("ps_out", [P, 4, CH], F32))
        turned, copied, stored = (phase_semaphore(nc, k, n) for n in ("out_turned", "out_copied", "out_stored"))
        block = ctx.enter_context(nc.Block())

        @block.tensor
        def _(pe):
            for n in range(NCH):
                wait(pe, copied, n - 3)
                for j in range(4):
                    m = pe.transpose(ps[:, n % 4, j * P:(j + 1) * P], k.xT[:, (4 * n + j) * P:(4 * n + j + 1) * P], k.ident[:, :])
                m.then_inc(turned, 1)

        @block.vector
        def _(dve):
            for n in range(NCH):
                dve.wait_ge(turned, n + 1)
                wait(dve, stored, 16 * (n - 2))
                dve.tensor_copy(rows[:, n % 3, :], ps[:, n % 4, :]).then_inc(copied, 1)

        @block.sync
        def _(sp):
            out = d["out"].rearrange("(n p) c -> p n c", p=P)
            for n in range(NCH):
                sp.wait_ge(copied, n + 1)
                sp.dma_start(out[:, 4 * n:4 * n + 4, :], rows[:, n % 3, :].rearrange("p (j c) -> p j c", j=4)).then_inc(stored, 16)
                sp.wait_ge(stored, 16 * (n + 1))


def build(nc, d):
    with ExitStack() as ctx:
        def sb(n, s, dt=F32):
            return ctx.enter_context(nc.sbuf_tensor(n, s, dt))

        k = Place()
        k.semaphores = []
        k.ident, k.mean_w, k.ones, k.eps = sb("ident", [P, P]), sb("mean_w", [P, P]), sb("ones", [P, P]), sb("eps", [P, 1])
        k.mod = sb("mod", [P, 2, 6, B])
        k.xT = sb("xT", [P, NTOK])
        k.zeros = sb("zeros", [P, 2 * CH])
        k.slots_zeroed = ctx.enter_context(nc.semaphore("slots_zeroed"))
        k.x_slots = nc.dram_tensor("x_slots", (XTILES * XS, C), F32, kind="Internal").ap()
        k.y_slots = nc.dram_tensor("y_slots", (XTILES * XS, C), F32, kind="Internal").ap()
        setup_phase(nc, d, k)
        layer0_attention(nc, d, k)
        layer0_experts(nc, d, k)
        clear_semaphores(nc, k)
        layer1_attention(nc, d, k)
        layer1_experts(nc, d, k)
        output_phase(nc, d, k)


def layer0_attention(nc, d, k):
    with ExitStack() as ctx:
        def sb(n, s, dt=F32):
            return ctx.enter_context(nc.sbuf_tensor(n, s, dt))

        a = Place()
        a.ek_line = nc.dram_tensor("ek_line", (REL_W, HD), F32, kind="Internal").ap()
        a.ev_line = nc.dram_tensor("ev_line", (REL_W, HD), F32, kind="Internal").ap()
        a.ek_skew = nc.dram_tensor("ek_skew", (P, SKEW_W + HD), F32, kind="Internal").ap()
        a.ev_skew = nc.dram_tensor("ev_skew", (P, SKEW_W + HD), F32, kind="Internal").ap()
        a.qT, a.kT, a.v = sb("qT0", [P, NTOK]), sb("kT0", [P, NTOK]), sb("v0", [P, NT * C])
        a.ve = sb("ve", [P, VE_BLOCKS * VE_W])
        a.e_rel = sb("e_rel", [P, 3 * P])
        a.wproj = sb("wproj0", [P, H, C])
        a.bproj, a.gate_bias = sb("bproj0", [P, 1]), sb("gate_bias0", [P, B])
        a.head_mask, a.y_mask, a.t_mask = sb("head_mask", [P, H]), sb("y_mask", [P, 2, 64]), sb("t_mask", [64, TB])
        a.spread = sb("spread", [P, H * TB * HD])
        a.q_rel = sb("q_rel", [P, 2, HALF_TILES * P])
        with nc.sbuf_tensor("hT0", [P, NTOK], F32) as hT:
            k.hT = hT
            norm_phase(nc, k, "_n00", 0, 0)
            rel_tables_phase(nc, d, k, a)
        a.q_diag = sb("q_diag", [P, 2, HALF_TILES * P])
        rel_attention_phase(nc, k, a)


INPUTS = [
    "L0_attn_x", "L0_attn_Wattn", "L0_attn_battn", "L0_attn_Wproj", "L0_attn_bproj", "L0_attn_embk", "L0_attn_embv",
    "L0_ffn_gate_w", "L0_ffn_c_fc", "L0_ffn_fc_bias", "L0_ffn_c_proj", "L0_ffn_proj_bias", "L0_c", "L0_wmod",
    "L1_attn_wq", "L1_attn_bq", "L1_attn_wk", "L1_attn_bk", "L1_attn_wv", "L1_attn_bv", "L1_attn_wo", "L1_attn_bo",
    "L1_attn_wi1", "L1_attn_bi1", "L1_attn_wi2", "L1_attn_bi2", "L1_ffn_Wr", "L1_ffn_br", "L1_ffn_Wi", "L1_ffn_bi",
    "L1_ffn_Wg", "L1_ffn_bg", "L1_ffn_Wo", "L1_ffn_bo", "L1_ffn_gamma", "L1_ffn_beta", "L1_c", "L1_wmod",
]


def kernel(**inputs):
    import numpy as np
    import concourse.bacc as bacc
    from concourse.bass_utils import run_bass_kernel_spmd

    nc = bacc.Bacc("TRN2", target_bir_lowering=False, num_devices=1)
    arrays, d = {}, {}
    for name in INPUTS:
        arrays[name] = np.ascontiguousarray(inputs[name])
        d[name] = nc.dram_tensor(name, arrays[name].shape, F32, kind="ExternalInput").ap()
    d["x"] = d["L0_attn_x"].rearrange("b t c -> (b t) c")
    out = nc.dram_tensor("out", (B, T, C), F32, kind="ExternalOutput").ap()
    d["out"] = out.rearrange("b t c -> (b t) c")
    build(nc, d)
    return run_bass_kernel_spmd(nc, [arrays], core_ids=[0]).results[0]["out"]
```

```python
from contextlib import ExitStack

import concourse.bass as bass
from concourse import mybir

ALU = mybir.AluOpType
ACT = mybir.ActivationFunctionType
AX = mybir.AxisListType
F32 = mybir.dt.float32
I32 = mybir.dt.int32
U32 = mybir.dt.uint32

P = 128
B, T, C, H = 16, 256, 128, 16
HD = C // H
NTOK = B * T
NT = NTOK // P
CH = 512
NCH = NTOK // CH
NREL = 128
LN_EPS = 1e-5
NEG = -1e30
QK_SCALE = HD ** -0.5
GATE_FLOOR = 0.25

TB = 8
TILES = T // TB
QUAD = 4
NQ = TILES // QUAD
HALF_TILES = P // TB
NG = H // 4
HALVES = 2 * B


def view(ap, offset, dims):
    return bass.AP(ap.tensor, ap.offset + offset, [list(ap.ap[0])] + dims)


def wait(eng, sem, value):
    if isinstance(value, int) and value <= 0:
        return
    eng.wait_ge(sem, value)


def phase_semaphore(nc, k, name):
    sem = nc.alloc_semaphore(name)
    k.semaphores.append(sem)
    return sem


def clear_semaphores(nc, k):
    nc.all_engine_barrier()
    nc.clear_and_free_semaphores(k.semaphores)
    nc.all_engine_barrier()
    k.semaphores = []


class Chain:

    def __init__(self, eng, sem):
        self.eng, self.sem, self.n = eng, sem, 0

    def __call__(self, ins):
        self.n += 1
        ins.then_inc(self.sem, 1)
        self.eng.wait_ge(self.sem, self.n)


def setup_phase(nc, d, k):
    with ExitStack() as ctx:
        def sb(n, s, dt=F32):
            return ctx.enter_context(nc.sbuf_tensor(n, s, dt))

        def sem(n):
            return phase_semaphore(nc, k, n)

        x_rows = sb("x_rows", [P, NT, C])
        cond = sb("cond", [B, 2, C])
        cond_exp = sb("cond_exp", [B, 2, C])
        cond_T = sb("cond_T", [P, 2, B])
        wmod = sb("wmod", [P, 2, 6 * C])
        gate_abs = sb("gate_abs", [P, 2, 2, B])
        gate_sign = sb("gate_sign", [P, 2, 2, B])
        ps = ctx.enter_context(nc.psum_tensor("ps_setup", [P, 8, CH], F32))
        x_in = [sem(f"x_in{i}") for i in range(4)]
        cond_in, wmod_in = sem("cond_in"), sem("wmod_in")
        ident_ready = sem("ident_ready")
        pool_step, dve_step = sem("pool_step0"), sem("dve_step0")
        x_turned, x_copied = sem("x_turned"), sem("x_copied")
        exp_ready, silu_ready, cond_turned, cond_copied = sem("exp_ready"), sem("silu_ready"), sem("cond_turned"), sem("cond_copied")
        mod_ready = sem("mod_ready")
        block = ctx.enter_context(nc.Block())

        @block.sync
        def _(sp):
            for l in range(2):
                sp.dma_start(cond[:, l, :], d[f"L{l}_c"]).then_inc(cond_in, 16)
            for i in range(4):
                r = slice(i * NT // 4, (i + 1) * NT // 4)
                sp.dma_start(x_rows[:, r, :], d["x"].rearrange("(n p) c -> p n c", p=P)[:, r, :]).then_inc(x_in[i], 16)
            for l in range(2):
                sp.dma_start(wmod[:, l, :], d[f"L{l}_wmod"]).then_inc(wmod_in, 16)

        @block.gpsimd
        def _(pool):
            step = Chain(pool, pool_step)
            step(pool.memset(k.ident[:, :], 0.0))
            pool.affine_select(out=k.ident[:, :], in_=k.ident[:, :], compare_op=ALU.not_equal, fill=1.0, base=0,
                               pattern=[[-1, P]], channel_multiplier=1).then_inc(ident_ready, 1)
            pool.memset(k.ones[:, :], 1.0)
            pool.memset(k.eps[:, :], LN_EPS)

        @block.tensor
        def _(pe):
            pe.wait_ge(ident_ready, 1)
            pe.wait_ge(silu_ready, 1)
            for l in range(2):
                m = pe.transpose(ps[:, 6, l * B:(l + 1) * B], cond[:, l, :], k.ident[0:B, 0:B])
            m.then_inc(cond_turned, 1)
            for n in range(NCH):
                pe.wait_ge(x_in[n // 2], 16)
                wait(pe, x_copied, n - 3)
                for j in range(4):
                    m = pe.transpose(ps[:, n % 4, j * P:(j + 1) * P], x_rows[:, 4 * n + j, :], k.ident[:, :])
                m.then_inc(x_turned, 1)
            pe.wait_ge(cond_copied, 1)
            pe.wait_ge(wmod_in, 32)
            for l in range(2):
                for j in range(6):
                    m = pe.matmul(ps[:, 7, (6 * l + j) * B:(6 * l + j + 1) * B], wmod[:, l, j * C:(j + 1) * C],
                                  cond_T[:, l, :], start=True, stop=True)
            m.then_inc(mod_ready, 1)

        @block.scalar
        def _(act):
            act.wait_ge(cond_in, 32)
            act.activation(cond_exp[:, :, :], cond[:, :, :], ACT.Exp, scale=-1.0).then_inc(exp_ready, 1)

        @block.vector
        def _(dve):
            step = Chain(dve, dve_step)
            dve.wait_ge(exp_ready, 1)
            step(dve.tensor_scalar(cond_exp[:, :, :], cond_exp[:, :, :], 1.0, None, ALU.add))
            step(dve.reciprocal(cond_exp[:, :, :], cond_exp[:, :, :]))
            dve.tensor_tensor(cond[:, :, :], cond[:, :, :], cond_exp[:, :, :], ALU.mult).then_inc(silu_ready, 1)
            dve.wait_ge(cond_turned, 1)
            dve.tensor_copy(cond_T[:, :, :], ps[:, 6, 0:2 * B]).then_inc(cond_copied, 1)
            for n in range(NCH):
                dve.wait_ge(x_turned, n + 1)
                dve.tensor_copy(k.xT[:, n * CH:(n + 1) * CH], ps[:, n % 4, :]).then_inc(x_copied, 1)
            dve.wait_ge(mod_ready, 1)
            step(dve.tensor_copy(k.mod[:, :, :, :], ps[:, 7, 0:12 * B]))
            scales = k.mod[:, :, 1::3, :]
            gates = k.mod[:, :, 2::3, :]
            for l in range(2):
                sc, ga, ab, sg = scales[:, l], gates[:, l], gate_abs[:, l], gate_sign[:, l]
                step(dve.tensor_scalar(sc, sc, 1.0, None, ALU.add))
                step(dve.tensor_scalar(ab, ga, -1.0, None, ALU.mult))
                step(dve.tensor_tensor(ab, ab, ga, ALU.max))
                step(dve.tensor_scalar(ab, ab, GATE_FLOOR, None, ALU.max))
                step(dve.tensor_scalar(sg, ga, 0.0, 2.0, ALU.is_ge, ALU.mult))
                step(dve.scalar_tensor_tensor(out=ga, in0=sg, scalar=-1.0, in1=ab, op0=ALU.add, op1=ALU.mult))


def norm_phase(nc, k, name, layer, which):
    shift_i, scale_i = 3 * which, 3 * which + 1
    with ExitStack() as ctx:
        def sb(n, s, dt=F32):
            return ctx.enter_context(nc.sbuf_tensor(n + name, s, dt))

        def sem(n):
            return phase_semaphore(nc, k, n + name)

        stats = sb("stats", [P, NT, 6])
        moments = sb("moments", [P, NT, 2])
        std, rstd = sb("std", [P, NT]), sb("rstd", [P, NT])
        normed = sb("normed", [P, 3, CH])
        ps_in = ctx.enter_context(nc.psum_tensor("ps_in" + name, [P, 4, CH], F32))
        ps_out = ctx.enter_context(nc.psum_tensor("ps_out" + name, [P, 4, CH], F32))
        turned, stats_ready, var_ready, std_ready = sem("turned"), sem("stats_ready"), sem("var_ready"), sem("std_ready")
        rstd_ready, norm_ready, back, h_ready = sem("rstd_ready"), sem("norm_ready"), sem("back"), sem("h_ready")
        block = ctx.enter_context(nc.Block())

        @block.tensor
        def _(pe):
            for n in range(NCH + 2):
                if n < NCH:
                    wait(pe, norm_ready, n - 3)
                    for j in range(4):
                        t = 4 * n + j
                        m = pe.transpose(ps_in[:, n % 4, j * P:(j + 1) * P], k.xT[:, t * P:(t + 1) * P], k.ident[:, :])
                    m.then_inc(turned, 1)
                if n >= 2:
                    c = n - 2
                    pe.wait_ge(norm_ready, c + 1)
                    wait(pe, h_ready, c - 3)
                    for j in range(4):
                        m = pe.transpose(ps_out[:, c % 4, j * P:(j + 1) * P], normed[:, c % 3, j * P:(j + 1) * P], k.ident[:, :])
                    m.then_inc(back, 1)

        @block.vector
        def _(dve):
            for n in range(NCH + 1):
                if n < NCH:
                    dve.wait_ge(turned, n + 1)
                    for j in range(4):
                        m = dve.bn_stats(stats[:, 4 * n + j, :], ps_in[:, n % 4, j * P:(j + 1) * P])
                    m.then_inc(stats_ready, 1)
                    dve.wait_ge(stats_ready, n + 1)
                    dve.nop(nofuse=True)
                    for j in range(4):
                        m = dve.bn_aggr(moments[:, 4 * n + j, :], stats[:, 4 * n + j, :])
                    m.then_inc(var_ready, 1)
                if n >= 1:
                    c = n - 1
                    dve.wait_ge(std_ready, c + 1)
                    dve.reciprocal(rstd[:, 4 * c:4 * c + 4], std[:, 4 * c:4 * c + 4]).then_inc(rstd_ready, 1)
                    dve.wait_ge(rstd_ready, c + 1)
                    wait(dve, back, c - 2)
                    for j in range(4):
                        t = 4 * c + j
                        m = dve.tensor_scalar(normed[:, c % 3, j * P:(j + 1) * P], ps_in[:, c % 4, j * P:(j + 1) * P],
                                              moments[:, t, 0:1], rstd[:, t:t + 1], ALU.subtract, ALU.mult)
                    m.then_inc(norm_ready, 1)

        @block.scalar
        def _(act):
            for n in range(NCH + 2):
                if n < NCH:
                    act.wait_ge(var_ready, n + 1)
                    act.activation(std[:, 4 * n:4 * n + 4], moments[:, 4 * n:4 * n + 4, 1], ACT.Sqrt,
                                   bias=k.eps[:, 0:1]).then_inc(std_ready, 1)
                if n >= 2:
                    c = n - 2
                    act.wait_ge(back, c + 1)
                    for s in range(CH // T):
                        b = c * (CH // T) + s
                        m = act.activation(k.hT[:, b * T:(b + 1) * T], ps_out[:, c % 4, s * T:(s + 1) * T], ACT.Identity,
                                           scale=k.mod[:, layer, scale_i, b:b + 1], bias=k.mod[:, layer, shift_i, b:b + 1])
                    m.then_inc(h_ready, 1)


REL_W = NREL + T + TB
VE_W = P
VE_BLOCKS = TILES + TILES // 2
TABLES = 3 + 2 + 2 * TB

SKEW_W = REL_W * HD


def ve_block(i, ch):
    return i if ch == 0 else TILES + i - TILES // 2


def rel_tables_phase(nc, d, k, a):
    with ExitStack() as ctx:
        def sb(n, s, dt=F32):
            return ctx.enter_context(nc.sbuf_tensor(n, s, dt))

        def sem(n):
            return phase_semaphore(nc, k, n)

        wqkv = sb("wqkv0", [P, 3 * C])
        bqk = sb("bqk0", [P, 2])
        bv = sb("bv0", [P, C])
        ek_wide = sb("ek_wide", [P, (T + TB) * HD])
        ps = ctx.enter_context(nc.psum_tensor("ps_qkv0", [P, 8, CH], F32))
        w_in, line_out, skew_out, table_in = sem("w_in0"), sem("line_out"), sem("skew_out"), sem("table_in")
        pool_step = sem("pool_step1")
        q_ready, k_ready, v_ready = sem("q_ready0"), sem("k_ready0"), sem("v_ready0")
        q_copied, k_copied, v_copied = sem("q_copied0"), sem("k_copied0"), sem("v_copied0")
        ek_turned, ek_copied = sem("ek_turned"), sem("ek_copied")
        block = ctx.enter_context(nc.Block())

        @block.sync
        def _(sp):
            sp.dma_start(wqkv[:, :], d["L0_attn_Wattn"]).then_inc(w_in, 16)
            sp.dma_start(bqk[:, :], d["L0_attn_battn"][0:2 * C].rearrange("(j p) -> p j", p=P),
                         allow_slow_non_contiguous=True).then_inc(w_in, 16)
            sp.dma_start(bv[:, :], bass.AP(d["L0_attn_battn"].tensor, 2 * C, [[0, P], [1, C]])).then_inc(w_in, 16)
            for line, emb in ((a.ek_line, d["L0_attn_embk"]), (a.ev_line, d["L0_attn_embv"])):
                sp.dma_start(line[0:NREL, :], bass.AP(emb.tensor, 0, [[0, NREL], [1, HD]])).then_inc(line_out, 16)
                sp.dma_start(line[NREL:2 * NREL, :], emb[:, :]).then_inc(line_out, 16)
                sp.dma_start(line[2 * NREL:REL_W, :],
                             bass.AP(emb.tensor, (NREL - 1) * HD, [[0, REL_W - 2 * NREL], [1, HD]])).then_inc(line_out, 16)
            sp.wait_ge(line_out, 16 * 6)
            for line, skew in ((a.ek_line, a.ek_skew), (a.ev_line, a.ev_skew)):
                sp.dma_start(bass.AP(skew.tensor, 0, [[SKEW_W + HD, P], [1, SKEW_W]]),
                             bass.AP(line.tensor, 0, [[0, P], [1, SKEW_W]])).then_inc(skew_out, 16)
            sp.wait_ge(skew_out, 32)
            sp.dma_start(ek_wide[:, :], bass.AP(a.ek_skew.tensor, NREL * HD, [[SKEW_W, P], [1, (T + TB) * HD]])).then_inc(table_in, 16)
            for ch in range(2):
                first, count = ve_block(ch * TILES // 2, ch), TILES // (1 + ch)
                sp.dma_start(view(a.ve[:, :], first * VE_W + 64, [[VE_W, count], [1, TB * HD]]),
                             bass.AP(a.ev_skew.tensor, NREL * HD, [[SKEW_W, P], [TB * HD, count], [1, TB * HD]])).then_inc(table_in, 16)
            wp = d["L0_attn_Wproj"]
            sp.dma_start(a.wproj[:, :], wp).then_inc(table_in, 16)
            for hh in range(2):
                for t in range(TB):
                    row = 64 * (1 - hh) + t * HD
                    sp.dma_start(a.wproj_rel[row:row + HD, :, :],
                                 bass.AP(wp.tensor, hh * 64 * C, [[C, HD], [HD * C, 8], [1, C]])).then_inc(table_in, 16)
            sp.dma_start(a.bproj[:, :], d["L0_attn_bproj"].rearrange("(p o) -> p o", o=1),
                         allow_slow_non_contiguous=True).then_inc(table_in, 16)
            sp.wait_ge(table_in, 16 * TABLES)

        @block.gpsimd
        def _(pool):
            step = Chain(pool, pool_step)

            def band(out, base, pattern, width, rows_mult=1):
                step(pool.memset(out, 1.0))
                step(pool.affine_select(out=out, in_=out, compare_op=ALU.is_ge, fill=0.0, base=base,
                                        pattern=pattern, channel_multiplier=rows_mult))
                step(pool.affine_select(out=out, in_=out, compare_op=ALU.is_ge, fill=0.0, base=width - 1 - base,
                                        pattern=[[-s, n] for s, n in pattern], channel_multiplier=-rows_mult))

            band(a.head_mask[:, :], 0, [[-HD, H]], HD)
            band(a.y_mask[0:64, :, :], 0, [[0, 2], [-HD, 8], [0, TB]], HD)
            for r in (slice(0, 64), slice(64, P)):
                band(a.t_mask[r, :], 0, [[-HD, TB]], HD)
            step(pool.tensor_copy(view(a.y_mask[64:P, 0, :], 0, [[TB, H], [1, TB]]),
                                  view(a.t_mask[64:P, :], 0, [[0, H], [1, TB]])))
            band(a.spread[:, :], 0, [[-HD, H], [0, TB], [-1, HD]], 1)
            for slot in range(2):
                out = a.q_rel[64:64 + TB, slot, :]
                band(out, 0, [[0, HALF_TILES * H], [-1, TB]], 1)
            m = a.e_rel[64:64 + TB, :]
            step(pool.memset(m, 0.0))
            step(pool.affine_select(out=m, in_=m, compare_op=ALU.is_ge, fill=NEG, base=T, pattern=[[-1, T + P]],
                                    channel_multiplier=1))

        @block.tensor
        def _(pe):
            pe.wait_ge(w_in, 48)
            for n in range(NCH):
                h = k.hT[:, n * CH:(n + 1) * CH]
                wait(pe, q_copied, n - 1)
                pe.matmul(ps[:, n % 2, :], wqkv[:, 0:C], h, start=True, stop=True).then_inc(q_ready, 1)
                wait(pe, k_copied, n - 1)
                pe.matmul(ps[:, 2 + n % 2, :], wqkv[:, C:2 * C], h, start=True, stop=True).then_inc(k_ready, 1)
                wait(pe, v_copied, n - 1)
                for j in range(4):
                    m = pe.matmul(ps[:, 4 + n % 2, j * P:(j + 1) * P], k.hT[:, n * CH + j * P:n * CH + (j + 1) * P],
                                  wqkv[:, 2 * C:3 * C], start=True, stop=True)
                m.then_inc(v_ready, 1)
            pe.wait_ge(table_in, 16 * TABLES)
            for i, u in enumerate((T, P, 0)):
                m = pe.transpose(ps[0:64, 6, i * P:(i + 1) * P], ek_wide[:, u * HD:(u + TB) * HD], k.ident[:, :])
            m.then_inc(ek_turned, 1)

        @block.scalar
        def _(act):
            act.wait_ge(w_in, 48)
            for n in range(NCH):
                act.wait_ge(q_ready, n + 1)
                act.activation(a.qT[:, n * CH:(n + 1) * CH], ps[:, n % 2, :], ACT.Identity,
                               bias=bqk[:, 0:1]).then_inc(q_copied, 1)
            act.wait_ge(ek_turned, 1)
            act.activation(a.e_rel[0:64, :], ps[0:64, 6, 0:3 * P], ACT.Copy).then_inc(ek_copied, 1)

        @block.vector
        def _(dve):
            dve.wait_ge(w_in, 48)
            dve.wait_ge(table_in, 16 * TABLES)
            dve.tensor_scalar(a.gate_bias[:, :], k.mod[:, 0, 2, :], a.bproj[:, 0:1], None, ALU.mult)
            for n in range(NCH):
                dve.wait_ge(k_ready, n + 1)
                dve.tensor_scalar(a.kT[:, n * CH:(n + 1) * CH], ps[:, 2 + n % 2, :], bqk[:, 1:2], QK_SCALE,
                                  ALU.add, ALU.mult).then_inc(k_copied, 1)
                dve.wait_ge(v_ready, n + 1)
                out = a.v[:, 4 * n * C:4 * (n + 1) * C]
                dve.tensor_tensor(view(out, 0, [[C, 4], [1, C]]), ps[:, 4 + n % 2, :].rearrange("p (j c) -> p j c", j=4),
                                  view(bv[:, :], 0, [[0, 4], [1, C]]), ALU.add).then_inc(v_copied, 1)


def rel_attention_phase(nc, k, a):
    with ExitStack() as ctx:
        def sb(n, s, dt=F32):
            return ctx.enter_context(nc.sbuf_tensor(n, s, dt))

        def sem(n):
            return phase_semaphore(nc, k, n)

        prob = sb("prob", [P, 4, QUAD, T])
        neg_max = sb("neg_max", [P, 4, QUAD])
        den = sb("den", [P, 4, QUAD])
        rden = sb("rden", [P, 4, QUAD])
        probT = sb("probT", [P, 2, 2, CH])
        y_all = sb("y_all", [64, CH])
        y_v, y_rel = sb("y_v", [P, 2, P]), sb("y_rel", [P, 2, HALF_TILES * 64])
        v_high = sb("v_high", [P, 2, 2, 64])
        upd = sb("upd", [P, 2, P])
        ps_s = ctx.enter_context(nc.psum_tensor("ps_s", [P, 2, QUAD, T], F32))
        ps_t = ctx.enter_context(nc.psum_tensor("ps_t", [P, 2, CH], F32))
        ps_y = ctx.enter_context(nc.psum_tensor("ps_y", [P, CH], F32))
        ps_m = ctx.enter_context(nc.psum_tensor("ps_m", [P, CH], F32))
        score, maxed, expd, rden_ready, probs = sem("score"), sem("maxed"), sem("expd"), sem("rden_ready"), sem("probs")
        turned, turned_out, pv, masked = sem("turned"), sem("turned_out"), sem("pv"), sem("masked")
        spread, q_rel_ready, q_diag_ready, v_ready = sem("spread_s"), sem("q_rel_ready"), sem("q_diag_ready"), sem("v_ready")
        y_ready, projd, gated, added = sem("y_ready"), sem("projd"), sem("gated"), sem("added")
        block = ctx.enter_context(nc.Block())

        def turns(b, q):
            return 12 * b + (q if q < 4 else 4 + 2 * (q - 4))

        def quad(b, q):
            return b + q // NQ, q % NQ

        def exists(b, q=0):
            return not isinstance(b, int) or 0 <= b < B

        def sequences(eng, body):
            body(-1)
            body(0)
            with eng.Fori(1, B - 1) as b:
                body(b)
            body(B - 1)

        def spread_group(b, q):
            if q < 1:
                return b, 1, 3
            if q < 5:
                return b + 1, 0, q - 1
            return b + 1, 1, q - 5

        @block.tensor
        def _(pe):
            def body(b):
                for q in range(NQ):
                    n = NQ * b + q
                    sb_, sq_ = quad(b, q + 2)
                    if exists(sb_):
                        sn = n + 2
                        half, slot, r = sq_ // 4, sq_ // 4, q % 2
                        if sq_ % 4 == 0:
                            c = 2 * sb_ + half
                            pe.wait_ge(q_diag_ready, c + 1)
                            pe.wait_ge(q_rel_ready, NG * c + NG)
                        wait(pe, expd, sn - 1)
                        keys = 4 * TB * (sq_ + 1)
                        for j in range(QUAD):
                            i = QUAD * sq_ + j
                            rows = slice((i % HALF_TILES) * P, (i % HALF_TILES + 1) * P)
                            pe.matmul(ps_s[:, r, j, 0:keys], a.q_diag[:, slot, rows], a.kT[:, bass.ds(sb_ * T, keys)],
                                      start=True, stop=False)
                            m = pe.matmul(ps_s[:, r, j, 0:keys], a.q_rel[0:64 + TB, slot, rows],
                                          a.e_rel[0:64 + TB, T - TB * i:T - TB * i + keys], start=False, stop=True)
                        m.then_inc(score, 1)
                    if q == 1 or q == 5:
                        c = 2 * b + (0 if q == 5 else -1)
                        if exists(b) and not (isinstance(c, int) and c < 0):
                            project(b, q, c)
                    if exists(b):
                        pe.wait_ge(probs, n + 1)
                        wait(pe, turned_out, turns(b, q))
                        pe.nop(nofuse=True)
                        keys = 4 * TB * (q + 1)
                        for ch in range(1 if q < 4 else 2):
                            ks = min(P, keys - ch * P)
                            for j in range(QUAD):
                                m = pe.transpose(ps_t[0:ks, ch, j * P:(j + 1) * P],
                                                 prob[:, q % 4, j, ch * P:ch * P + ks], k.ident[:, :])
                            m.then_inc(turned, 1)
                    pb, pq = quad(b, q - 1)
                    if exists(pb):
                        values(pb, pq, n - 1)
                    gb, half, g = spread_group(b, q)
                    if exists(gb):
                        c = 2 * gb + half
                        wait(pe, q_rel_ready, NG * c + g)
                        wait(pe, gated, 2 * b + (-1 if q < 1 else 0 if q < 5 else 1))
                        pe.nop(nofuse=True)
                        for h in range(2):
                            w = (4 * g + 2 * h) * TB * HD
                            m = pe.matmul(ps_m[:, h * P:(h + 1) * P], a.spread[:, w:w + P],
                                          a.qT[:, bass.ds(gb * T + half * P, P)], start=True, stop=True)
                        m.then_inc(spread, 1)

            def values(b, q, n):
                pe.wait_ge(turned_out, turns(b, q) + (1 if q < 4 else 2))
                pe.wait_ge(v_ready, n + (4 if q % 4 == 0 else 1))
                wait(pe, masked, n)
                keys = 4 * TB * (q + 1)
                chunks = [(ch, min(P, keys - ch * P)) for ch in range(1 if q < 4 else 2)]
                for j in range(QUAD):
                    for ch, ks in chunks:
                        at = ve_block(QUAD * q + j, ch) * VE_W
                        pe.matmul(ps_y[:, j * P:(j + 1) * P], a.ve[0:ks, at:at + P], probT[0:ks, q % 2, ch, j * P:(j + 1) * P],
                                  start=ch == 0, stop=ch == len(chunks) - 1)
                for ch, ks in chunks:
                    m = pe.matmul(view(ps_y[0:64, :], 64, [[P, QUAD], [1, 64]]), v_high[0:ks, q // 4, ch, :],
                                  view(probT[0:ks, q % 2, ch, :], 64, [[P, QUAD], [1, 64]]),
                                  start=ch == 0, stop=ch == len(chunks) - 1)
                m.then_inc(pv, 1)

            def project(b, q, c):
                pe.wait_ge(y_ready, 4 * c + 4)
                wait(pe, gated, c)
                gb, half, _ = spread_group(b, q - 1)
                pe.wait_ge(q_rel_ready, NG * (2 * gb + half + 1) if exists(gb) else NG * HALVES)
                slot = 1 if q == 1 else 0
                pe.matmul(ps_m[:, 0:P], a.wproj[:, :], y_v[:, slot, :], start=True, stop=False)
                for h in range(8):
                    m = pe.matmul(ps_m[:, 0:P], a.wproj_rel[:, h, :],
                                  view(y_rel[:, slot, :], h * TB, [[64, HALF_TILES], [1, TB]]), start=False, stop=h == 7)
                m.then_inc(projd, 1)

            sequences(pe, body)
            values(B - 1, NQ - 1, NQ * B - 1)
            project(B, 1, HALVES - 1)

        @block.vector
        def _(dve):
            def body(b):
                for q in range(NQ):
                    n = NQ * b + q
                    sb_, sq_ = quad(b, q + 2)
                    sn = n + 2
                    keys = 4 * TB * (sq_ + 1)
                    if exists(sb_):
                        dve.wait_ge(score, sn + 1)
                        dve.tensor_reduce(neg_max[:, sq_ % 4, :], ps_s[:, q % 2, :, 0:keys], AX.X, ALU.max,
                                          negate=True).then_inc(maxed, 1)
                    pb, pq = quad(b, q - 1)
                    if exists(pb):
                        mask(pb, pq, n - 1)
                    vb, vq = quad(b, q + 6)
                    if exists(vb):
                        place_values(vb, vq, n + 6)
                    if exists(sb_):
                        dve.wait_ge(expd, sn + 1)
                        dve.reciprocal(rden[:, sq_ % 4, :], den[:, sq_ % 4, :]).then_inc(rden_ready, 1)
                    if (q == 2 or q == 6) and exists(b):
                        c = 2 * b + (0 if q == 6 else -1)
                        if not (isinstance(c, int) and c < 0):
                            add(c, 1 if q == 2 else 0)
                    gb, half, g = spread_group(b, q)
                    if exists(gb):
                        c = 2 * gb + half
                        dve.wait_ge(spread, NG * c + g + 1)
                        wait(dve, score, 4 * c - 4)
                        for x in range(2):
                            r = slice(64 * x, 64 * x + 64)
                            out = view(a.q_rel[0:64, half, :], (4 * g + x) * TB, [[2 * TB, 2], [P, HALF_TILES], [1, TB]])
                            m = dve.tensor_tensor(out, view(ps_m[r, :], 0, [[P, 2], [TB, HALF_TILES], [1, TB]]),
                                                  view(a.t_mask[r, :], 0, [[0, 2], [0, HALF_TILES], [1, TB]]), ALU.mult)
                        m.then_inc(q_rel_ready, 1)

            def mask(b, q, n):
                dve.wait_ge(pv, n + 1)
                if q % 4 == 0:
                    wait(dve, projd, 2 * b + q // 4 - 1)
                for hh in range(2):
                    out = y_rel[64 * (1 - hh):64 * (2 - hh), q // 4, (q % 4) * QUAD * 64:(q % 4 + 1) * QUAD * 64]
                    dve.tensor_tensor(view(out, 0, [[64, QUAD], [1, 64]]), view(ps_y[64:P, :], 64 * hh, [[P, QUAD], [1, 64]]),
                                      view(a.y_mask[64:P, 0, :], 0, [[0, QUAD], [1, 64]]), ALU.mult)
                wait(dve, y_ready, n)
                dve.nop(nofuse=True)
                dve.tensor_tensor(y_all[:, :], ps_y[0:64, :], view(a.y_mask[0:64, 0, :], 0, [[0, QUAD], [1, P]]),
                                  ALU.mult).then_inc(masked, 1)
                dve.wait_ge(masked, n + 1)
                for hh in range(2):
                    out = y_v[64 * hh:64 * hh + 64, q // 4, (q % 4) * QUAD * TB:(q % 4 + 1) * QUAD * TB]
                    m = dve.tensor_reduce(view(out, 0, [[TB, QUAD], [1, TB]]),
                                          view(y_all[:, :], 64 * hh, [[P, QUAD], [1, TB], [TB, 8]]), AX.X, ALU.add)
                m.then_inc(y_ready, 1)

            def place_values(b, q, n):
                wait(dve, pv, n - 7)
                dve.nop(nofuse=True)
                if q % 4 == 3:
                    for ch in range(1 + q // 4):
                        dve.tensor_copy(v_high[:, q // 4, ch, :], a.v[:, bass.ds(b * 2 * C + ch * C + 64, 64)])
                for ch in range(1 if q < 4 else 2):
                    at = ve_block(QUAD * q, ch) * VE_W
                    m = dve.tensor_copy(view(a.ve[:, :], at, [[VE_W, QUAD], [1, 64]]),
                                        view(a.v[:, bass.ds(b * 2 * C + ch * C, 64)], 0, [[0, QUAD], [1, 64]]))
                m.then_inc(v_ready, 1)

            def add(c, half):
                dve.wait_ge(gated, c + 1)
                xs = k.xT[:, bass.ds(c * P, P)]
                dve.tensor_tensor(xs, xs, upd[:, half, :], ALU.add).then_inc(added, 1)

            sequences(dve, body)
            mask(B - 1, NQ - 1, NQ * B - 1)
            add(HALVES - 1, 1)

        @block.scalar
        def _(act):
            def body(b):
                for q in range(NQ):
                    n = NQ * b + q
                    sb_, sq_ = quad(b, q + 2)
                    sn = n + 2
                    keys = 4 * TB * (sq_ + 1)
                    if exists(sb_):
                        act.wait_ge(maxed, sn + 1)
                        ob, oq = quad(sb_, sq_ - 3)
                        wait(act, turned, turns(ob, oq))
                        for j in range(QUAD):
                            m = act.activation(prob[:, sq_ % 4, j, 0:keys], ps_s[:, q % 2, j, 0:keys], ACT.Exp,
                                               bias=neg_max[:, sq_ % 4, j:j + 1], accum_out=den[:, sq_ % 4, j:j + 1])
                        m.then_inc(expd, 1)
                    if exists(b):
                        if q == 1 or q == 5:
                            c = 2 * b + (0 if q == 5 else -1)
                            if not (isinstance(c, int) and c < 0):
                                gate(b if q == 5 else b - 1, 0 if q == 5 else 1, c)
                        keys = 4 * TB * (q + 1)
                        wait(act, pv, n - 1)
                        for ch in range(1 if q < 4 else 2):
                            ks = min(P, keys - ch * P)
                            act.wait_ge(turned, turns(b, q) + ch + 1)
                            act.activation(probT[0:ks, q % 2, ch, :], ps_t[0:ks, ch, :], ACT.Copy).then_inc(turned_out, 1)

            def gate(b, half, c):
                act.wait_ge(projd, c + 1)
                wait(act, added, c - 1)
                act.activation(upd[:, half, :], ps_m[:, 0:P], ACT.Identity, scale=k.mod[:, 0, 2, bass.ds(b, 1)],
                               bias=a.gate_bias[:, bass.ds(b, 1)]).then_inc(gated, 1)

            sequences(act, body)
            gate(B - 1, 1, HALVES - 1)

        @block.gpsimd
        def _(pool):
            def body(b):
                for q in range(NQ):
                    n = NQ * b + q
                    if q == 2 or q == 6:
                        half = 0 if q == 2 else 1
                        if exists(b + 1):
                            c = 2 * (b + 1) + half
                            wait(pool, score, 4 * c - 4)
                            out = a.q_diag[:, half, :]
                            q_in = a.qT[:, bass.ds((b + 1) * T + half * P, P)]
                            pool.tensor_tensor(view(out, 0, [[P, HALF_TILES], [TB, H], [1, TB]]),
                                               view(q_in, 0, [[TB, HALF_TILES], [0, H], [1, TB]]),
                                               view(a.head_mask[:, :], 0, [[0, HALF_TILES], [1, H], [0, TB]]),
                                               ALU.mult).then_inc(q_diag_ready, 1)
                    sb_, sq_ = quad(b, q + 2)
                    if exists(sb_):
                        keys = 4 * TB * (sq_ + 1)
                        pool.wait_ge(rden_ready, n + 3)
                        ps_ = prob[:, sq_ % 4, :, 0:keys]
                        pool.tensor_tensor(ps_, ps_, view(rden[:, sq_ % 4, :], 0, [[1, QUAD], [0, keys]]),
                                           ALU.mult).then_inc(probs, 1)

            sequences(pool, body)


KEPT = max(1, int(T * 0.3))
PARTS = ((0, 6), (6, 6), (12, 4))


def sparse_project_phase(nc, d, k, a):
    with ExitStack() as ctx:
        def sb(n, s, dt=F32):
            return ctx.enter_context(nc.sbuf_tensor(n, s, dt))

        def sem(n):
            return phase_semaphore(nc, k, n)

        w_rows = sb("w_rows1", [P, 4, C])
        wi1_rows = sb("wi1_rows", [C // 2, C])
        w_T = sb("w_T1", [P, 3 * C])
        wi1_T = sb("wi1_T", [P, C // 2])
        bq, bi1, bi2, wi2 = sb("bq1", [P, 1]), sb("bi1", [C // 2, 1]), sb("bi2", [P, 1]), sb("wi2", [C // 2, 1])
        wi2_rep = sb("wi2_rep", [C // 2, P])
        bkv = sb("bkv1", [P, 2 * C])
        hid = sb("hid1", [C // 2, 2, CH])
        imp_row = sb("imp_row", [P, NTOK])
        imp_col = sb("imp_col", [P, NT])
        picked = sb("picked", [P, P])
        compared = sb("compared", [P, 2, T])
        before = sb("before", [P, 2, T])
        above = sb("above", [P, NT])
        tied = sb("tied", [P, NT])
        ps = ctx.enter_context(nc.psum_tensor("ps_proj1", [P, 8, CH], F32))
        w_in, w_turned, w_copied = sem("w_in1"), sem("w_turned1"), sem("w_copied1")
        pool_step, const_ready, wi2_ready = sem("pool_step3"), sem("const_ready3"), sem("wi2_ready")
        q_ready, kv_ready, hid_ready, imp_ready = sem("q_ready1"), sem("kv_ready1"), sem("hid_ready1"), sem("imp_ready1")
        q_copied, kv_copied, hid_copied, imp_copied = sem("q_copied1"), sem("kv_copied1"), sem("hid_copied1"), sem("imp_copied1")
        col_ready, ranked = sem("col_ready"), sem("ranked")
        block = ctx.enter_context(nc.Block())

        def column(name, n):
            return d[name].rearrange("(p o) -> p o", o=1)[0:n, :]

        @block.sync
        def _(sp):
            for i, name in enumerate(("wq", "wk", "wv", "wo")):
                sp.dma_start(w_rows[:, i, :], d["L1_attn_" + name]).then_inc(w_in, 16)
            sp.dma_start(wi1_rows[:, :], d["L1_attn_wi1"]).then_inc(w_in, 16)
            sp.dma_start(bq[:, :], column("L1_attn_bq", P), allow_slow_non_contiguous=True).then_inc(w_in, 16)
            sp.dma_start(a.bo[:, :], column("L1_attn_bo", P), allow_slow_non_contiguous=True).then_inc(w_in, 16)
            sp.dma_start(bi1[:, :], column("L1_attn_bi1", C // 2), allow_slow_non_contiguous=True).then_inc(w_in, 16)
            sp.dma_start(wi2[:, :], d["L1_attn_wi2"].rearrange("o p -> p o"), allow_slow_non_contiguous=True).then_inc(w_in, 16)
            sp.dma_start(bi2[:, :], bass.AP(d["L1_attn_bi2"].tensor, 0, [[0, P], [1, 1]]),
                         allow_slow_non_contiguous=True).then_inc(w_in, 16)
            for i, name in enumerate(("bk", "bv")):
                sp.dma_start(bkv[:, i * C:(i + 1) * C],
                             bass.AP(d["L1_attn_" + name].tensor, 0, [[0, P], [1, C]])).then_inc(w_in, 16)

        @block.gpsimd
        def _(pool):
            step = Chain(pool, pool_step)
            step(pool.memset(before[:, :, :], 1.0))
            step(pool.affine_select(out=before[:, :, :], in_=before[:, :, :], compare_op=ALU.is_gt, fill=0.0, base=0,
                                    pattern=[[P, 2], [-1, T]], channel_multiplier=1))
            m = a.group_mask[:, :, :]
            step(pool.memset(m, 1.0))
            step(pool.affine_select(out=m, in_=m, compare_op=ALU.is_ge, fill=0.0, base=0,
                                    pattern=[[-HD, 4], [1, 4 * HD]], channel_multiplier=0))
            step(pool.affine_select(out=m, in_=m, compare_op=ALU.is_ge, fill=0.0, base=HD - 1,
                                    pattern=[[HD, 4], [-1, 4 * HD]], channel_multiplier=0))
            m = a.head_mask[:, :]
            step(pool.memset(m, 1.0))
            step(pool.affine_select(out=m, in_=m, compare_op=ALU.is_ge, fill=0.0, base=0,
                                    pattern=[[-HD, H]], channel_multiplier=1))
            step(pool.affine_select(out=m, in_=m, compare_op=ALU.is_ge, fill=0.0, base=HD - 1,
                                    pattern=[[HD, H]], channel_multiplier=-1))
            pool.iota(a.places[:, :], [[1, KEPT]], base=0, channel_multiplier=0,
                      allow_small_or_imprecise_dtypes=True).then_inc(const_ready, 1)

        @block.tensor
        def _(pe):
            pe.wait_ge(w_in, 16 * 12)
            for i in range(4):
                pe.transpose(ps[:, 0, i * C:(i + 1) * C], w_rows[:, i, :], k.ident[:, :])
            pe.transpose(ps[:, 1, 0:C // 2], wi1_rows[:, :], k.ident[0:C // 2, 0:C // 2]).then_inc(w_turned, 1)
            pe.wait_ge(w_copied, 3)
            pe.wait_ge(wi2_ready, 1)
            for n in range(NCH + 1):
                if n < NCH:
                    h = k.hT[:, n * CH:(n + 1) * CH]
                    wait(pe, hid_copied, n)
                    pe.matmul(ps[0:C // 2, 4, :], wi1_T[:, :], h, start=True, stop=True).then_inc(hid_ready, 1)
                    wait(pe, q_copied, n - 1)
                    pe.matmul(ps[:, n % 2, :], w_T[:, 0:C], h, start=True, stop=True).then_inc(q_ready, 1)
                if n >= 1:
                    m = n - 1
                    pe.wait_ge(hid_copied, m + 1)
                    wait(pe, imp_copied, m)
                    pe.matmul(ps[:, 5, :], wi2_rep[:, :], hid[:, m % 2, :], start=True, stop=True).then_inc(imp_ready, 1)
                if n < NCH:
                    for g in range(2):
                        u = 2 * n + g
                        wait(pe, kv_copied, u - 1)
                        for j in range(2):
                            t = 4 * n + 2 * g + j
                            m = pe.matmul(ps[:, 2 + u % 2, j * 2 * C:(j + 1) * 2 * C], k.hT[:, t * P:(t + 1) * P],
                                          w_T[:, C:3 * C], start=True, stop=True)
                        m.then_inc(kv_ready, 1)

        @block.scalar
        def _(act):
            act.wait_ge(w_turned, 1)
            act.activation(w_T[:, :], ps[:, 0, 0:3 * C], ACT.Copy).then_inc(w_copied, 1)
            act.activation(a.wo_T[:, :], ps[:, 0, 3 * C:4 * C], ACT.Copy).then_inc(w_copied, 1)
            act.activation(wi1_T[:, :], ps[:, 1, 0:C // 2], ACT.Copy).then_inc(w_copied, 1)
            for n in range(NCH + 1):
                if n < NCH:
                    act.wait_ge(hid_ready, n + 1)
                    wait(act, imp_ready, n - 1)
                    act.activation(hid[:, n % 2, :], ps[0:C // 2, 4, :], ACT.Relu, bias=bi1[:, 0:1]).then_inc(hid_copied, 1)
                if n >= 1:
                    act.wait_ge(imp_ready, n)
                    act.activation(imp_row[:, (n - 1) * CH:n * CH], ps[:, 5, :], ACT.Identity, bias=bi2[:, 0:1]).then_inc(imp_copied, 1)

        @block.vector
        def _(dve):
            dve.wait_ge(w_in, 16 * 12)
            dve.tensor_scalar(wi2_rep[:, :], k.ones[0:C // 2, :], wi2[:, 0:1], None, ALU.mult).then_inc(wi2_ready, 1)
            dve.tensor_scalar(a.gate_bias[:, :], k.mod[:, 1, 2, :], a.bo[:, 0:1], None, ALU.mult)
            for n in range(NCH):
                dve.wait_ge(q_ready, n + 1)
                dve.tensor_scalar(a.qT[:, n * CH:(n + 1) * CH], ps[:, n % 2, :], bq[:, 0:1], QK_SCALE,
                                  ALU.add, ALU.mult).then_inc(q_copied, 1)
                for g in range(2):
                    u = 2 * n + g
                    dve.wait_ge(kv_ready, u + 1)
                    dve.tensor_tensor(a.kv[:, 2 * u:2 * u + 2, :], ps[:, 2 + u % 2, :].rearrange("p (j c) -> p j c", j=2),
                                      view(bkv[:, :], 0, [[0, 2], [1, 2 * C]]), ALU.add).then_inc(kv_copied, 1)
            dve.wait_ge(const_ready, 1)
            dve.wait_ge(imp_copied, NCH)
            for t in range(NT):
                dve.scalar_tensor_tensor(out=picked[:, :], in0=imp_row[:, t * P:(t + 1) * P], scalar=1.0,
                                         in1=k.ident[:, :], op0=ALU.mult, op1=ALU.mult,
                                         accum_out=imp_col[:, t:t + 1]).then_inc(col_ready, 1)
                dve.wait_ge(col_ready, t + 1)
            for t in range(NT):
                row = imp_row[:, t // 2 * T:(t // 2 + 1) * T]
                dve.tensor_scalar(compared[:, 0, :], row, imp_col[:, t:t + 1], 0.0, ALU.is_gt, ALU.add,
                                  accum_out=above[:, t:t + 1]).then_inc(ranked, 1)
                dve.scalar_tensor_tensor(out=compared[:, 1, :], in0=row, scalar=imp_col[:, t:t + 1],
                                         in1=before[:, t % 2, :], op0=ALU.is_equal, op1=ALU.mult,
                                         accum_out=tied[:, t:t + 1]).then_inc(ranked, 1)
                dve.wait_ge(ranked, 2 * t + 2)
            dve.tensor_tensor(a.rank[:, :], above[:, :], tied[:, :], ALU.add)


def sparse_attention_phase(nc, k, a):
    with ExitStack() as ctx:
        def sb(n, s, dt=F32):
            return ctx.enter_context(nc.sbuf_tensor(n, s, dt))

        def sem(n):
            return phase_semaphore(nc, k, n)

        select = sb("select", [P, 2, 2, KEPT])
        kv_kept = sb("kv_kept", [KEPT, 2, 2 * C])
        k_diag = sb("k_diag", [P, 2, H * KEPT])
        v_diag = sb("v_diag", [KEPT, 2, H, 4 * HD])
        q_now = sb("q_now", [P, 2, T])
        prob = sb("prob1", [P, 2, H, KEPT])
        top = sb("top1", [P, 2, H])
        den = sb("den1", [P, 2, H])
        rden = sb("rden1", [P, 2, H])
        probT = sb("probT1", [KEPT, 2, CH])
        y_T = sb("y_T1", [P, 2, P])
        upd = sb("upd1", [P, 2, P])
        ps_s = ctx.enter_context(nc.psum_tensor("ps_s1", [P, 3, CH], F32))
        ps_g = ctx.enter_context(nc.psum_tensor("ps_g1", [P, CH], F32))
        ps_t = ctx.enter_context(nc.psum_tensor("ps_t1", [P, 2, CH], F32))
        ps_y = ctx.enter_context(nc.psum_tensor("ps_y1", [P, CH], F32))
        ps_o = ctx.enter_context(nc.psum_tensor("ps_o1", [P, CH], F32))
        selected, gathered, kept, k_turned = sem("selected"), sem("gathered"), sem("kept"), sem("k_turned")
        k_ready, v_ready, q_ready = sem("k_ready4"), sem("v_ready4"), sem("q_ready4")
        score, maxed, shifted, expd, summed = sem("score1"), sem("maxed1"), sem("shifted1"), sem("expd1"), sem("summed1")
        rden_ready, probs, turned, turned_out = sem("rden1_ready"), sem("probs1"), sem("turned1"), sem("turned_out1")
        pv, y_out, projd, gated, added = sem("pv1"), sem("y_out1"), sem("projd1"), sem("gated1"), sem("added1")
        block = ctx.enter_context(nc.Block())

        def exists(w):
            return not isinstance(w, int) or 0 <= w < HALVES

        def pairs(eng, step):
            def body(i):
                for s in range(4):
                    step(4 * i + s, 2 * i + s // 2, s)
            body(-1)
            body(0)
            with eng.Fori(1, B // 2 - 1) as i:
                body(i)
            body(B // 2 - 1)

        @block.tensor
        def _(pe):
            def scores(w, b, s, part):
                first, count = PARTS[part]
                if part == 0:
                    pe.wait_ge(k_ready, b + 1)
                    pe.wait_ge(q_ready, b + 1)
                wait(pe, shifted, 3 * w + part - 2)
                pe.matmul(ps_s[:, part, 0:count * KEPT], q_now[:, s // 2, (s % 2) * P:(s % 2 + 1) * P],
                          k_diag[:, s // 2, first * KEPT:(first + count) * KEPT], start=True, stop=True).then_inc(score, 1)

            def turn(w, s, g):
                pe.wait_ge(probs, 3 * w + (1, 2, 2, 3)[g])
                wait(pe, turned_out, 4 * w + g - 1)
                for h in range(4):
                    m = pe.transpose(ps_t[0:KEPT, g % 2, h * P:(h + 1) * P], prob[:, s % 2, 4 * g + h, :], k.ident[:, :])
                m.then_inc(turned, 1)

            def values(w, b, s, g):
                pe.wait_ge(turned_out, 4 * w + g + 1)
                if g == 0:
                    pe.wait_ge(v_ready, b + 1)
                    wait(pe, y_out, w - 1)
                pe.nop(nofuse=True)
                for h in range(4):
                    m = pe.matmul(ps_y[4 * HD * g:4 * HD * (g + 1), (s % 2) * P:(s % 2 + 1) * P],
                                  v_diag[:, s // 2, 4 * g + h, :], probT[:, g % 2, h * P:(h + 1) * P],
                                  start=h == 0, stop=h == 3)
                m.then_inc(pv, 1)

            def project(w, s):
                pe.wait_ge(y_out, w + 1)
                wait(pe, gated, w)
                pe.matmul(ps_o[:, 0:P], a.wo_T[:, :], y_T[:, s % 2, :], start=True, stop=True).then_inc(projd, 1)

            def step(w, b, s):
                ahead = s % 2 == 0 and exists(2 * (b + 1))
                if ahead:
                    pe.wait_ge(selected, b + 2)
                    wait(pe, kept, b + 1)
                    for ch in range(2):
                        m = pe.matmul(ps_g[0:KEPT, 0:2 * C], select[:, (s // 2 + 1) % 2, ch, :],
                                      a.kv[:, bass.ds(2 * (b + 1) + ch, 1), :], start=ch == 0, stop=ch == 1)
                    m.then_inc(gathered, 1)
                now, nxt = exists(w), exists(w + 1)
                nb, ns = b + s % 2, (s + 1) % 4
                if now:
                    turn(w, s, 0)
                if nxt:
                    scores(w + 1, nb, ns, 0)
                if now:
                    turn(w, s, 1)
                    values(w, b, s, 0)
                if nxt:
                    scores(w + 1, nb, ns, 1)
                if now:
                    turn(w, s, 2)
                    values(w, b, s, 1)
                if ahead:
                    pe.wait_ge(kept, b + 2)
                    wait(pe, k_ready, b + 1)
                    pe.transpose(ps_g[:, 2 * C:2 * C + KEPT], kv_kept[:, (s // 2 + 1) % 2, 0:C],
                                 k.ident[0:KEPT, 0:KEPT]).then_inc(k_turned, 1)
                if nxt:
                    scores(w + 1, nb, ns, 2)
                if now:
                    turn(w, s, 3)
                    values(w, b, s, 2)
                if exists(w - 1) and exists(w):
                    project(w - 1, s + 1)
                if now:
                    values(w, b, s, 3)

            pairs(pe, step)
            project(HALVES - 1, HALVES - 1)

        @block.vector
        def _(dve):
            def shift(w, s, part):
                first, count = PARTS[part]
                r = slice(first, first + count)
                scores = ps_s[:, part, 0:count * KEPT].rearrange("p (h r) -> p h r", h=count)
                dve.wait_ge(score, 3 * w + part + 1)
                dve.tensor_reduce(top[:, s % 2, r], scores, AX.X, ALU.max).then_inc(maxed, 1)
                dve.wait_ge(maxed, 3 * w + part + 1)
                wait(dve, turned, 4 * w - 4)
                dve.tensor_tensor(prob[:, s % 2, r, :], scores, view(top[:, s % 2, r], 0, [[1, count], [0, KEPT]]),
                                  ALU.subtract).then_inc(shifted, 1)

            def total(w, s, part):
                first, count = PARTS[part]
                r = slice(first, first + count)
                dve.wait_ge(expd, 3 * w + part + 1)
                dve.tensor_reduce(den[:, s % 2, r], prob[:, s % 2, r, :], AX.X, ALU.add).then_inc(summed, 1)
                dve.wait_ge(summed, 3 * w + part + 1)
                dve.reciprocal(rden[:, s % 2, r], den[:, s % 2, r]).then_inc(rden_ready, 1)

            def step(w, b, s):
                ahead = s % 2 == 0 and exists(2 * (b + 1))
                slot = (s // 2 + 1) % 2
                if ahead:
                    wait(dve, gathered, b)
                    dve.nop(nofuse=True)
                    for ch in range(2):
                        m = dve.tensor_scalar(select[:, slot, ch, :], a.places[:, :],
                                              a.rank[:, bass.ds(2 * (b + 1) + ch, 1)], None, ALU.is_equal)
                    m.then_inc(selected, 1)
                nxt, ns = exists(w + 1), (s + 1) % 4
                if nxt:
                    shift(w + 1, ns, 0)
                    shift(w + 1, ns, 1)
                    total(w + 1, ns, 0)
                if ahead:
                    dve.wait_ge(k_turned, b + 2)
                    wait(dve, score, 6 * (b + 1) - 6)
                    dve.tensor_tensor(k_diag[:, slot, :].rearrange("p (h r) -> p h r", h=H),
                                      view(ps_g[:, 2 * C:2 * C + KEPT], 0, [[0, H], [1, KEPT]]),
                                      view(a.head_mask[:, :], 0, [[1, H], [0, KEPT]]), ALU.mult).then_inc(k_ready, 1)
                if nxt:
                    shift(w + 1, ns, 2)
                    total(w + 1, ns, 1)
                    total(w + 1, ns, 2)
                if exists(w - 1) and exists(w):
                    add(w - 1, s + 1)

            def add(w, s):
                dve.wait_ge(gated, w + 1)
                xs = k.xT[:, bass.ds(w * P, P)]
                dve.tensor_tensor(xs, xs, upd[:, s % 2, :], ALU.add).then_inc(added, 1)

            pairs(dve, step)
            add(HALVES - 1, HALVES - 1)

        @block.scalar
        def _(act):
            def exp(w, s, part):
                first, count = PARTS[part]
                act.wait_ge(shifted, 3 * w + part + 1)
                p = prob[:, s % 2, first:first + count, :]
                act.activation(p, p, ACT.Exp).then_inc(expd, 1)

            def copy(w, s, g):
                act.wait_ge(turned, 4 * w + g + 1)
                wait(act, pv, 4 * w + g - 1)
                act.activation(probT[:, g % 2, :], ps_t[0:KEPT, g % 2, :], ACT.Copy).then_inc(turned_out, 1)

            def gate(w, b, s):
                act.wait_ge(projd, w + 1)
                wait(act, added, w - 1)
                act.nop(nofuse=True)
                act.activation(upd[:, s % 2, :], ps_o[:, 0:P], ACT.Identity, scale=k.mod[:, 1, 2, bass.ds(b, 1)],
                               bias=a.gate_bias[:, bass.ds(b, 1)]).then_inc(gated, 1)

            def step(w, b, s):
                if s % 2 == 0 and exists(2 * (b + 1)):
                    act.wait_ge(gathered, b + 2)
                    wait(act, v_ready, b)
                    act.activation(kv_kept[:, (s // 2 + 1) % 2, :], ps_g[0:KEPT, 0:2 * C], ACT.Copy).then_inc(kept, 1)
                now, nxt, ns = exists(w), exists(w + 1), (s + 1) % 4
                for g in range(4):
                    if now:
                        copy(w, s, g)
                    if nxt and g < 3:
                        exp(w + 1, ns, g)
                if exists(w - 1) and exists(w):
                    gate(w - 1, b - (1 - s % 2), s + 1)
                if now:
                    act.wait_ge(pv, 4 * w + 4)
                    wait(act, projd, w - 1)
                    act.activation(y_T[:, s % 2, :], ps_y[:, (s % 2) * P:(s % 2 + 1) * P], ACT.Copy).then_inc(y_out, 1)

            pairs(act, step)
            gate(HALVES - 1, B - 1, HALVES - 1)

        @block.gpsimd
        def _(pool):
            def step(w, b, s):
                if s % 2 == 0 and exists(2 * (b + 1)):
                    slot = (s // 2 + 1) % 2
                    wait(pool, score, 6 * (b + 1) - 6)
                    pool.nop(nofuse=True)
                    pool.tensor_copy(q_now[:, slot, :], a.qT[:, bass.ds((b + 1) * T, T)]).then_inc(q_ready, 1)
                    pool.wait_ge(kept, b + 2)
                    wait(pool, pv, 8 * (b + 1) - 8)
                    pool.tensor_tensor(view(v_diag[:, slot, 0, :], 0, [[16 * HD, 4], [4 * HD, 4], [1, 4 * HD]]),
                                       view(kv_kept[:, slot, C:2 * C], 0, [[4 * HD, 4], [0, 4], [1, 4 * HD]]),
                                       view(a.group_mask[:, 0, :], 0, [[0, 4], [4 * HD, 4], [1, 4 * HD]]),
                                       ALU.mult).then_inc(v_ready, 1)
                if exists(w + 1):
                    for part, (first, count) in enumerate(PARTS):
                        r = slice(first, first + count)
                        ns = (s + 1) % 2
                        pool.wait_ge(rden_ready, 3 * (w + 1) + part + 1)
                        pool.tensor_tensor(prob[:, ns, r, :], prob[:, ns, r, :],
                                           view(rden[:, ns, r], 0, [[1, count], [0, KEPT]]), ALU.mult).then_inc(probs, 1)

            pairs(pool, step)


def layer1_attention(nc, d, k):
    with ExitStack() as ctx:
        def sb(n, s, dt=F32):
            return ctx.enter_context(nc.sbuf_tensor(n, s, dt))

        a = Place()
        a.qT, a.kv = sb("qT1", [P, NTOK]), sb("kv1", [P, NT, 2 * C])
        a.wo_T, a.bo, a.gate_bias = sb("wo_T", [P, C]), sb("bo1", [P, 1]), sb("gate_bias1", [P, B])
        a.rank, a.places = sb("rank", [P, NT]), sb("places", [P, KEPT])
        a.group_mask, a.head_mask = sb("group_mask", [KEPT, 4, 4 * HD]), sb("head_mask1", [P, H])
        with nc.sbuf_tensor("hT1", [P, NTOK], F32) as hT:
            k.hT = hT
            norm_phase(nc, k, "_n10", 1, 0)
            sparse_project_phase(nc, d, k, a)
        sparse_attention_phase(nc, k, a)


E, TOPK = 8, 2
FF = 4 * C
FK = FF // P
CAPACITY = int(1.25 * NTOK * TOPK / E)
XS = 2 * P
XTILES = 40
MAXT = NTOK // XS
SC = XTILES * XS // P
KT = TOPK * NT
assert NTOK * TOPK // XS + E - 1 <= XTILES and XTILES % 2 == 0


def route_phase(nc, d, k, r, name, gate_w, gate_b, capacity):
    with ExitStack() as ctx:
        def sb(n, s, dt=F32):
            return ctx.enter_context(nc.sbuf_tensor(n + name, s, dt))

        def sem(n):
            return phase_semaphore(nc, k, n + name)

        w = sb("gate_w", [P, E])
        bias = sb("gate_b", [P, E])
        rows = sb("h_rows", [P, NT, C])
        logit = sb("logit", [P, NT, E])
        hit = sb("hit", [P, TOPK, NT, E])
        eq = sb("eq", [P, NT, E])
        top = sb("top", [P, TOPK, NT])
        best = sb("best", [P, NT])
        prio = sb("prio", [P, E])
        earlier = sb("earlier", [P, P])
        gap = sb("gap", [P, NT])
        total = sb("total", [P, KT, E])
        upto = sb("upto", [P, KT, E])
        rank = sb("rank_e", [P, KT, E])
        ranked = sb("ranked_e", [P, KT, E])
        keep = sb("keep", [P, KT])
        steps = sb("steps", [P, E, MAXT])
        need = sb("need", [P, E])
        past = sb("past", [P, E])
        start = sb("start", [P, E])
        more = sb("more", [P, E, MAXT])
        slot = sb("slot_f", [P, KT])
        tile_no = sb("tile_no", [P, XTILES, E])
        tile_e = sb("tile_e", [P, XTILES])
        slot_i, part_i = sb("slot_i", [P, KT], I32), sb("part_i", [P, 2, KT], I32)
        part_f = sb("part_f", [P, 2, KT])
        lane = sb("lane", [P, P])
        column = sb("column", [P, SC])
        choice_id = sb("choice_id", [P, KT])
        slot_id = sb("slot_id", [P, SC])
        lane_hit = sb("lane_hit", [P, 4, P])
        column_hit = sb("column_hit", [P, 4, SC])
        owner = sb("owner", [P, SC])
        token_f, second, free = sb("token_f", [P, SC]), sb("second", [P, SC]), sb("free", [P, SC])
        ps = ctx.enter_context(nc.psum_tensor("ps_route" + name, [P, 8, CH], F32))
        w_in, const_ready, pool_step, dve_step = sem("w_in"), sem("const_ready"), sem("pool_step"), sem("dve_step")
        logit_ready, turned, copied = sem("logit_ready"), sem("turned"), sem("copied")
        gap_ready, exp_ready, hit_ready, prefix_ready = sem("gap_ready"), sem("exp_ready"), sem("hit_ready"), sem("prefix_ready")
        slot_ready, stored = sem("slot_ready"), sem("h_stored")
        lane_ready, column_ready, placed = sem("lane_ready"), sem("column_ready"), sem("placed")
        block = ctx.enter_context(nc.Block())

        @block.sync
        def _(sp):
            sp.dma_start(w[:, :], gate_w).then_inc(w_in, 16)
            if gate_b is not None:
                sp.dma_start(bias[:, :], bass.AP(gate_b.tensor, 0, [[0, P], [1, E]])).then_inc(w_in, 16)

            for n in range(NCH):
                sp.wait_ge(copied, n + 1)
                sp.dma_start(k.h_dram.rearrange("(n p) c -> p n c", p=P)[:, 4 * n:4 * n + 4, :],
                             rows[:, 4 * n:4 * n + 4, :]).then_inc(stored, 16)
            sp.wait_ge(stored, 16 * NCH)

        loads = 16 if gate_b is None else 32

        @block.gpsimd
        def _(pool):
            step = Chain(pool, pool_step)
            step(pool.memset(earlier[:, :], 1.0))
            step(pool.affine_select(out=earlier[:, :], in_=earlier[:, :], compare_op=ALU.is_gt, fill=0.0, base=0,
                                    pattern=[[1, P]], channel_multiplier=-1))
            step(pool.iota(prio[:, :], [[-1, E]], base=E, channel_multiplier=0, allow_small_or_imprecise_dtypes=True))
            step(pool.iota(steps[:, :, :], [[0, E], [XS, MAXT]], base=0, channel_multiplier=0,
                           allow_small_or_imprecise_dtypes=True))
            step(pool.iota(lane[:, :], [[1, P]], base=0, channel_multiplier=0, allow_small_or_imprecise_dtypes=True))
            step(pool.iota(column[:, :], [[1, SC]], base=0, channel_multiplier=0, allow_small_or_imprecise_dtypes=True))
            step(pool.iota(choice_id[:, :], [[P, KT]], base=1, channel_multiplier=1, allow_small_or_imprecise_dtypes=True))
            step(pool.iota(slot_id[:, :], [[P, SC]], base=TOPK * NTOK + 1, channel_multiplier=1,
                           allow_small_or_imprecise_dtypes=True))
            pool.iota(tile_no[:, :, :], [[1, XTILES], [0, E]], base=0, channel_multiplier=0,
                      allow_small_or_imprecise_dtypes=True).then_inc(const_ready, 1)
            pool.wait_ge(slot_ready, 1)
            for n in range(KT):
                wait(pool, placed, n - 3)
                pool.tensor_scalar(column_hit[:, n % 4, :], column[:, :], part_f[:, 0, n:n + 1], choice_id[:, n:n + 1],
                                   ALU.is_equal, ALU.mult).then_inc(column_ready, 1)

        @block.tensor
        def _(pe):
            pe.wait_ge(w_in, loads)
            for t in range(NT):
                m = pe.matmul(ps[:, 4, t * E:(t + 1) * E], k.hT[:, t * P:(t + 1) * P], w[:, :], start=True, stop=True)
            m.then_inc(logit_ready, 1)
            for n in range(NCH):
                wait(pe, copied, n - 3)
                for j in range(4):
                    t = 4 * n + j
                    m = pe.transpose(ps[:, n % 4, j * P:(j + 1) * P], k.hT[:, t * P:(t + 1) * P], k.ident[:, :])
                m.then_inc(turned, 1)
            pe.wait_ge(const_ready, 1)
            pe.wait_ge(hit_ready, 1)
            h = hit[:, :, :, :].rearrange("p c t e -> p (c t e)")
            pe.matmul(ps[:, 5, :], earlier[:, :], h, start=True, stop=True)
            pe.matmul(ps[:, 6, :], k.ones[:, :], h, start=True, stop=True).then_inc(prefix_ready, 1)
            for n in range(KT):
                pe.wait_ge(lane_ready, n + 1)
                pe.wait_ge(column_ready, n + 1)
                pe.matmul(ps[:, 7, 0:SC], lane_hit[:, n % 4, :], column_hit[:, n % 4, :], start=n == 0,
                          stop=n == KT - 1).then_inc(placed, 1)

        @block.scalar
        def _(act):
            for n in range(NCH):
                act.wait_ge(turned, n + 1)
                act.activation(rows[:, 4 * n:4 * n + 4, :], ps[:, n % 4, :].rearrange("p (j c) -> p j c", j=4),
                               ACT.Copy).then_inc(copied, 1)
            act.wait_ge(gap_ready, 1)
            act.activation(gap[:, :], gap[:, :], ACT.Exp).then_inc(exp_ready, 1)

        @block.vector
        def _(dve):
            step = Chain(dve, dve_step)

            def over_e(v, n=NT):
                return view(v, 0, [[1, n], [0, E]])

            def for_all(v, n=NT):
                return view(v, 0, [[0, n], [1, E]])

            dve.wait_ge(logit_ready, 1)
            dve.wait_ge(const_ready, 1)
            dve.wait_ge(w_in, loads)
            logits = ps[:, 4, 0:NT * E].rearrange("p (t e) -> p t e", e=E)
            if gate_b is None:
                step(dve.tensor_copy(logit[:, :, :], logits))
            else:
                step(dve.tensor_tensor(logit[:, :, :], logits, for_all(bias[:, :]), ALU.add))
            for c in range(TOPK):
                step(dve.tensor_reduce(top[:, c, :], logit[:, :, :], AX.X, ALU.max))
                step(dve.tensor_tensor(eq[:, :, :], logit[:, :, :], over_e(top[:, c, :]), ALU.is_equal))
                step(dve.tensor_tensor(eq[:, :, :], eq[:, :, :], for_all(prio[:, :]), ALU.mult))
                step(dve.tensor_reduce(best[:, :], eq[:, :, :], AX.X, ALU.max))
                step(dve.tensor_tensor(hit[:, c, :, :], eq[:, :, :], over_e(best[:, :]), ALU.is_equal))
                if c == 0:
                    step(dve.scalar_tensor_tensor(out=logit[:, :, :], in0=hit[:, 0, :, :], scalar=NEG, in1=logit[:, :, :],
                                                  op0=ALU.mult, op1=ALU.add))
            dve.tensor_tensor(gap[:, :], top[:, 1, :], top[:, 0, :], ALU.subtract).then_inc(gap_ready, 1)
            dve.sem_inc(hit_ready, 1)
            dve.wait_ge(exp_ready, 1)
            step(dve.tensor_scalar(best[:, :], gap[:, :], 1.0, None, ALU.add))
            step(dve.reciprocal(r.weight[:, 0:NT], best[:, :]))
            step(dve.tensor_tensor(r.weight[:, NT:KT], r.weight[:, 0:NT], gap[:, :], ALU.mult))
            dve.wait_ge(prefix_ready, 1)
            within = ps[:, 5, :].rearrange("p (n e) -> p n e", e=E)
            step(dve.tensor_copy(total[:, :, :], ps[:, 6, :].rearrange("p (n e) -> p n e", e=E)))
            for e in range(E):
                m = dve.tensor_tensor_scan(view(upto[:, :, :], e, [[E, KT]]), k.ones[:, 0:KT],
                                           view(total[:, :, :], e, [[E, KT]]), 0.0, ALU.mult, ALU.add)
                step(m)
            step(dve.tensor_tensor(rank[:, :, :], upto[:, :, :], total[:, :, :], ALU.subtract))
            step(dve.tensor_tensor(rank[:, :, :], rank[:, :, :], within, ALU.add))
            step(dve.tensor_tensor(more[:, :, :], view(upto[:, KT - 1, :], 0, [[1, E], [0, MAXT]]), steps[:, :, :], ALU.is_gt))
            step(dve.tensor_reduce(need[:, :], more[:, :, :], AX.X, ALU.add))
            step(dve.tensor_tensor_scan(past[:, :], k.ones[:, 0:E], need[:, :], 0.0, ALU.mult, ALU.add))
            step(dve.tensor_tensor(start[:, :], past[:, :], need[:, :], ALU.subtract))
            step(dve.tensor_scalar(start[:, :], start[:, :], float(XS), None, ALU.mult))
            hits = hit[:, :, :, :].rearrange("p c t e -> p (c t) e")
            if capacity is not None:
                step(dve.tensor_tensor(ranked[:, :, :], rank[:, :, :], hits, ALU.mult))
                step(dve.tensor_reduce(keep[:, :], ranked[:, :, :], AX.X, ALU.add))
                step(dve.scalar_tensor_tensor(out=r.weight[:, :], in0=keep[:, :], scalar=float(capacity), in1=r.weight[:, :],
                                              op0=ALU.is_lt, op1=ALU.mult))
            step(dve.tensor_tensor(rank[:, :, :], rank[:, :, :], for_all(start[:, :], KT), ALU.add))
            step(dve.tensor_tensor(ranked[:, :, :], rank[:, :, :], hits, ALU.mult))
            step(dve.tensor_reduce(slot[:, :], ranked[:, :, :], AX.X, ALU.add))
            step(dve.tensor_copy(slot_i[:, :], slot[:, :]))
            step(dve.tensor_scalar(part_i[:, 0, :], slot_i[:, :], P.bit_length() - 1, None, ALU.logical_shift_right))
            step(dve.tensor_scalar(part_i[:, 1, :], slot_i[:, :], P - 1, None, ALU.bitwise_and))
            step(dve.tensor_copy(part_f[:, :, :], part_i[:, :, :]))
            dve.sem_inc(slot_ready, 1)
            for n in range(KT):
                wait(dve, placed, n - 3)
                dve.tensor_scalar(lane_hit[:, n % 4, :], lane[:, :], part_f[:, 1, n:n + 1], None,
                                  ALU.is_equal).then_inc(lane_ready, 1)
            step(dve.tensor_tensor(tile_no[:, :, :], tile_no[:, :, :], for_all(past[:, :], XTILES), ALU.is_ge))
            step(dve.tensor_reduce(tile_e[:, :], tile_no[:, :, :], AX.X, ALU.add))
            step(dve.tensor_scalar(r.expert[:, :], tile_e[:, :], float(E - 1), None, ALU.min))
            dve.wait_ge(placed, KT)
            step(dve.tensor_copy(owner[:, :], ps[:, 7, 0:SC]))
            step(dve.tensor_scalar(second[:, :], owner[:, :], float(NTOK), float(-NTOK), ALU.is_gt, ALU.mult))
            step(dve.scalar_tensor_tensor(out=token_f[:, :], in0=owner[:, :], scalar=-1.0, in1=second[:, :],
                                          op0=ALU.add, op1=ALU.add))
            step(dve.tensor_scalar(r.token[:, :], token_f[:, :], 0.0, None, ALU.max))
            step(dve.scalar_tensor_tensor(out=free[:, :], in0=owner[:, :], scalar=0.0, in1=slot_id[:, :],
                                          op0=ALU.is_equal, op1=ALU.mult))
            step(dve.scalar_tensor_tensor(out=r.dest[:, :], in0=owner[:, :], scalar=-1.0, in1=free[:, :],
                                          op0=ALU.add, op1=ALU.add))


UNROLL = 4
assert XTILES % UNROLL == 0


def expert_phase(nc, k, r, name, weights, gated):
    nf = len(weights.fc)
    nr = len(weights.rows)
    nw = nf + 2
    with ExitStack() as ctx:
        def sb(n, s, dt=F32):
            return ctx.enter_context(nc.sbuf_tensor(n + name, s, dt))

        def sem(n):
            return phase_semaphore(nc, k, n + name)

        fc = sb("fc", [P, UNROLL, nf, FF])
        proj = sb("proj", [P, UNROLL, FK, C])
        fc_bias = sb("fc_bias", [P, UNROLL, nf * FK])
        fc_biases = sb("fc_biases", [P, E, nf, FK])
        out_rows = sb("out_rows", [P, nr, E, C])
        x_rows = sb("x_rows", [P, UNROLL, 2, C])
        x_T = sb("x_T", [P, 2, XS])
        act1 = sb("act1", [P, 2, FK, XS])
        act2 = sb("act2", [P, 2, FK, XS]) if gated else None
        y = sb("y", [P, 2, 2, C])
        token_now, dest_now = sb("token_now", [P, UNROLL, 2], I32), sb("dest_now", [P, 2, 2], I32)
        ps_x = ctx.enter_context(nc.psum_tensor("ps_x" + name, [P, CH], F32))
        ps_h = ctx.enter_context(nc.psum_tensor("ps_h" + name, [P, nf, 2, 2, XS], F32))
        ps_o = ctx.enter_context(nc.psum_tensor("ps_o" + name, [P, 2, CH], F32))
        if gated:
            cen = sb("cen", [P, 2, 2, C])
            stats = sb("stats", [P, 2, 6])
            moments = sb("moments", [P, 2, 2, 2])
            inv_std = sb("inv_std", [P, 2, 2])
            exponent = sb("exponent", [P, 2])
            exponent_ready, var_ready, inv_ready = sem("exponent_ready"), sem("var_ready"), sem("inv_ready")
            summed, biased, scaled = sem("summed"), sem("biased"), sem("scaled")
            stats_ready, normed = sem("stats_ready"), sem("normed")
        tables_in, halved = sem("tables_in"), sem("halved")
        w_in = [sem(f"w_in{i}_") for i in range(UNROLL)]
        x_in = [sem(f"x_in{i}_") for i in range(UNROLL)]
        x_turned, x_copied, fc_ready, act_ready = sem("x_turned"), sem("x_copied"), sem("fc_ready"), sem("act_ready")
        g_ready, out_ready, out_read, y_ready = sem("g_ready"), sem("out_ready"), sem("out_read"), sem("y_ready")
        token_ready, dest_ready = sem("token_ready"), sem("dest_ready")
        stored = [sem(f"stored{i}_") for i in range(2)]
        block = ctx.enter_context(nc.Block())

        def exists(j):
            return not isinstance(j, int) or 0 <= j < XTILES

        def tiles(eng, step, first=0, last=XTILES):
            for j in range(first, UNROLL):
                step(j // UNROLL, j % UNROLL)
            with eng.Fori(1, XTILES // UNROLL - 1) as i:
                for s in range(UNROLL):
                    step(i, s)
            for j in range(XTILES - UNROLL, last):
                step(j // UNROLL, j % UNROLL)

        def ring(i, s, n):
            return (s + n) % UNROLL, i + (s + n) // UNROLL + 1

        @block.sync
        def _(sp):
            for f, (_, b) in enumerate(weights.fc):
                sp.dma_start(fc_biases[:, :, f, :], b.rearrange("e (p f) -> p e f", p=P)).then_inc(tables_in, 16)
            for i, t in enumerate(weights.rows):
                sp.dma_start(out_rows[:, i, :, :], bass.AP(t.tensor, 0, [[0, P], [1, E * C]])).then_inc(tables_in, 16)
            if gated:
                sp.wait_ge(halved, 1)
            else:
                sp.wait_ge(tables_in, 16 * (nf + nr))

            def step(i, s):
                j = UNROLL * i + s
                wait(sp, out_ready, j - UNROLL + 1)
                e = sp.value_load(r.expert[0:1, bass.ds(j, 1)], min_val=0, max_val=E - 1)
                for f, (w, _) in enumerate(weights.fc):
                    sp.dma_start(fc[:, s, f, :], w[bass.ds(e, 1), :, :].rearrange("o p f -> (o p) f")).then_inc(w_in[s], 16)
                sp.dma_start(proj[:, s, :, :], weights.proj[bass.ds(e, 1), :, :].rearrange("o (p f) c -> (o p) f c", p=P)).then_inc(w_in[s], 16)
                sp.dma_start(fc_bias[:, s, :], fc_biases[:, bass.ds(e, 1), :, :]).then_inc(w_in[s], 16)

            tiles(sp, step)

        @block.tensor
        def _(pe):
            def first_layer(i, s):
                n = UNROLL * i + s + 1
                slot, count = ring(i, s, 1)
                pe.wait_ge(w_in[slot], 16 * nw * count)
                pe.wait_ge(x_copied, n + 1)
                for g in range(2):
                    for l in range(nf):
                        wait(pe, act_ready, 2 * nf * (n - 1) + g * nf + l + 1)
                        for f in (2 * g, 2 * g + 1):
                            m = pe.matmul(ps_h[:, l, g, f % 2, :], fc[:, slot, l, f:FF:FK], x_T[:, slot % 2, :],
                                          start=True, stop=True)
                        m.then_inc(fc_ready, 1)

            def turn(i, s):
                n = UNROLL * i + s + 2
                slot, count = ring(i, s, 2)
                pe.wait_ge(x_in[slot], 32 * count)
                wait(pe, x_copied, n)
                for h in range(2):
                    m = pe.transpose(ps_x[:, h * P:(h + 1) * P], x_rows[:, slot, h, :], k.ident[:, :])
                m.then_inc(x_turned, 1)

            def second_layer(j, s):
                pe.wait_ge(g_ready if gated else act_ready, j + 1 if gated else 2 * j + 2)
                wait(pe, out_read if gated else y_ready, j - 1)
                for h in range(2):
                    for f in range(FK):
                        m = pe.matmul(ps_o[:, s % 2, h * P:(h + 1) * P], act1[:, s % 2, f, h * P:(h + 1) * P],
                                      proj[:, s, f, :], start=f == 0, stop=f == FK - 1)
                m.then_inc(out_ready, 1)

            def step(i, s):
                j = UNROLL * i + s
                if exists(j + 1):
                    first_layer(i, s)
                if exists(j + 2):
                    turn(i, s)
                if exists(j):
                    second_layer(j, s)

            tiles(pe, step, first=-2)

        @block.scalar
        def _(act):
            def step(i, s):
                n = UNROLL * i + s + 1
                if exists(n):
                    slot, _ = ring(i, s, 1)
                    for g in range(2):
                        for l in range(nf):
                            act.wait_ge(fc_ready, 2 * nf * n + g * nf + l + 1)
                            wait(act, out_ready, n - 1)
                            out = (act1, act2)[l]
                            for f in (2 * g, 2 * g + 1):
                                m = act.activation(out[:, slot % 2, f, :], ps_h[:, l, g, f % 2, :],
                                                   ACT.Tanh if l else ACT.Gelu, scale=0.5 if l else 1.0,
                                                   bias=fc_bias[:, slot, l * FK + f:l * FK + f + 1])
                            m.then_inc(act_ready, 1)
                n = n + 1
                if exists(n):
                    act.wait_ge(x_turned, n + 1)
                    wait(act, fc_ready, 2 * nf * (n - 1))
                    act.activation(x_T[:, s % 2, :], ps_x[:, 0:XS], ACT.Copy).then_inc(x_copied, 1)

            tiles(act, step, first=-2)

        @block.vector
        def _(dve):
            dve.wait_ge(tables_in, 16 * (nf + nr))
            if gated:
                dve.tensor_scalar(fc_biases[:, :, 1, :], fc_biases[:, :, 1, :], 0.5, None, ALU.mult).then_inc(halved, 1)

            def gate(n, slot):
                for g in range(2):
                    dve.wait_ge(act_ready, 4 * n + 2 * g + 2)
                    a1 = act1[:, slot, 2 * g:2 * g + 2, :]
                    m = dve.scalar_tensor_tensor(out=a1, in0=act2[:, slot, 2 * g:2 * g + 2, :], scalar=1.0, in1=a1,
                                                 op0=ALU.add, op1=ALU.mult)
                m.then_inc(g_ready, 1)

            def rows(j):
                e = dve.value_load(r.expert[0:1, bass.ds(j, 1)], min_val=0, max_val=E - 1)
                return [view(out_rows[:, i, bass.ds(e, 1), :], 0, [[0, 2], [1, C]]) for i in range(nr)]

            def y_free(i, s):
                if isinstance(i, int):
                    wait(dve, stored[s % 2], 32 * ((UNROLL * i + s) // 2))
                else:
                    dve.wait_ge(stored[s % 2], 32 * (2 * i + s // 2))

            def finish(i, s):
                j = UNROLL * i + s
                out_b, = rows(j)
                dve.wait_ge(out_ready, j + 1)
                y_free(i, s)
                dve.nop(nofuse=True)
                dve.tensor_tensor(y[:, s % 2, :, :], ps_o[:, s % 2, 0:XS].rearrange("p (h c) -> p h c", h=2), out_b,
                                  ALU.add).then_inc(y_ready, 1)

            def residual(j, s, out_b):
                c = cen[:, s % 2, :, :]
                dve.wait_ge(out_ready, j + 1)
                dve.scalar_tensor_tensor(out=c, in0=ps_o[:, s % 2, 0:XS].rearrange("p (h c) -> p h c", h=2), scalar=0.5,
                                         in1=x_rows[:, s, :, :], op0=ALU.mult, op1=ALU.add).then_inc(out_read, 1)
                dve.wait_ge(out_read, j + 1)
                dve.nop(nofuse=True)
                dve.tensor_tensor(c, c, out_b, ALU.add).then_inc(biased, 1)
                dve.wait_ge(biased, j + 1)
                for h in range(2):
                    m = dve.bn_stats(stats[:, h, :], cen[:, s % 2, h, :])
                m.then_inc(stats_ready, 1)
                dve.wait_ge(stats_ready, j + 1)
                dve.nop(nofuse=True)
                for h in range(2):
                    m = dve.bn_aggr(moments[:, s % 2, h, :], stats[:, h, :])
                m.then_inc(var_ready, 1)

            def normalize(i, s, gamma, beta):
                j = UNROLL * i + s
                dve.wait_ge(inv_ready, j + 1)
                y_free(i, s)
                for h in range(2):
                    m = dve.tensor_scalar(y[:, s % 2, h, :], cen[:, s % 2, h, :], moments[:, s % 2, h, 0:1],
                                          inv_std[:, s % 2, h:h + 1], ALU.subtract, ALU.mult)
                m.then_inc(normed, 1)
                dve.wait_ge(normed, j + 1)
                dve.nop(nofuse=True)
                dve.tensor_tensor(y[:, s % 2, :, :], y[:, s % 2, :, :], gamma, ALU.mult).then_inc(scaled, 1)
                dve.wait_ge(scaled, j + 1)
                dve.nop(nofuse=True)
                dve.tensor_tensor(y[:, s % 2, :, :], y[:, s % 2, :, :], beta, ALU.add).then_inc(y_ready, 1)

            def step(i, s):
                j = UNROLL * i + s
                if gated:
                    if exists(j + 1):
                        gate(j + 1, (s + 1) % 2)
                    if exists(j):
                        residual(j, s, rows(j)[0])
                    if exists(j - 1):
                        pi, ps_ = i + (s - 1) // UNROLL, (s - 1) % UNROLL
                        normalize(pi, ps_, *rows(j - 1)[1:])
                elif exists(j):
                    finish(i, s)

            tiles(dve, step, first=-1, last=XTILES + 1)

        @block.gpsimd
        def _(pool):
            if gated:
                pool.memset(exponent[:, :], -0.5).then_inc(exponent_ready, 1)
                pool.wait_ge(exponent_ready, 1)

            def gather(j, slot):
                pool.tensor_copy(token_now[:, slot, :], r.token[:, bass.ds(2 * j, 2)]).then_inc(token_ready, 1)
                pool.wait_ge(token_ready, j + 1)
                pool.nop(nofuse=True)
                for h in range(2):
                    pool.indirect_dma_start(out=x_rows[:, slot, h, :], out_offset=None, in_=k.h_dram,
                                            in_offset=bass.IndirectOffsetOnAxis(ap=token_now[:, slot, h:h + 1], axis=0)).then_inc(x_in[slot], 16)

            def scatter(j, slot):
                pool.wait_ge(y_ready, j + 1)
                pool.nop(nofuse=True)
                pool.tensor_copy(dest_now[:, slot, :], r.dest[:, bass.ds(2 * j, 2)]).then_inc(dest_ready, 1)
                pool.wait_ge(dest_ready, j + 1)
                pool.nop(nofuse=True)
                for h in range(2):
                    pool.indirect_dma_start(out=k.y_dram, out_offset=bass.IndirectOffsetOnAxis(ap=dest_now[:, slot, h:h + 1], axis=0),
                                            in_=y[:, slot, h, :], in_offset=None).then_inc(stored[slot], 16)

            for j in range(UNROLL):
                gather(j, j)

            def step(i, s):
                j = UNROLL * i + s
                if gated and exists(j):
                    pool.wait_ge(var_ready, j + 1)
                    pool.tensor_tensor(inv_std[:, s % 2, :], moments[:, s % 2, :, 1], exponent[:, :], ALU.pow).then_inc(inv_ready, 1)
                if exists(j + UNROLL) and exists(j):
                    pool.wait_ge(x_turned, j + 1)
                    if gated:
                        pool.wait_ge(out_read, j + 1)
                    pool.nop(nofuse=True)
                    gather(j + UNROLL, s)
                if exists(j - 1):
                    scatter(j - 1, (s - 1) % 2)

            tiles(pool, step, last=XTILES + 1)
            for s in range(2):
                pool.wait_ge(stored[s], 16 * XTILES)


def combine_phase(nc, k, r, name, layer):
    with ExitStack() as ctx:
        def sb(n, s, dt=F32):
            return ctx.enter_context(nc.sbuf_tensor(n + name, s, dt))

        def sem(n):
            return phase_semaphore(nc, k, n + name)

        got = sb("got", [P, TOPK, NT, C])
        part = sb("part", [P, 2, 4, C])
        both = sb("both", [P, 2, 4, C])
        ps = ctx.enter_context(nc.psum_tensor("ps_comb" + name, [P, 2, CH], F32))
        rows_in = [sem(f"rows_in{n}_") for n in range(NCH)]
        part_ready, both_ready, turned, added = sem("part_ready"), sem("both_ready"), sem("turned"), sem("added")
        block = ctx.enter_context(nc.Block())

        @block.sync
        def _(sp):
            src = k.y_dram.rearrange("(n p) c -> p n c", p=P)
            for n in range(NCH):
                for c in range(TOPK):
                    sp.dma_start(got[:, c, 4 * n:4 * n + 4, :], src[:, c * NT + 4 * n:c * NT + 4 * n + 4, :]).then_inc(rows_in[n], 16)

        @block.tensor
        def _(pe):
            for n in range(NCH):
                pe.wait_ge(both_ready, 4 * (n + 1))
                wait(pe, added, 2 * (n - 1))
                for j in range(4):
                    m = pe.transpose(ps[:, n % 2, j * P:(j + 1) * P], both[:, n % 2, j, :], k.ident[:, :])
                m.then_inc(turned, 1)

        @block.scalar
        def _(act):
            for n in range(NCH):
                act.wait_ge(rows_in[n], 16 * TOPK)
                wait(act, both_ready, 4 * (n - 1))
                for j in range(4):
                    t = 4 * n + j
                    act.activation(part[:, n % 2, j, :], got[:, 0, t, :], ACT.Copy, scale=r.weight[:, t:t + 1]).then_inc(part_ready, 1)

        @block.vector
        def _(dve):
            for n in range(NCH + 1):
                if n < NCH:
                    wait(dve, turned, n - 1)
                    for j in range(4):
                        t = 4 * n + j
                        dve.wait_ge(part_ready, t + 1)
                        dve.scalar_tensor_tensor(out=both[:, n % 2, j, :], in0=got[:, 1, t, :], scalar=r.weight[:, NT + t:NT + t + 1],
                                                 in1=part[:, n % 2, j, :], op0=ALU.mult, op1=ALU.add).then_inc(both_ready, 1)
                if n >= 1:
                    m = n - 1
                    dve.wait_ge(turned, m + 1)
                    for s in range(2):
                        b = 2 * m + s
                        xs = k.xT[:, b * T:(b + 1) * T]
                        dve.scalar_tensor_tensor(out=xs, in0=ps[:, m % 2, s * T:(s + 1) * T], scalar=k.mod[:, layer, 5, b:b + 1],
                                                 in1=xs, op0=ALU.mult, op1=ALU.add).then_inc(added, 1)


def experts(nc, d, k, name, layer, gate_w, gate_b, capacity, weights, gated):
    with ExitStack() as ctx:
        def sb(n, s, dt=F32):
            return ctx.enter_context(nc.sbuf_tensor(n + name, s, dt))

        r = Place()
        r.weight, r.expert = sb("weight", [P, KT]), sb("expert", [P, XTILES], I32)
        r.token, r.dest = sb("token", [P, SC], I32), sb("dest", [P, SC], I32)
        with nc.sbuf_tensor("hT" + name, [P, NTOK], F32) as hT:
            k.hT = hT
            norm_phase(nc, k, "_n" + name, layer, 1)
            route_phase(nc, d, k, r, name, gate_w, gate_b, capacity)
        expert_phase(nc, k, r, "_x" + name, weights, gated)
        combine_phase(nc, k, r, "_c" + name, layer)


def layer0_experts(nc, d, k):
    w = Place()
    w.fc = [(d["L0_ffn_c_fc"], d["L0_ffn_fc_bias"].rearrange("e o f -> (e o) f"))]
    w.proj = d["L0_ffn_c_proj"]
    w.rows = [d["L0_ffn_proj_bias"]]
    experts(nc, d, k, "_m0", 0, d["L0_ffn_gate_w"], None, CAPACITY, w, False)


def layer1_experts(nc, d, k):
    w = Place()
    w.fc = [(d["L1_ffn_Wi"], d["L1_ffn_bi"]), (d["L1_ffn_Wg"], d["L1_ffn_bg"])]
    w.proj = d["L1_ffn_Wo"]
    w.rows = [d["L1_ffn_bo"], d["L1_ffn_gamma"], d["L1_ffn_beta"]]
    experts(nc, d, k, "_m1", 1, d["L1_ffn_Wr"], d["L1_ffn_br"], None, w, True)


class Place:
    pass


def output_phase(nc, d, k):
    with ExitStack() as ctx:
        rows = ctx.enter_context(nc.sbuf_tensor("out_rows", [P, 3, CH], F32))
        ps = ctx.enter_context(nc.psum_tensor("ps_out", [P, 4, CH], F32))
        turned, copied, stored = (phase_semaphore(nc, k, n) for n in ("out_turned", "out_copied", "out_stored"))
        block = ctx.enter_context(nc.Block())

        @block.tensor
        def _(pe):
            for n in range(NCH):
                wait(pe, copied, n - 3)
                for j in range(4):
                    m = pe.transpose(ps[:, n % 4, j * P:(j + 1) * P], k.xT[:, (4 * n + j) * P:(4 * n + j + 1) * P], k.ident[:, :])
                m.then_inc(turned, 1)

        @block.vector
        def _(dve):
            for n in range(NCH):
                dve.wait_ge(turned, n + 1)
                wait(dve, stored, 16 * (n - 2))
                dve.tensor_copy(rows[:, n % 3, :], ps[:, n % 4, :]).then_inc(copied, 1)

        @block.sync
        def _(sp):
            out = d["out"].rearrange("(n p) c -> p n c", p=P)
            for n in range(NCH):
                sp.wait_ge(copied, n + 1)
                sp.dma_start(out[:, 4 * n:4 * n + 4, :], rows[:, n % 3, :].rearrange("p (j c) -> p j c", j=4)).then_inc(stored, 16)
                sp.wait_ge(stored, 16 * (n + 1))


def build(nc, d):
    with ExitStack() as ctx:
        def sb(n, s, dt=F32):
            return ctx.enter_context(nc.sbuf_tensor(n, s, dt))

        k = Place()
        k.semaphores = []
        k.ident, k.ones, k.eps = sb("ident", [P, P]), sb("ones", [P, P]), sb("eps", [P, 1])
        k.mod = sb("mod", [P, 2, 6, B])
        k.xT = sb("xT", [P, NTOK])
        k.h_dram = nc.dram_tensor("h_dram", (NTOK, C), F32, kind="Internal").ap()
        k.y_dram = nc.dram_tensor("y_dram", (TOPK * NTOK + XTILES * XS, C), F32, kind="Internal").ap()
        setup_phase(nc, d, k)
        layer0_attention(nc, d, k)
        layer0_experts(nc, d, k)
        clear_semaphores(nc, k)
        layer1_attention(nc, d, k)
        layer1_experts(nc, d, k)
        output_phase(nc, d, k)


def layer0_attention(nc, d, k):
    with ExitStack() as ctx:
        def sb(n, s, dt=F32):
            return ctx.enter_context(nc.sbuf_tensor(n, s, dt))

        a = Place()
        a.ek_line = nc.dram_tensor("ek_line", (REL_W, HD), F32, kind="Internal").ap()
        a.ev_line = nc.dram_tensor("ev_line", (REL_W, HD), F32, kind="Internal").ap()
        a.ek_skew = nc.dram_tensor("ek_skew", (P, SKEW_W + HD), F32, kind="Internal").ap()
        a.ev_skew = nc.dram_tensor("ev_skew", (P, SKEW_W + HD), F32, kind="Internal").ap()
        a.qT, a.kT, a.v = sb("qT0", [P, NTOK]), sb("kT0", [P, NTOK]), sb("v0", [P, NT * C])
        a.ve = sb("ve", [P, VE_BLOCKS * VE_W])
        a.e_rel = sb("e_rel", [P, 3 * P])
        a.wproj, a.wproj_rel = sb("wproj0", [P, C]), sb("wproj_rel", [P, 8, C])
        a.bproj, a.gate_bias = sb("bproj0", [P, 1]), sb("gate_bias0", [P, B])
        a.head_mask, a.y_mask, a.t_mask = sb("head_mask", [P, H]), sb("y_mask", [P, 2, 64]), sb("t_mask", [P, TB])
        a.spread = sb("spread", [P, H * TB * HD])
        a.q_rel = sb("q_rel", [P, 2, HALF_TILES * P])
        with nc.sbuf_tensor("hT0", [P, NTOK], F32) as hT:
            k.hT = hT
            norm_phase(nc, k, "_n00", 0, 0)
            rel_tables_phase(nc, d, k, a)
        a.q_diag = sb("q_diag", [P, 2, HALF_TILES * P])
        rel_attention_phase(nc, k, a)


INPUTS = [
    "L0_attn_x", "L0_attn_Wattn", "L0_attn_battn", "L0_attn_Wproj", "L0_attn_bproj", "L0_attn_embk", "L0_attn_embv",
    "L0_ffn_gate_w", "L0_ffn_c_fc", "L0_ffn_fc_bias", "L0_ffn_c_proj", "L0_ffn_proj_bias", "L0_c", "L0_wmod",
    "L1_attn_wq", "L1_attn_bq", "L1_attn_wk", "L1_attn_bk", "L1_attn_wv", "L1_attn_bv", "L1_attn_wo", "L1_attn_bo",
    "L1_attn_wi1", "L1_attn_bi1", "L1_attn_wi2", "L1_attn_bi2", "L1_ffn_Wr", "L1_ffn_br", "L1_ffn_Wi", "L1_ffn_bi",
    "L1_ffn_Wg", "L1_ffn_bg", "L1_ffn_Wo", "L1_ffn_bo", "L1_ffn_gamma", "L1_ffn_beta", "L1_c", "L1_wmod",
]


def kernel(**inputs):
    import numpy as np
    import concourse.bacc as bacc
    from concourse.bass_utils import run_bass_kernel_spmd

    nc = bacc.Bacc("TRN2", target_bir_lowering=False, num_devices=1)
    arrays, d = {}, {}
    for name in INPUTS:
        arrays[name] = np.ascontiguousarray(inputs[name])
        d[name] = nc.dram_tensor(name, arrays[name].shape, F32, kind="ExternalInput").ap()
    d["x"] = d["L0_attn_x"].rearrange("b t c -> (b t) c")
    out = nc.dram_tensor("out", (B, T, C), F32, kind="ExternalOutput").ap()
    d["out"] = out.rearrange("b t c -> (b t) c")
    build(nc, d)
    return run_bass_kernel_spmd(nc, [arrays], core_ids=[0]).results[0]["out"]
```

```python
from contextlib import ExitStack

import concourse.bass as bass
from concourse import mybir

ALU = mybir.AluOpType
ACT = mybir.ActivationFunctionType
AX = mybir.AxisListType
F32 = mybir.dt.float32
I32 = mybir.dt.int32
U32 = mybir.dt.uint32

P = 128
B, T, C, H = 16, 256, 128, 16
HD = C // H
NTOK = B * T
NT = NTOK // P
CH = 512
NCH = NTOK // CH
NREL = 128
LN_EPS = 1e-5
NEG = -1e30
QK_SCALE = HD ** -0.5
GATE_FLOOR = 0.25

TB = 8
TILES = T // TB
QUAD = 4
NQ = TILES // QUAD
HALF_TILES = P // TB
NG = H // 4
HALVES = 2 * B
E = 8


def view(ap, offset, dims):
    return bass.AP(ap.tensor, ap.offset + offset, [list(ap.ap[0])] + dims)


def wait(eng, sem, value):
    if isinstance(value, int) and value <= 0:
        return
    eng.wait_ge(sem, value)


def phase_semaphore(nc, k, name):
    sem = nc.alloc_semaphore(name)
    k.semaphores.append(sem)
    return sem


def clear_semaphores(nc, k):
    nc.all_engine_barrier()
    nc.clear_and_free_semaphores(k.semaphores)
    nc.all_engine_barrier()
    k.semaphores = []


class Chain:

    def __init__(self, eng, sem):
        self.eng, self.sem, self.n = eng, sem, 0

    def __call__(self, ins):
        self.n += 1
        ins.then_inc(self.sem, 1)
        self.eng.wait_ge(self.sem, self.n)


def setup_phase(nc, d, k):
    with ExitStack() as ctx:
        def sb(n, s, dt=F32):
            return ctx.enter_context(nc.sbuf_tensor(n, s, dt))

        def sem(n):
            return phase_semaphore(nc, k, n)

        x_rows = sb("x_rows", [P, NT, C])
        cond = sb("cond", [B, 2, C])
        cond_exp = sb("cond_exp", [B, 2, C])
        cond_T = sb("cond_T", [P, 2, B])
        wmod = sb("wmod", [P, 2, 6 * C])
        gate_abs = sb("gate_abs", [P, 2, 2, B])
        gate_sign = sb("gate_sign", [P, 2, 2, B])
        ps = ctx.enter_context(nc.psum_tensor("ps_setup", [P, 8, CH], F32))
        x_in = [sem(f"x_in{i}") for i in range(4)]
        cond_in, wmod_in = sem("cond_in"), sem("wmod_in")
        ident_ready = sem("ident_ready")
        pool_step, dve_step = sem("pool_step0"), sem("dve_step0")
        x_turned, x_copied = sem("x_turned"), sem("x_copied")
        exp_ready, silu_ready, cond_turned, cond_copied = sem("exp_ready"), sem("silu_ready"), sem("cond_turned"), sem("cond_copied")
        mod_ready = sem("mod_ready")
        block = ctx.enter_context(nc.Block())

        @block.sync
        def _(sp):
            for l in range(2):
                sp.dma_start(cond[:, l, :], d[f"L{l}_c"]).then_inc(cond_in, 16)
            for i in range(4):
                r = slice(i * NT // 4, (i + 1) * NT // 4)
                sp.dma_start(x_rows[:, r, :], d["x"].rearrange("(n p) c -> p n c", p=P)[:, r, :]).then_inc(x_in[i], 16)
            for l in range(2):
                sp.dma_start(wmod[:, l, :], d[f"L{l}_wmod"]).then_inc(wmod_in, 16)

        @block.gpsimd
        def _(pool):
            step = Chain(pool, pool_step)
            step(pool.memset(k.ident[:, :], 0.0))
            pool.affine_select(out=k.ident[:, :], in_=k.ident[:, :], compare_op=ALU.not_equal, fill=1.0, base=0,
                               pattern=[[-1, P]], channel_multiplier=1).then_inc(ident_ready, 1)
            pool.memset(k.ones[:, :], 1.0)
            pool.memset(k.eps[:, :], LN_EPS)

        @block.tensor
        def _(pe):
            pe.wait_ge(ident_ready, 1)
            pe.wait_ge(silu_ready, 1)
            for l in range(2):
                m = pe.transpose(ps[:, 6, l * B:(l + 1) * B], cond[:, l, :], k.ident[0:B, 0:B])
            m.then_inc(cond_turned, 1)
            for n in range(NCH):
                pe.wait_ge(x_in[n // 2], 16)
                wait(pe, x_copied, n - 3)
                for j in range(4):
                    m = pe.transpose(ps[:, n % 4, j * P:(j + 1) * P], x_rows[:, 4 * n + j, :], k.ident[:, :])
                m.then_inc(x_turned, 1)
            pe.wait_ge(cond_copied, 1)
            pe.wait_ge(wmod_in, 32)
            for l in range(2):
                for j in range(6):
                    m = pe.matmul(ps[:, 7, (6 * l + j) * B:(6 * l + j + 1) * B], wmod[:, l, j * C:(j + 1) * C],
                                  cond_T[:, l, :], start=True, stop=True)
            m.then_inc(mod_ready, 1)

        @block.scalar
        def _(act):
            act.wait_ge(cond_in, 32)
            act.activation(cond_exp[:, :, :], cond[:, :, :], ACT.Exp, scale=-1.0).then_inc(exp_ready, 1)

        @block.vector
        def _(dve):
            step = Chain(dve, dve_step)
            dve.wait_ge(exp_ready, 1)
            step(dve.tensor_scalar(cond_exp[:, :, :], cond_exp[:, :, :], 1.0, None, ALU.add))
            step(dve.reciprocal(cond_exp[:, :, :], cond_exp[:, :, :]))
            dve.tensor_tensor(cond[:, :, :], cond[:, :, :], cond_exp[:, :, :], ALU.mult).then_inc(silu_ready, 1)
            dve.wait_ge(cond_turned, 1)
            dve.tensor_copy(cond_T[:, :, :], ps[:, 6, 0:2 * B]).then_inc(cond_copied, 1)
            for n in range(NCH):
                dve.wait_ge(x_turned, n + 1)
                dve.tensor_copy(k.xT[:, n * CH:(n + 1) * CH], ps[:, n % 4, :]).then_inc(x_copied, 1)
            dve.wait_ge(mod_ready, 1)
            step(dve.tensor_copy(k.mod[:, :, :, :], ps[:, 7, 0:12 * B]))
            scales = k.mod[:, :, 1::3, :]
            gates = k.mod[:, :, 2::3, :]
            for l in range(2):
                sc, ga, ab, sg = scales[:, l], gates[:, l], gate_abs[:, l], gate_sign[:, l]
                step(dve.tensor_scalar(sc, sc, 1.0, None, ALU.add))
                step(dve.tensor_scalar(ab, ga, -1.0, None, ALU.mult))
                step(dve.tensor_tensor(ab, ab, ga, ALU.max))
                step(dve.tensor_scalar(ab, ab, GATE_FLOOR, None, ALU.max))
                step(dve.tensor_scalar(sg, ga, 0.0, 2.0, ALU.is_ge, ALU.mult))
                step(dve.scalar_tensor_tensor(out=ga, in0=sg, scalar=-1.0, in1=ab, op0=ALU.add, op1=ALU.mult))


def norm_phase(nc, k, name, layer, which, beside, r=None):
    shift_i, scale_i = 3 * which, 3 * which + 1
    with ExitStack() as ctx:
        def sb(n, s, dt=F32):
            return ctx.enter_context(nc.sbuf_tensor(n + name, s, dt))

        def sem(n):
            return phase_semaphore(nc, k, n + name)

        stats = sb("stats", [P, NT, 6])
        moments = sb("moments", [P, NT, 2])
        std, rstd, shift = sb("std", [P, NT]), sb("rstd", [P, NT]), sb("shift", [P, NT])
        normed = sb("normed", [P, 3, CH])
        ps_in = ctx.enter_context(nc.psum_tensor("ps_in" + name, [P, 3, CH], F32))
        ps_out = ctx.enter_context(nc.psum_tensor("ps_out" + name, [P, 2, CH], F32))
        if r:
            ps_rows = ctx.enter_context(nc.psum_tensor("ps_rows" + name, [P, 2, CH], F32))
            ps_logit = ctx.enter_context(nc.psum_tensor("ps_logit" + name, [P, CH], F32))
            rows_turned, logit_ready = sem("rows_turned"), sem("logit_ready")
        turned, stats_ready, var_ready, std_ready = sem("turned"), sem("stats_ready"), sem("var_ready"), sem("std_ready")
        rstd_ready, shift_ready, norm_dve, norm_act = sem("rstd_ready"), sem("shift_ready"), sem("norm_dve"), sem("norm_act")
        back, h_ready = sem("back"), sem("h_ready")
        block = ctx.enter_context(nc.Block())
        beside(block)

        def wait_normed(eng, c):
            if c >= 0:
                eng.wait_ge(norm_act if c % 2 else norm_dve, c // 2 + 1)

        @block.tensor
        def _(pe):
            for n in range(NCH + (3 if r else 2)):
                if n < NCH:
                    wait_normed(pe, n - 3)
                    for j in range(4):
                        t = 4 * n + j
                        m = pe.transpose(ps_in[:, n % 3, j * P:(j + 1) * P], k.xT[:, t * P:(t + 1) * P], k.ident[:, :])
                    m.then_inc(turned, 1)
                if 2 <= n < NCH + 2:
                    c = n - 2
                    wait_normed(pe, c)
                    wait(pe, h_ready, c - 1)
                    for j in range(4):
                        m = pe.transpose(ps_out[:, c % 2, j * P:(j + 1) * P], normed[:, c % 3, j * P:(j + 1) * P], k.ident[:, :])
                    m.then_inc(back, 1)
                if r and n >= 3:
                    c = n - 3
                    pe.wait_ge(h_ready, c + 1)
                    wait(pe, r.rows_copied, c - 1)
                    for j in range(4):
                        t = 4 * c + j
                        m = pe.transpose(ps_rows[:, c % 2, j * P:(j + 1) * P], k.hT[:, t * P:(t + 1) * P], k.ident[:, :])
                    m.then_inc(rows_turned, 1)
                    if c == 0:
                        pe.wait_ge(r.w_in, r.loads)
                    for j in range(4):
                        t = 4 * c + j
                        m = pe.matmul(ps_logit[:, t * E:(t + 1) * E], k.hT[:, t * P:(t + 1) * P], r.w[:, :], start=True, stop=True)
                    m.then_inc(logit_ready, 1)

        @block.vector
        def _(dve):
            for n in range(NCH + 1):
                if n < NCH:
                    dve.wait_ge(turned, n + 1)
                    for j in range(4):
                        m = dve.bn_stats(stats[:, 4 * n + j, :], ps_in[:, n % 3, j * P:(j + 1) * P])
                    m.then_inc(stats_ready, 1)
                    dve.wait_ge(stats_ready, n + 1)
                    dve.nop(nofuse=True)
                    for j in range(4):
                        m = dve.bn_aggr(moments[:, 4 * n + j, :], stats[:, 4 * n + j, :])
                    m.then_inc(var_ready, 1)
                if n >= 1:
                    c = n - 1
                    dve.wait_ge(std_ready, c + 1)
                    dve.reciprocal(rstd[:, 4 * c:4 * c + 4], std[:, 4 * c:4 * c + 4]).then_inc(rstd_ready, 1)
                    dve.wait_ge(rstd_ready, c + 1)
                    if c % 2:
                        dve.scalar_tensor_tensor(out=shift[:, 4 * c:4 * c + 4], in0=moments[:, 4 * c:4 * c + 4, 0], scalar=-1.0,
                                                 in1=rstd[:, 4 * c:4 * c + 4], op0=ALU.mult, op1=ALU.mult).then_inc(shift_ready, 1)
                        continue
                    wait(dve, back, c - 2)
                    for j in range(4):
                        t = 4 * c + j
                        m = dve.tensor_scalar(normed[:, c % 3, j * P:(j + 1) * P], ps_in[:, c % 3, j * P:(j + 1) * P],
                                              moments[:, t, 0:1], rstd[:, t:t + 1], ALU.subtract, ALU.mult)
                    m.then_inc(norm_dve, 1)

        @block.scalar
        def _(act):
            for n in range(NCH + (3 if r else 2)):
                if n < NCH:
                    act.wait_ge(var_ready, n + 1)
                    act.activation(std[:, 4 * n:4 * n + 4], moments[:, 4 * n:4 * n + 4, 1], ACT.Sqrt,
                                   bias=k.eps[:, 0:1]).then_inc(std_ready, 1)
                if 1 <= n <= NCH and n % 2 == 0:
                    c = n - 1
                    act.wait_ge(shift_ready, c // 2 + 1)
                    wait(act, back, c - 2)
                    for j in range(4):
                        t = 4 * c + j
                        m = act.activation(normed[:, c % 3, j * P:(j + 1) * P], ps_in[:, c % 3, j * P:(j + 1) * P], ACT.Identity,
                                           scale=rstd[:, t:t + 1], bias=shift[:, t:t + 1])
                    m.then_inc(norm_act, 1)
                if 2 <= n < NCH + 2:
                    c = n - 2
                    act.wait_ge(back, c + 1)
                    for s in range(CH // T):
                        b = c * (CH // T) + s
                        m = act.activation(k.hT[:, b * T:(b + 1) * T], ps_out[:, c % 2, s * T:(s + 1) * T], ACT.Identity,
                                           scale=k.mod[:, layer, scale_i, b:b + 1], bias=k.mod[:, layer, shift_i, b:b + 1])
                    m.then_inc(h_ready, 1)
                if r and n >= 3:
                    c = n - 3
                    act.wait_ge(rows_turned, c + 1)
                    act.activation(r.rows[:, 4 * c:4 * c + 4, :], ps_rows[:, c % 2, :].rearrange("p (j c) -> p j c", j=4),
                                   ACT.Copy).then_inc(r.rows_copied, 1)
            if r:
                act.wait_ge(logit_ready, NCH)
                act.activation(r.logits[:, :, :], ps_logit[:, 0:NT * E].rearrange("p (t e) -> p t e", e=E),
                               ACT.Copy).then_inc(r.logits_ready, 1)


REL_W = NREL + T + TB
VE_W = P
VE_BLOCKS = TILES + TILES // 2
TABLES = 3 + 2 + 2 * TB

SKEW_W = REL_W * HD


def ve_block(i, ch):
    return i if ch == 0 else TILES + i - TILES // 2


def rel_tables(nc, d, k, a):
    a.w_in, a.line_out, a.skew_out, a.table_in = (phase_semaphore(nc, k, n) for n in ("w_in0", "line_out", "skew_out", "table_in"))
    pool_step = phase_semaphore(nc, k, "pool_step1")
    wqkv, bqk, bv, ek_wide = a.wqkv, a.bqk, a.bv, a.ek_wide
    w_in, line_out, skew_out, table_in = a.w_in, a.line_out, a.skew_out, a.table_in

    def beside(block):
        @block.sync
        def _(sp):
            sp.dma_start(wqkv[:, :], d["L0_attn_Wattn"]).then_inc(w_in, 16)
            sp.dma_start(bqk[:, :], d["L0_attn_battn"][0:2 * C].rearrange("(j p) -> p j", p=P),
                         allow_slow_non_contiguous=True).then_inc(w_in, 16)
            sp.dma_start(bv[:, :], bass.AP(d["L0_attn_battn"].tensor, 2 * C, [[0, P], [1, C]])).then_inc(w_in, 16)
            for line, emb in ((a.ek_line, d["L0_attn_embk"]), (a.ev_line, d["L0_attn_embv"])):
                sp.dma_start(line[0:NREL, :], bass.AP(emb.tensor, 0, [[0, NREL], [1, HD]])).then_inc(line_out, 16)
                sp.dma_start(line[NREL:2 * NREL, :], emb[:, :]).then_inc(line_out, 16)
                sp.dma_start(line[2 * NREL:REL_W, :],
                             bass.AP(emb.tensor, (NREL - 1) * HD, [[0, REL_W - 2 * NREL], [1, HD]])).then_inc(line_out, 16)
            sp.wait_ge(line_out, 16 * 6)
            for line, skew in ((a.ek_line, a.ek_skew), (a.ev_line, a.ev_skew)):
                sp.dma_start(bass.AP(skew.tensor, 0, [[SKEW_W + HD, P], [1, SKEW_W]]),
                             bass.AP(line.tensor, 0, [[0, P], [1, SKEW_W]])).then_inc(skew_out, 16)
            sp.wait_ge(skew_out, 32)
            sp.dma_start(ek_wide[:, :], bass.AP(a.ek_skew.tensor, NREL * HD, [[SKEW_W, P], [1, (T + TB) * HD]])).then_inc(table_in, 16)
            for ch in range(2):
                first, count = ve_block(ch * TILES // 2, ch), TILES // (1 + ch)
                sp.dma_start(view(a.ve[:, :], first * VE_W + 64, [[VE_W, count], [1, TB * HD]]),
                             bass.AP(a.ev_skew.tensor, NREL * HD, [[SKEW_W, P], [TB * HD, count], [1, TB * HD]])).then_inc(table_in, 16)
            wp = d["L0_attn_Wproj"]
            sp.dma_start(a.wproj[:, :], wp).then_inc(table_in, 16)
            for hh in range(2):
                for t in range(TB):
                    row = 64 * (1 - hh) + t * HD
                    sp.dma_start(a.wproj_rel[row:row + HD, :, :],
                                 bass.AP(wp.tensor, hh * 64 * C, [[C, HD], [HD * C, 8], [1, C]])).then_inc(table_in, 16)
            sp.dma_start(a.bproj[:, :], d["L0_attn_bproj"].rearrange("(p o) -> p o", o=1),
                         allow_slow_non_contiguous=True).then_inc(table_in, 16)

        @block.gpsimd
        def _(pool):
            step = Chain(pool, pool_step)

            def band(out, base, pattern, width, rows_mult=1):
                if width == 1:
                    step(pool.memset(out, 0.0))
                    step(pool.affine_select(out=out, in_=out, compare_op=ALU.not_equal, fill=1.0, base=base,
                                            pattern=pattern, channel_multiplier=rows_mult))
                    return
                step(pool.memset(out, 1.0))
                step(pool.affine_select(out=out, in_=out, compare_op=ALU.is_ge, fill=0.0, base=base,
                                        pattern=pattern, channel_multiplier=rows_mult))
                step(pool.affine_select(out=out, in_=out, compare_op=ALU.is_ge, fill=0.0, base=width - 1 - base,
                                        pattern=[[-s, n] for s, n in pattern], channel_multiplier=-rows_mult))

            band(a.head_mask[:, :], 0, [[-HD, H]], HD)
            band(a.y_mask[0:64, :, :], 0, [[0, 2], [-HD, 8], [0, TB]], HD)
            for r in (slice(0, 64), slice(64, P)):
                band(a.t_mask[r, :], 0, [[-HD, TB]], HD)
            step(pool.tensor_copy(view(a.y_mask[64:P, 0, :], 0, [[TB, H], [1, TB]]),
                                  view(a.t_mask[64:P, :], 0, [[0, H], [1, TB]])))
            band(a.spread[:, :], 0, [[-HD, H], [0, TB], [-1, HD]], 1)
            for slot in range(2):
                out = a.q_rel[64:64 + TB, slot, :]
                band(out, 0, [[0, HALF_TILES * H], [-1, TB]], 1)
            m = a.e_rel[64:64 + TB, :]
            step(pool.memset(m, 0.0))
            step(pool.affine_select(out=m, in_=m, compare_op=ALU.is_ge, fill=NEG, base=T, pattern=[[-1, T + P]],
                                    channel_multiplier=1))

    return beside


def rel_project_phase(nc, k, a):
    with ExitStack() as ctx:
        def sem(n):
            return phase_semaphore(nc, k, n)

        wqkv, bqk, bv, ek_wide = a.wqkv, a.bqk, a.bv, a.ek_wide
        w_in, table_in = a.w_in, a.table_in
        ps = ctx.enter_context(nc.psum_tensor("ps_qkv0", [P, 8, CH], F32))
        q_ready, k_ready, v_ready = sem("q_ready0"), sem("k_ready0"), sem("v_ready0")
        q_copied, k_copied, v_copied = sem("q_copied0"), sem("k_copied0"), sem("v_copied0")
        ek_turned, ek_copied = sem("ek_turned"), sem("ek_copied")
        block = ctx.enter_context(nc.Block())

        @block.tensor
        def _(pe):
            pe.wait_ge(w_in, 48)
            for n in range(NCH):
                h = k.hT[:, n * CH:(n + 1) * CH]
                wait(pe, q_copied, n - 1)
                pe.matmul(ps[:, n % 2, :], wqkv[:, 0:C], h, start=True, stop=True).then_inc(q_ready, 1)
                wait(pe, k_copied, n - 1)
                pe.matmul(ps[:, 2 + n % 2, :], wqkv[:, C:2 * C], h, start=True, stop=True).then_inc(k_ready, 1)
                wait(pe, v_copied, n - 1)
                for j in range(4):
                    m = pe.matmul(ps[:, 4 + n % 2, j * P:(j + 1) * P], k.hT[:, n * CH + j * P:n * CH + (j + 1) * P],
                                  wqkv[:, 2 * C:3 * C], start=True, stop=True)
                m.then_inc(v_ready, 1)
            pe.wait_ge(table_in, 16 * TABLES)
            for i, u in enumerate((T, P, 0)):
                m = pe.transpose(ps[0:64, 6, i * P:(i + 1) * P], ek_wide[:, u * HD:(u + TB) * HD], k.ident[:, :])
            m.then_inc(ek_turned, 1)

        @block.scalar
        def _(act):
            act.wait_ge(w_in, 48)
            for n in range(NCH):
                act.wait_ge(q_ready, n + 1)
                act.activation(a.qT[:, n * CH:(n + 1) * CH], ps[:, n % 2, :], ACT.Identity,
                               bias=bqk[:, 0:1]).then_inc(q_copied, 1)
            act.wait_ge(ek_turned, 1)
            act.activation(a.e_rel[0:64, :], ps[0:64, 6, 0:3 * P], ACT.Copy).then_inc(ek_copied, 1)

        @block.vector
        def _(dve):
            dve.wait_ge(w_in, 48)
            for n in range(NCH):
                dve.wait_ge(k_ready, n + 1)
                dve.tensor_scalar(a.kT[:, n * CH:(n + 1) * CH], ps[:, 2 + n % 2, :], bqk[:, 1:2], QK_SCALE,
                                  ALU.add, ALU.mult).then_inc(k_copied, 1)
                dve.wait_ge(v_ready, n + 1)
                out = a.v[:, 4 * n * C:4 * (n + 1) * C]
                dve.tensor_tensor(view(out, 0, [[C, 4], [1, C]]), ps[:, 4 + n % 2, :].rearrange("p (j c) -> p j c", j=4),
                                  view(bv[:, :], 0, [[0, 4], [1, C]]), ALU.add).then_inc(v_copied, 1)
            dve.wait_ge(table_in, 16 * TABLES)
            dve.tensor_scalar(a.gate_bias[:, :], k.mod[:, 0, 2, :], a.bproj[:, 0:1], None, ALU.mult)


def rel_attention_phase(nc, k, a):
    with ExitStack() as ctx:
        def sb(n, s, dt=F32):
            return ctx.enter_context(nc.sbuf_tensor(n, s, dt))

        def sem(n):
            return phase_semaphore(nc, k, n)

        prob = sb("prob", [P, 4, QUAD, T])
        neg_max = sb("neg_max", [P, 4, QUAD])
        den = sb("den", [P, 4, QUAD])
        rden = sb("rden", [P, 4, QUAD])
        probT = sb("probT", [P, 2, 2, CH])
        y_all = sb("y_all", [64, CH])
        y_v, y_rel = sb("y_v", [P, 2, P]), sb("y_rel", [P, 2, HALF_TILES * 64])
        v_high = sb("v_high", [P, 2, 2, 64])
        upd = sb("upd", [P, 2, P])
        ps_s = ctx.enter_context(nc.psum_tensor("ps_s", [P, 2, QUAD, T], F32))
        ps_t = ctx.enter_context(nc.psum_tensor("ps_t", [P, 2, CH], F32))
        ps_y = ctx.enter_context(nc.psum_tensor("ps_y", [P, CH], F32))
        ps_m = ctx.enter_context(nc.psum_tensor("ps_m", [P, CH], F32))
        score, maxed, expd, rden_ready, probs = sem("score"), sem("maxed"), sem("expd"), sem("rden_ready"), sem("probs")
        turned, turned_out, pv, masked = sem("turned"), sem("turned_out"), sem("pv"), sem("masked")
        spread, q_rel_ready, q_diag_ready, v_ready = sem("spread_s"), sem("q_rel_ready"), sem("q_diag_ready"), sem("v_ready")
        y_ready, projd, gated, added = sem("y_ready"), sem("projd"), sem("gated"), sem("added")
        block = ctx.enter_context(nc.Block())

        def turns(b, q):
            return 12 * b + (q if q < 4 else 4 + 2 * (q - 4))

        def quad(b, q):
            return b + q // NQ, q % NQ

        def exists(b, q=0):
            return not isinstance(b, int) or 0 <= b < B

        def sequences(eng, body):
            body(-1)
            body(0)
            with eng.Fori(1, B - 1) as b:
                body(b)
            body(B - 1)

        def spread_group(b, q):
            if q < 1:
                return b, 1, 3
            if q < 5:
                return b + 1, 0, q - 1
            return b + 1, 1, q - 5

        @block.tensor
        def _(pe):
            def body(b):
                for q in range(NQ):
                    n = NQ * b + q
                    sb_, sq_ = quad(b, q + 2)
                    if exists(sb_):
                        sn = n + 2
                        half, slot, r = sq_ // 4, sq_ // 4, q % 2
                        if sq_ % 4 == 0:
                            c = 2 * sb_ + half
                            pe.wait_ge(q_diag_ready, c + 1)
                            pe.wait_ge(q_rel_ready, NG * c + NG)
                        wait(pe, expd, sn - 1)
                        keys = 4 * TB * (sq_ + 1)
                        for j in range(QUAD):
                            i = QUAD * sq_ + j
                            rows = slice((i % HALF_TILES) * P, (i % HALF_TILES + 1) * P)
                            pe.matmul(ps_s[:, r, j, 0:keys], a.q_diag[:, slot, rows], a.kT[:, bass.ds(sb_ * T, keys)],
                                      start=True, stop=False)
                            m = pe.matmul(ps_s[:, r, j, 0:keys], a.q_rel[0:64 + TB, slot, rows],
                                          a.e_rel[0:64 + TB, T - TB * i:T - TB * i + keys], start=False, stop=True)
                        m.then_inc(score, 1)
                    if exists(b):
                        pe.wait_ge(probs, n + 1)
                        wait(pe, turned_out, turns(b, q))
                        pe.nop(nofuse=True)
                        keys = 4 * TB * (q + 1)
                        for ch in range(1 if q < 4 else 2):
                            ks = min(P, keys - ch * P)
                            for j in range(QUAD):
                                m = pe.transpose(ps_t[0:ks, ch, j * P:(j + 1) * P],
                                                 prob[:, q % 4, j, ch * P:ch * P + ks], k.ident[:, :])
                            m.then_inc(turned, 1)
                    if q == 1 or q == 5:
                        c = 2 * b + (0 if q == 5 else -1)
                        if exists(b) and not (isinstance(c, int) and c < 0):
                            project(b, q, c)
                    pb, pq = quad(b, q - 1)
                    if exists(pb):
                        values(pb, pq, n - 1)
                    gb, half, g = spread_group(b, q)
                    if exists(gb):
                        c = 2 * gb + half
                        wait(pe, q_rel_ready, NG * c + g)
                        wait(pe, gated, 2 * b + (-1 if q < 1 else 0 if q < 5 else 1))
                        pe.nop(nofuse=True)
                        for h in range(2):
                            w = (4 * g + 2 * h) * TB * HD
                            m = pe.matmul(ps_m[:, h * P:(h + 1) * P], a.spread[:, w:w + P],
                                          a.qT[:, bass.ds(gb * T + half * P, P)], start=True, stop=True)
                        m.then_inc(spread, 1)

            def values(b, q, n):
                pe.wait_ge(turned_out, turns(b, q) + (1 if q < 4 else 2))
                pe.wait_ge(v_ready, n + (4 if q % 4 == 0 else 1))
                wait(pe, masked, n)
                keys = 4 * TB * (q + 1)
                chunks = [(ch, min(P, keys - ch * P)) for ch in range(1 if q < 4 else 2)]
                for j in range(QUAD):
                    for ch, ks in chunks:
                        at = ve_block(QUAD * q + j, ch) * VE_W
                        pe.matmul(ps_y[:, j * P:(j + 1) * P], a.ve[0:ks, at:at + P], probT[0:ks, q % 2, ch, j * P:(j + 1) * P],
                                  start=ch == 0, stop=ch == len(chunks) - 1)
                for ch, ks in chunks:
                    m = pe.matmul(view(ps_y[0:64, :], 64, [[P, QUAD], [1, 64]]), v_high[0:ks, q // 4, ch, :],
                                  view(probT[0:ks, q % 2, ch, :], 64, [[P, QUAD], [1, 64]]),
                                  start=ch == 0, stop=ch == len(chunks) - 1)
                m.then_inc(pv, 1)

            def project(b, q, c):
                pe.wait_ge(y_ready, 4 * c + 4)
                wait(pe, gated, c)
                gb, half, _ = spread_group(b, q - 1)
                pe.wait_ge(q_rel_ready, NG * (2 * gb + half + 1) if exists(gb) else NG * HALVES)
                slot = 1 if q == 1 else 0
                pe.matmul(ps_m[:, 0:P], a.wproj[:, :], y_v[:, slot, :], start=True, stop=False)
                for h in range(8):
                    m = pe.matmul(ps_m[:, 0:P], a.wproj_rel[:, h, :],
                                  view(y_rel[:, slot, :], h * TB, [[64, HALF_TILES], [1, TB]]), start=False, stop=h == 7)
                m.then_inc(projd, 1)

            sequences(pe, body)
            values(B - 1, NQ - 1, NQ * B - 1)
            project(B, 1, HALVES - 1)

        @block.vector
        def _(dve):
            def body(b):
                for q in range(NQ):
                    n = NQ * b + q
                    sb_, sq_ = quad(b, q + 2)
                    sn = n + 2
                    keys = 4 * TB * (sq_ + 1)
                    if exists(sb_):
                        dve.wait_ge(score, sn + 1)
                        dve.tensor_reduce(neg_max[:, sq_ % 4, :], ps_s[:, q % 2, :, 0:keys], AX.X, ALU.max,
                                          negate=True).then_inc(maxed, 1)
                    pb, pq = quad(b, q - 1)
                    if exists(pb):
                        mask(pb, pq, n - 1)
                    gb, half, g = spread_group(b, q)
                    if exists(gb):
                        c = 2 * gb + half
                        dve.wait_ge(spread, NG * c + g + 1)
                        wait(dve, score, 4 * c - 4)
                        for x in range(2):
                            r = slice(64 * x, 64 * x + 64)
                            out = view(a.q_rel[0:64, half, :], (4 * g + x) * TB, [[2 * TB, 2], [P, HALF_TILES], [1, TB]])
                            m = dve.tensor_tensor(out, view(ps_m[r, :], 0, [[P, 2], [TB, HALF_TILES], [1, TB]]),
                                                  view(a.t_mask[r, :], 0, [[0, 2], [0, HALF_TILES], [1, TB]]), ALU.mult)
                        m.then_inc(q_rel_ready, 1)
                    vb, vq = quad(b, q + 6)
                    if exists(vb):
                        place_values(vb, vq, n + 6)
                    if exists(sb_):
                        dve.wait_ge(expd, sn + 1)
                        dve.reciprocal(rden[:, sq_ % 4, :], den[:, sq_ % 4, :]).then_inc(rden_ready, 1)
                    if (q == 2 or q == 6) and exists(b):
                        c = 2 * b + (0 if q == 6 else -1)
                        if not (isinstance(c, int) and c < 0):
                            add(c, 1 if q == 2 else 0)

            def mask(b, q, n):
                dve.wait_ge(pv, n + 1)
                if q % 4 == 0:
                    wait(dve, projd, 2 * b + q // 4 - 1)
                for hh in range(2):
                    out = y_rel[64 * (1 - hh):64 * (2 - hh), q // 4, (q % 4) * QUAD * 64:(q % 4 + 1) * QUAD * 64]
                    dve.tensor_tensor(view(out, 0, [[64, QUAD], [1, 64]]), view(ps_y[64:P, :], 64 * hh, [[P, QUAD], [1, 64]]),
                                      view(a.y_mask[64:P, 0, :], 0, [[0, QUAD], [1, 64]]), ALU.mult)
                wait(dve, y_ready, n)
                dve.nop(nofuse=True)
                dve.tensor_tensor(y_all[:, :], ps_y[0:64, :], view(a.y_mask[0:64, 0, :], 0, [[0, QUAD], [1, P]]),
                                  ALU.mult).then_inc(masked, 1)
                dve.wait_ge(masked, n + 1)
                for hh in range(2):
                    out = y_v[64 * hh:64 * hh + 64, q // 4, (q % 4) * QUAD * TB:(q % 4 + 1) * QUAD * TB]
                    m = dve.tensor_reduce(view(out, 0, [[TB, QUAD], [1, TB]]),
                                          view(y_all[:, :], 64 * hh, [[P, QUAD], [1, TB], [TB, 8]]), AX.X, ALU.add)
                m.then_inc(y_ready, 1)

            def place_values(b, q, n):
                wait(dve, pv, n - 7)
                dve.nop(nofuse=True)
                if q % 4 == 3:
                    for ch in range(1 + q // 4):
                        dve.tensor_copy(v_high[:, q // 4, ch, :], a.v[:, bass.ds(b * 2 * C + ch * C + 64, 64)])
                for ch in range(1 if q < 4 else 2):
                    at = ve_block(QUAD * q, ch) * VE_W
                    m = dve.tensor_copy(view(a.ve[:, :], at, [[VE_W, QUAD], [1, 64]]),
                                        view(a.v[:, bass.ds(b * 2 * C + ch * C, 64)], 0, [[0, QUAD], [1, 64]]))
                m.then_inc(v_ready, 1)

            def add(c, half):
                dve.wait_ge(gated, c + 1)
                xs = k.xT[:, bass.ds(c * P, P)]
                dve.tensor_tensor(xs, xs, upd[:, half, :], ALU.add).then_inc(added, 1)

            sequences(dve, body)
            mask(B - 1, NQ - 1, NQ * B - 1)
            add(HALVES - 1, 1)

        @block.scalar
        def _(act):
            def body(b):
                for q in range(NQ):
                    n = NQ * b + q
                    sb_, sq_ = quad(b, q + 2)
                    sn = n + 2
                    keys = 4 * TB * (sq_ + 1)
                    if exists(sb_):
                        act.wait_ge(maxed, sn + 1)
                        ob, oq = quad(sb_, sq_ - 3)
                        wait(act, turned, turns(ob, oq))
                        for j in range(QUAD):
                            m = act.activation(prob[:, sq_ % 4, j, 0:keys], ps_s[:, q % 2, j, 0:keys], ACT.Exp,
                                               bias=neg_max[:, sq_ % 4, j:j + 1], accum_out=den[:, sq_ % 4, j:j + 1])
                        m.then_inc(expd, 1)
                    if exists(b):
                        if q == 1 or q == 5:
                            c = 2 * b + (0 if q == 5 else -1)
                            if not (isinstance(c, int) and c < 0):
                                gate(b if q == 5 else b - 1, 0 if q == 5 else 1, c)
                        keys = 4 * TB * (q + 1)
                        wait(act, pv, n - 1)
                        for ch in range(1 if q < 4 else 2):
                            ks = min(P, keys - ch * P)
                            act.wait_ge(turned, turns(b, q) + ch + 1)
                            act.activation(probT[0:ks, q % 2, ch, :], ps_t[0:ks, ch, :], ACT.Copy).then_inc(turned_out, 1)

            def gate(b, half, c):
                act.wait_ge(projd, c + 1)
                wait(act, added, c - 1)
                act.activation(upd[:, half, :], ps_m[:, 0:P], ACT.Identity, scale=k.mod[:, 0, 2, bass.ds(b, 1)],
                               bias=a.gate_bias[:, bass.ds(b, 1)]).then_inc(gated, 1)

            sequences(act, body)
            gate(B - 1, 1, HALVES - 1)

        @block.gpsimd
        def _(pool):
            def body(b):
                for q in range(NQ):
                    n = NQ * b + q
                    if q == 2 or q == 6:
                        half = 0 if q == 2 else 1
                        if exists(b + 1):
                            c = 2 * (b + 1) + half
                            wait(pool, score, 4 * c - 4)
                            out = a.q_diag[:, half, :]
                            q_in = a.qT[:, bass.ds((b + 1) * T + half * P, P)]
                            pool.tensor_tensor(view(out, 0, [[P, HALF_TILES], [TB, H], [1, TB]]),
                                               view(q_in, 0, [[TB, HALF_TILES], [0, H], [1, TB]]),
                                               view(a.head_mask[:, :], 0, [[0, HALF_TILES], [1, H], [0, TB]]),
                                               ALU.mult).then_inc(q_diag_ready, 1)
                    sb_, sq_ = quad(b, q + 2)
                    if exists(sb_):
                        keys = 4 * TB * (sq_ + 1)
                        pool.wait_ge(rden_ready, n + 3)
                        ps_ = prob[:, sq_ % 4, :, 0:keys]
                        pool.tensor_tensor(ps_, ps_, view(rden[:, sq_ % 4, :], 0, [[1, QUAD], [0, keys]]),
                                           ALU.mult).then_inc(probs, 1)

            sequences(pool, body)


KEPT = max(1, int(T * 0.3))
PARTS = ((0, 6), (6, 6), (12, 4))


def sparse_tables(nc, d, k, a):
    a.w_in, a.const_ready, pool_step = (phase_semaphore(nc, k, n) for n in ("w_in1", "const_ready3", "pool_step3"))
    w_in, const_ready, before = a.w_in, a.const_ready, a.before
    w_rows, wi1_rows, bq, bi1, bi2, wi2, bkv = a.w_rows, a.wi1_rows, a.bq, a.bi1, a.bi2, a.wi2, a.bkv

    def column(name, n):
        return d[name].rearrange("(p o) -> p o", o=1)[0:n, :]

    def beside(block):
        @block.sync
        def _(sp):
            for i, name in enumerate(("wq", "wk", "wv", "wo")):
                sp.dma_start(w_rows[:, i, :], d["L1_attn_" + name]).then_inc(w_in, 16)
            sp.dma_start(wi1_rows[:, :], d["L1_attn_wi1"]).then_inc(w_in, 16)
            sp.dma_start(bq[:, :], column("L1_attn_bq", P), allow_slow_non_contiguous=True).then_inc(w_in, 16)
            sp.dma_start(a.bo[:, :], column("L1_attn_bo", P), allow_slow_non_contiguous=True).then_inc(w_in, 16)
            sp.dma_start(bi1[:, :], column("L1_attn_bi1", C // 2), allow_slow_non_contiguous=True).then_inc(w_in, 16)
            sp.dma_start(wi2[:, :], d["L1_attn_wi2"].rearrange("o p -> p o"), allow_slow_non_contiguous=True).then_inc(w_in, 16)
            sp.dma_start(bi2[:, :], bass.AP(d["L1_attn_bi2"].tensor, 0, [[0, P], [1, 1]]),
                         allow_slow_non_contiguous=True).then_inc(w_in, 16)
            for i, name in enumerate(("bk", "bv")):
                sp.dma_start(bkv[:, i * C:(i + 1) * C],
                             bass.AP(d["L1_attn_" + name].tensor, 0, [[0, P], [1, C]])).then_inc(w_in, 16)

        @block.gpsimd
        def _(pool):
            step = Chain(pool, pool_step)
            step(pool.memset(before[:, :, :], 1.0))
            step(pool.affine_select(out=before[:, :, :], in_=before[:, :, :], compare_op=ALU.is_gt, fill=0.0, base=0,
                                    pattern=[[P, 2], [-1, T]], channel_multiplier=1))
            m = a.group_mask[:, :, :]
            step(pool.memset(m, 1.0))
            step(pool.affine_select(out=m, in_=m, compare_op=ALU.is_ge, fill=0.0, base=0,
                                    pattern=[[-HD, 4], [1, 4 * HD]], channel_multiplier=0))
            step(pool.affine_select(out=m, in_=m, compare_op=ALU.is_ge, fill=0.0, base=HD - 1,
                                    pattern=[[HD, 4], [-1, 4 * HD]], channel_multiplier=0))
            m = a.head_mask[:, :]
            step(pool.memset(m, 1.0))
            step(pool.affine_select(out=m, in_=m, compare_op=ALU.is_ge, fill=0.0, base=0,
                                    pattern=[[-HD, H]], channel_multiplier=1))
            step(pool.affine_select(out=m, in_=m, compare_op=ALU.is_ge, fill=0.0, base=HD - 1,
                                    pattern=[[HD, H]], channel_multiplier=-1))
            pool.iota(a.places[:, :], [[1, KEPT]], base=0, channel_multiplier=0,
                      allow_small_or_imprecise_dtypes=True).then_inc(const_ready, 1)

    return beside


def sparse_project_phase(nc, k, a):
    with ExitStack() as ctx:
        def sb(n, s, dt=F32):
            return ctx.enter_context(nc.sbuf_tensor(n, s, dt))

        def sem(n):
            return phase_semaphore(nc, k, n)

        w_in, const_ready, before = a.w_in, a.const_ready, a.before
        w_rows, wi1_rows, bq, bi1, bi2, wi2, bkv = a.w_rows, a.wi1_rows, a.bq, a.bi1, a.bi2, a.wi2, a.bkv
        w_T = sb("w_T1", [P, 3 * C])
        wi1_T = sb("wi1_T", [P, C // 2])
        wi2_rep = sb("wi2_rep", [C // 2, P])
        hid = sb("hid1", [C // 2, 2, CH])
        imp_row = sb("imp_row", [P, NTOK])
        imp_col = sb("imp_col", [P, NT])
        compared = sb("compared", [P, 4, 2, T])
        above = sb("above", [P, NT])
        tied = sb("tied", [P, NT])
        ps = ctx.enter_context(nc.psum_tensor("ps_proj1", [P, 8, CH], F32))
        w_turned, w_copied, wi2_ready = sem("w_turned1"), sem("w_copied1"), sem("wi2_ready")
        q_ready, kv_ready, hid_ready, imp_ready = sem("q_ready1"), sem("kv_ready1"), sem("hid_ready1"), sem("imp_ready1")
        q_copied, kv_copied, hid_copied, imp_copied = sem("q_copied1"), sem("kv_copied1"), sem("hid_copied1"), sem("imp_copied1")
        turned, col_ready, ranked = sem("imp_turned"), sem("col_ready"), sem("ranked")
        block = ctx.enter_context(nc.Block())

        @block.tensor
        def _(pe):
            pe.wait_ge(w_in, 16 * 12)
            for i in range(4):
                pe.transpose(ps[:, 0, i * C:(i + 1) * C], w_rows[:, i, :], k.ident[:, :])
            pe.transpose(ps[:, 1, 0:C // 2], wi1_rows[:, :], k.ident[0:C // 2, 0:C // 2]).then_inc(w_turned, 1)
            pe.wait_ge(w_copied, 3)
            pe.wait_ge(wi2_ready, 1)
            for n in range(NCH + 2):
                if n < NCH:
                    h = k.hT[:, n * CH:(n + 1) * CH]
                    wait(pe, hid_copied, n)
                    pe.matmul(ps[0:C // 2, 4, :], wi1_T[:, :], h, start=True, stop=True).then_inc(hid_ready, 1)
                    wait(pe, q_copied, n - 1)
                    pe.matmul(ps[:, n % 2, :], w_T[:, 0:C], h, start=True, stop=True).then_inc(q_ready, 1)
                if 1 <= n <= NCH:
                    m = n - 1
                    pe.wait_ge(hid_copied, m + 1)
                    wait(pe, imp_copied, m)
                    pe.matmul(ps[:, 5, :], wi2_rep[:, :], hid[:, m % 2, :], start=True, stop=True).then_inc(imp_ready, 1)
                if n < NCH:
                    for g in range(2):
                        u = 2 * n + g
                        wait(pe, kv_copied, u - 1)
                        for j in range(2):
                            t = 4 * n + 2 * g + j
                            m = pe.matmul(ps[:, 2 + u % 2, j * 2 * C:(j + 1) * 2 * C], k.hT[:, t * P:(t + 1) * P],
                                          w_T[:, C:3 * C], start=True, stop=True)
                        m.then_inc(kv_ready, 1)
                if n >= 2:
                    c = n - 2
                    pe.wait_ge(imp_copied, c + 1)
                    wait(pe, col_ready, c - 1)
                    for j in range(4):
                        t = 4 * c + j
                        m = pe.transpose(ps[:, 6 + c % 2, j:j + 1], imp_row[0:1, t * P:(t + 1) * P], k.ident[0:1, 0:1])
                    m.then_inc(turned, 1)

        @block.scalar
        def _(act):
            act.wait_ge(w_turned, 1)
            act.activation(w_T[:, :], ps[:, 0, 0:3 * C], ACT.Copy).then_inc(w_copied, 1)
            act.activation(a.wo_T[:, :], ps[:, 0, 3 * C:4 * C], ACT.Copy).then_inc(w_copied, 1)
            act.activation(wi1_T[:, :], ps[:, 1, 0:C // 2], ACT.Copy).then_inc(w_copied, 1)
            for n in range(NCH + 1):
                if n < NCH:
                    act.wait_ge(hid_ready, n + 1)
                    wait(act, imp_ready, n - 1)
                    act.activation(hid[:, n % 2, :], ps[0:C // 2, 4, :], ACT.Relu, bias=bi1[:, 0:1]).then_inc(hid_copied, 1)
                if n >= 1:
                    act.wait_ge(imp_ready, n)
                    act.activation(imp_row[:, (n - 1) * CH:n * CH], ps[:, 5, :], ACT.Identity, bias=bi2[:, 0:1]).then_inc(imp_copied, 1)

        @block.vector
        def _(dve):
            dve.wait_ge(w_in, 16 * 12)
            dve.tensor_scalar(wi2_rep[:, :], k.ones[0:C // 2, :], wi2[:, 0:1], None, ALU.mult).then_inc(wi2_ready, 1)
            dve.tensor_scalar(a.gate_bias[:, :], k.mod[:, 1, 2, :], a.bo[:, 0:1], None, ALU.mult)
            for n in range(NCH + 2):
                if n < NCH:
                    dve.wait_ge(q_ready, n + 1)
                    dve.tensor_scalar(a.qT[:, n * CH:(n + 1) * CH], ps[:, n % 2, :], bq[:, 0:1], QK_SCALE,
                                      ALU.add, ALU.mult).then_inc(q_copied, 1)
                    for g in range(2):
                        u = 2 * n + g
                        dve.wait_ge(kv_ready, u + 1)
                        dve.tensor_tensor(a.kv[:, 2 * u:2 * u + 2, :], ps[:, 2 + u % 2, :].rearrange("p (j c) -> p j c", j=2),
                                          view(bkv[:, :], 0, [[0, 2], [1, 2 * C]]), ALU.add).then_inc(kv_copied, 1)
                if n >= 2:
                    c = n - 2
                    dve.wait_ge(turned, c + 1)
                    if c == 0:
                        dve.wait_ge(const_ready, 1)
                    dve.tensor_copy(imp_col[:, 4 * c:4 * c + 4], ps[:, 6 + c % 2, 0:4]).then_inc(col_ready, 1)
                    dve.wait_ge(col_ready, c + 1)
                    wait(dve, ranked, c)
                    dve.nop(nofuse=True)
                    for j in range(4):
                        t = 4 * c + j
                        row = imp_row[:, t // 2 * T:(t // 2 + 1) * T]
                        dve.tensor_scalar(compared[:, j, 0, :], row, imp_col[:, t:t + 1], 0.0, ALU.is_gt, ALU.add,
                                          accum_out=above[:, t:t + 1])
                        m = dve.scalar_tensor_tensor(out=compared[:, j, 1, :], in0=row, scalar=imp_col[:, t:t + 1],
                                                     in1=before[:, t % 2, :], op0=ALU.is_equal, op1=ALU.mult,
                                                     accum_out=tied[:, t:t + 1])
                    m.then_inc(ranked, 1)
            dve.wait_ge(ranked, NCH)
            dve.tensor_tensor(a.rank[:, :], above[:, :], tied[:, :], ALU.add)


def sparse_attention_phase(nc, k, a):
    with ExitStack() as ctx:
        def sb(n, s, dt=F32):
            return ctx.enter_context(nc.sbuf_tensor(n, s, dt))

        def sem(n):
            return phase_semaphore(nc, k, n)

        select = sb("select", [P, 2, 2, KEPT])
        kv_kept = sb("kv_kept", [KEPT, 2, 2 * C])
        k_diag = sb("k_diag", [P, 2, H * KEPT])
        v_diag = sb("v_diag", [KEPT, 2, H, 4 * HD])
        q_now = sb("q_now", [P, 2, T])
        prob = sb("prob1", [P, 4, H, KEPT])
        top = sb("top1", [P, 4, H])
        den = sb("den1", [P, 4, H])
        rden = sb("rden1", [P, 4, H])
        probT = sb("probT1", [KEPT, 2, CH])
        y_T = sb("y_T1", [P, 2, P])
        upd = sb("upd1", [P, 2, P])
        ps_s = ctx.enter_context(nc.psum_tensor("ps_s1", [P, 3, CH], F32))
        ps_g = ctx.enter_context(nc.psum_tensor("ps_g1", [P, CH], F32))
        ps_t = ctx.enter_context(nc.psum_tensor("ps_t1", [P, 2, CH], F32))
        ps_y = ctx.enter_context(nc.psum_tensor("ps_y1", [P, CH], F32))
        ps_o = ctx.enter_context(nc.psum_tensor("ps_o1", [P, CH], F32))
        selected, gathered, kept, k_turned = sem("selected"), sem("gathered"), sem("kept"), sem("k_turned")
        k_ready, v_ready, q_ready = sem("k_ready4"), sem("v_ready4"), sem("q_ready4")
        score, maxed, shifted, expd, summed = sem("score1"), sem("maxed1"), sem("shifted1"), sem("expd1"), sem("summed1")
        rden_ready, probs, turned, turned_out = sem("rden1_ready"), sem("probs1"), sem("turned1"), sem("turned_out1")
        pv, y_out, projd, gated, added = sem("pv1"), sem("y_out1"), sem("projd1"), sem("gated1"), sem("added1")
        block = ctx.enter_context(nc.Block())

        def exists(w):
            return not isinstance(w, int) or 0 <= w < HALVES

        def pairs(eng, step):
            def body(i):
                for s in range(4):
                    step(4 * i + s, 2 * i + s // 2, s)
            body(-1)
            body(0)
            with eng.Fori(1, B // 2 - 1) as i:
                body(i)
            body(B // 2 - 1)

        @block.tensor
        def _(pe):
            def scores(w, b, s, part):
                first, count = PARTS[part]
                if part == 0:
                    pe.wait_ge(k_ready, b + 1)
                    pe.wait_ge(q_ready, b + 1)
                if part < 2:
                    wait(pe, shifted, 2 * w + part - 1)
                else:
                    wait(pe, expd, 3 * w)
                pe.matmul(ps_s[:, part, 0:count * KEPT], q_now[:, s // 2, (s % 2) * P:(s % 2 + 1) * P],
                          k_diag[:, s // 2, first * KEPT:(first + count) * KEPT], start=True, stop=True).then_inc(score, 1)

            def turn(w, s, g):
                pe.wait_ge(probs, 3 * w + (1, 2, 2, 3)[g])
                wait(pe, turned_out, 4 * w + g - 1)
                for h in range(4):
                    m = pe.transpose(ps_t[0:KEPT, g % 2, h * P:(h + 1) * P], prob[:, s, 4 * g + h, :], k.ident[:, :])
                m.then_inc(turned, 1)

            def values(w, b, s, g):
                pe.wait_ge(turned_out, 4 * w + g + 1)
                if g == 0:
                    pe.wait_ge(v_ready, b + 1)
                    wait(pe, y_out, w - 1)
                pe.nop(nofuse=True)
                for h in range(4):
                    m = pe.matmul(ps_y[4 * HD * g:4 * HD * (g + 1), (s % 2) * P:(s % 2 + 1) * P],
                                  v_diag[:, s // 2, 4 * g + h, :], probT[:, g % 2, h * P:(h + 1) * P],
                                  start=h == 0, stop=h == 3)
                m.then_inc(pv, 1)

            def project(w, s):
                pe.wait_ge(y_out, w + 1)
                wait(pe, gated, w)
                pe.matmul(ps_o[:, 0:P], a.wo_T[:, :], y_T[:, s % 2, :], start=True, stop=True).then_inc(projd, 1)

            def step(w, b, s):
                nb = b + 2
                ahead = exists(2 * nb)
                if ahead and s % 2 == 1:
                    pe.wait_ge(kept, nb + 1)
                    pe.transpose(ps_g[:, 2 * C:2 * C + KEPT], kv_kept[:, s // 2, 0:C],
                                 k.ident[0:KEPT, 0:KEPT]).then_inc(k_turned, 1)
                now, nxt = exists(w), exists(w + 2)
                ns = (s + 2) % 4
                if now:
                    turn(w, s, 0)
                if nxt:
                    scores(w + 2, b + 1, ns, 0)
                if now:
                    turn(w, s, 1)
                    values(w, b, s, 0)
                if nxt:
                    scores(w + 2, b + 1, ns, 1)
                if now:
                    turn(w, s, 2)
                    values(w, b, s, 1)
                if ahead and s % 2 == 0:
                    pe.wait_ge(selected, nb + 1)
                    wait(pe, kept, nb)
                    wait(pe, k_ready, nb)
                    pe.nop(nofuse=True)
                    for ch in range(2):
                        m = pe.matmul(ps_g[0:KEPT, 0:2 * C], select[:, s // 2, ch, :],
                                      a.kv[:, bass.ds(2 * nb + ch, 1), :], start=ch == 0, stop=ch == 1)
                    m.then_inc(gathered, 1)
                if nxt:
                    scores(w + 2, b + 1, ns, 2)
                if now:
                    turn(w, s, 3)
                    values(w, b, s, 2)
                if exists(w - 1) and exists(w):
                    project(w - 1, s + 1)
                if now:
                    values(w, b, s, 3)

            pairs(pe, step)
            project(HALVES - 1, HALVES - 1)

        @block.vector
        def _(dve):
            def largest(w, s, part):
                first, count = PARTS[part]
                r = slice(first, first + count)
                scores = ps_s[:, part, 0:count * KEPT].rearrange("p (h r) -> p h r", h=count)
                dve.wait_ge(score, 3 * w + part + 1)
                dve.tensor_reduce(top[:, s, r], scores, AX.X, ALU.max, negate=part == 2).then_inc(maxed, 1)

            def shift(w, s, part):
                first, count = PARTS[part]
                r = slice(first, first + count)
                scores = ps_s[:, part, 0:count * KEPT].rearrange("p (h r) -> p h r", h=count)
                largest(w, s, part)
                dve.wait_ge(maxed, 3 * w + part + 1)
                wait(dve, turned, 4 * w - 12)
                dve.tensor_tensor(prob[:, s, r, :], scores, view(top[:, s, r], 0, [[1, count], [0, KEPT]]),
                                  ALU.subtract).then_inc(shifted, 1)

            def total(w, s, part):
                first, count = PARTS[part]
                r = slice(first, first + count)
                dve.wait_ge(expd, 3 * w + part + 1)
                if part < 2:
                    dve.tensor_reduce(den[:, s, r], prob[:, s, r, :], AX.X, ALU.add).then_inc(summed, 1)
                    dve.wait_ge(summed, 2 * w + part + 1)
                dve.reciprocal(rden[:, s, r], den[:, s, r]).then_inc(rden_ready, 1)

            def step(w, b, s):
                nb = b + 2
                nxt, ns = exists(w + 2), (s + 2) % 4
                if s % 2 == 1 and exists(2 * nb):
                    dve.wait_ge(k_turned, nb + 1)
                    wait(dve, score, 6 * (nb - 1))
                    dve.tensor_tensor(k_diag[:, s // 2, :].rearrange("p (h r) -> p h r", h=H),
                                      view(ps_g[:, 2 * C:2 * C + KEPT], 0, [[0, H], [1, KEPT]]),
                                      view(a.head_mask[:, :], 0, [[1, H], [0, KEPT]]), ALU.mult).then_inc(k_ready, 1)
                if s % 2 == 0 and exists(2 * nb):
                    wait(dve, gathered, nb - 1)
                    dve.nop(nofuse=True)
                    for ch in range(2):
                        m = dve.tensor_scalar(select[:, s // 2, ch, :], a.places[:, :],
                                              a.rank[:, bass.ds(2 * nb + ch, 1)], None, ALU.is_equal)
                    m.then_inc(selected, 1)
                if nxt:
                    shift(w + 2, ns, 0)
                if exists(w + 1):
                    total(w + 1, (s + 1) % 4, 2)
                if nxt:
                    shift(w + 2, ns, 1)
                    total(w + 2, ns, 0)
                    largest(w + 2, ns, 2)
                    total(w + 2, ns, 1)
                if exists(w - 1) and exists(w):
                    add(w - 1, s + 1)

            def add(w, s):
                dve.wait_ge(gated, w + 1)
                xs = k.xT[:, bass.ds(w * P, P)]
                dve.tensor_tensor(xs, xs, upd[:, s % 2, :], ALU.add).then_inc(added, 1)

            pairs(dve, step)
            add(HALVES - 1, HALVES - 1)

        @block.scalar
        def _(act):
            def exp(w, s, part):
                first, count = PARTS[part]
                if part < 2:
                    act.wait_ge(shifted, 2 * w + part + 1)
                    p = prob[:, s, first:first + count, :]
                    act.activation(p, p, ACT.Exp).then_inc(expd, 1)
                else:
                    act.wait_ge(maxed, 3 * w + part + 1)
                    wait(act, turned, 4 * w - 12)
                    for h in range(count):
                        m = act.activation(prob[:, s, first + h, :], ps_s[:, part, h * KEPT:(h + 1) * KEPT], ACT.Exp,
                                           bias=top[:, s, first + h:first + h + 1],
                                           accum_out=den[:, s, first + h:first + h + 1])
                    m.then_inc(expd, 1)

            def copy(w, s, g):
                act.wait_ge(turned, 4 * w + g + 1)
                wait(act, pv, 4 * w + g - 1)
                act.activation(probT[:, g % 2, :], ps_t[0:KEPT, g % 2, :], ACT.Copy).then_inc(turned_out, 1)

            def gate(w, b, s):
                act.wait_ge(projd, w + 1)
                wait(act, added, w - 1)
                act.nop(nofuse=True)
                act.activation(upd[:, s % 2, :], ps_o[:, 0:P], ACT.Identity, scale=k.mod[:, 1, 2, bass.ds(b, 1)],
                               bias=a.gate_bias[:, bass.ds(b, 1)]).then_inc(gated, 1)

            def step(w, b, s):
                nb = b + 2
                now, nxt, ns = exists(w), exists(w + 2), (s + 2) % 4
                if now:
                    copy(w, s, 0)
                if exists(w + 1):
                    exp(w + 1, (s + 1) % 4, 2)
                if now:
                    copy(w, s, 1)
                if nxt:
                    exp(w + 2, ns, 0)
                if now:
                    copy(w, s, 2)
                if s % 2 == 0 and exists(2 * nb):
                    act.wait_ge(gathered, nb + 1)
                    wait(act, v_ready, nb - 1)
                    act.activation(kv_kept[:, s // 2, :], ps_g[0:KEPT, 0:2 * C], ACT.Copy).then_inc(kept, 1)
                if now:
                    copy(w, s, 3)
                if nxt:
                    exp(w + 2, ns, 1)
                if exists(w - 1) and exists(w):
                    gate(w - 1, b - (1 - s % 2), s + 1)
                if now:
                    act.wait_ge(pv, 4 * w + 4)
                    wait(act, projd, w - 1)
                    act.activation(y_T[:, s % 2, :], ps_y[:, (s % 2) * P:(s % 2 + 1) * P], ACT.Copy).then_inc(y_out, 1)

            pairs(act, step)
            gate(HALVES - 1, B - 1, HALVES - 1)

        @block.gpsimd
        def _(pool):
            def step(w, b, s):
                nb = b + 2
                if s % 2 == 0 and exists(2 * (b + 1)):
                    slot = (s // 2 + 1) % 2
                    pool.wait_ge(kept, b + 2)
                    wait(pool, pv, 8 * b)
                    pool.nop(nofuse=True)
                    pool.tensor_tensor(view(v_diag[:, slot, 0, :], 0, [[16 * HD, 4], [4 * HD, 4], [1, 4 * HD]]),
                                       view(kv_kept[:, slot, C:2 * C], 0, [[4 * HD, 4], [0, 4], [1, 4 * HD]]),
                                       view(a.group_mask[:, 0, :], 0, [[0, 4], [4 * HD, 4], [1, 4 * HD]]),
                                       ALU.mult).then_inc(v_ready, 1)
                if s % 2 == 1 and exists(2 * nb):
                    wait(pool, score, 6 * (nb - 1))
                    pool.nop(nofuse=True)
                    pool.tensor_copy(q_now[:, s // 2, :], a.qT[:, bass.ds(nb * T, T)]).then_inc(q_ready, 1)
                if exists(w + 1):
                    normalize(w + 1, (s + 1) % 4, 2)
                if exists(w + 2):
                    normalize(w + 2, (s + 2) % 4, 0)
                    normalize(w + 2, (s + 2) % 4, 1)

            def normalize(w, slot, part):
                first, count = PARTS[part]
                r = slice(first, first + count)
                pool.wait_ge(rden_ready, 3 * w + part + 1)
                pool.tensor_tensor(prob[:, slot, r, :], prob[:, slot, r, :],
                                   view(rden[:, slot, r], 0, [[1, count], [0, KEPT]]), ALU.mult).then_inc(probs, 1)

            pairs(pool, step)


def layer1_attention(nc, d, k):
    with ExitStack() as ctx:
        def sb(n, s, dt=F32):
            return ctx.enter_context(nc.sbuf_tensor(n, s, dt))

        a = Place()
        a.qT, a.kv = sb("qT1", [P, NTOK]), sb("kv1", [P, NT, 2 * C])
        a.wo_T, a.bo, a.gate_bias = sb("wo_T", [P, C]), sb("bo1", [P, 1]), sb("gate_bias1", [P, B])
        a.rank, a.places = sb("rank", [P, NT]), sb("places", [P, KEPT])
        a.group_mask, a.head_mask = sb("group_mask", [KEPT, 4, 4 * HD]), sb("head_mask1", [P, H])
        with ExitStack() as early:
            def tb(n, s):
                return early.enter_context(nc.sbuf_tensor(n, s, F32))

            k.hT = tb("hT1", [P, NTOK])
            a.w_rows = tb("w_rows1", [P, 4, C])
            a.wi1_rows, a.wi2, a.bi2 = tb("wi1_rows", [C // 2, C]), tb("wi2", [C // 2, 1]), tb("bi2", [P, 1])
            a.bq, a.bi1, a.bkv = tb("bq1", [P, 1]), tb("bi1", [C // 2, 1]), tb("bkv1", [P, 2 * C])
            a.before = tb("before", [P, 2, T])
            norm_phase(nc, k, "_n10", 1, 0, sparse_tables(nc, d, k, a))
            sparse_project_phase(nc, k, a)
        sparse_attention_phase(nc, k, a)


TOPK = 2
FF = 4 * C
FK = FF // P
CAPACITY = int(1.25 * NTOK * TOPK / E)
XS = 2 * P
XTILES = NTOK * TOPK // XS + E - 1
MAXT = NTOK // XS
SC = XTILES * XS // P
KT = TOPK * NT


def route_tables(nc, k, r, name, gate_w, gate_b, weights):
    r.w_in, r.const_ready, pool_step = (phase_semaphore(nc, k, n + name) for n in ("w_in", "const_ready", "pool_step"))
    r.rows_copied, r.logits_ready, r.h_stored = (phase_semaphore(nc, k, n + name) for n in ("rows_copied", "logits_ready", "h_stored"))
    r.tables_in = phase_semaphore(nc, k, "tables_in" + name)
    r.loads = 16 if gate_b is None else 32

    def beside(block):
        @block.sync
        def _(sp):
            sp.dma_start(r.w[:, :], gate_w).then_inc(r.w_in, 16)
            if gate_b is not None:
                sp.dma_start(r.bias[:, :], bass.AP(gate_b.tensor, 0, [[0, P], [1, E]])).then_inc(r.w_in, 16)
            for f, (_, b) in enumerate(weights.fc):
                sp.dma_start(r.fc_biases[:, :, f, :], b.rearrange("e (p f) -> p e f", p=P)).then_inc(r.tables_in, 16)
            for i, t in enumerate(weights.rows):
                sp.dma_start(r.out_rows[:, i, :, :], bass.AP(t.tensor, 0, [[0, P], [1, E * C]])).then_inc(r.tables_in, 16)
            for n in range(NCH):
                sp.wait_ge(r.rows_copied, n + 1)
                sp.dma_start(k.h_dram.rearrange("(n p) c -> p n c", p=P)[:, 4 * n:4 * n + 4, :],
                             r.rows[:, 4 * n:4 * n + 4, :]).then_inc(r.h_stored, 16)

        @block.gpsimd
        def _(pool):
            step = Chain(pool, pool_step)

            def count(out, pattern, base=0, channel_multiplier=0):
                step(pool.iota(out, pattern, base=base, channel_multiplier=channel_multiplier,
                               allow_small_or_imprecise_dtypes=True))

            step(pool.memset(r.earlier[:, :], 1.0))
            step(pool.affine_select(out=r.earlier[:, :], in_=r.earlier[:, :], compare_op=ALU.is_gt, fill=0.0, base=0,
                                    pattern=[[1, P]], channel_multiplier=-1))
            count(r.prio[:, :], [[-1, E]], base=E)
            count(r.steps[:, :, :], [[0, E], [XS, MAXT]])
            count(r.lane[:, :], [[1, P]])
            count(r.column[:, :], [[1, SC]])
            count(r.choice_id[:, :], [[P, KT]], base=1, channel_multiplier=1)
            count(r.slot_id[:, :], [[P, SC]], base=TOPK * NTOK + 1, channel_multiplier=1)
            count(r.tile_no[:, :, :], [[1, XTILES], [0, E]])
            pool.sem_inc(r.const_ready, 1)

    return beside


def route_phase(nc, k, r, name, biased, capacity):
    with ExitStack() as ctx:
        def sb(n, s, dt=F32):
            return ctx.enter_context(nc.sbuf_tensor(n + name, s, dt))

        def sem(n):
            return phase_semaphore(nc, k, n + name)

        logit = r.logits
        hit = sb("hit", [P, TOPK, NT, E])
        eq = sb("eq", [P, NT, E])
        top = sb("top", [P, TOPK, NT])
        best = sb("best", [P, NT])
        gap = sb("gap", [P, NT])
        total = sb("total", [P, KT, E])
        upto = sb("upto", [P, KT, E])
        rank = sb("rank_e", [P, KT, E])
        ranked = sb("ranked_e", [P, KT, E])
        keep = sb("keep", [P, KT])
        need = sb("need", [P, E])
        past = sb("past", [P, E])
        start = sb("start", [P, E])
        more = sb("more", [P, E, MAXT])
        slot = sb("slot_f", [P, KT])
        tile_e = sb("tile_e", [P, XTILES])
        slot_i, part_i = sb("slot_i", [P, KT], I32), sb("part_i", [P, 2, KT], I32)
        part_f = sb("part_f", [P, 2, KT])
        lane_hit = sb("lane_hit", [P, 8, P])
        column_hit = sb("column_hit", [P, 8, SC])
        owner = sb("owner", [P, SC])
        token_f, second, free = sb("token_f", [P, SC]), sb("second", [P, SC]), sb("free", [P, SC])
        ps = ctx.enter_context(nc.psum_tensor("ps_route" + name, [P, 3, CH], F32))
        bias, prio, earlier, steps, tile_no = r.bias, r.prio, r.earlier, r.steps, r.tile_no
        lane, column, choice_id, slot_id = r.lane, r.column, r.choice_id, r.slot_id
        dve_step = sem("dve_step")
        gap_ready, exp_ready, hit_ready, prefix_ready = sem("gap_ready"), sem("exp_ready"), sem("hit_ready"), sem("prefix_ready")
        slot_ready = sem("slot_ready")
        lane_ready, column_ready, placed = sem("lane_ready"), sem("column_ready"), sem("placed")
        block = ctx.enter_context(nc.Block())

        @block.sync
        def _(sp):
            sp.wait_ge(r.h_stored, 16 * NCH)

        @block.gpsimd
        def _(pool):
            pool.wait_ge(slot_ready, 1)
            for n in range(0, KT, 2):
                wait(pool, placed, n - 7)
                pool.tensor_scalar(column_hit[:, n % 8, :], column[:, :], part_f[:, 0, n:n + 1], choice_id[:, n:n + 1],
                                   ALU.is_equal, ALU.mult).then_inc(column_ready, 1)

        @block.tensor
        def _(pe):
            pe.wait_ge(r.const_ready, 1)
            pe.wait_ge(hit_ready, 1)
            h = hit[:, :, :, :].rearrange("p c t e -> p (c t e)")
            pe.matmul(ps[:, 0, :], earlier[:, :], h, start=True, stop=True)
            pe.matmul(ps[:, 1, :], k.ones[:, :], h, start=True, stop=True).then_inc(prefix_ready, 1)
            for n in range(KT):
                pe.wait_ge(lane_ready, n + 1)
                if n % 2 == 0:
                    pe.wait_ge(column_ready, n // 2 + 1)
                pe.matmul(ps[:, 2, 0:SC], lane_hit[:, n % 8, :], column_hit[:, n % 8, :], start=n == 0,
                          stop=n == KT - 1).then_inc(placed, 1)

        @block.scalar
        def _(act):
            act.wait_ge(gap_ready, 1)
            act.activation(gap[:, :], gap[:, :], ACT.Exp).then_inc(exp_ready, 1)

        @block.vector
        def _(dve):
            step = Chain(dve, dve_step)

            def over_e(v, n=NT):
                return view(v, 0, [[1, n], [0, E]])

            def for_all(v, n=NT):
                return view(v, 0, [[0, n], [1, E]])

            dve.wait_ge(r.logits_ready, 1)
            dve.wait_ge(r.const_ready, 1)
            dve.wait_ge(r.w_in, r.loads)
            if biased:
                step(dve.tensor_tensor(logit[:, :, :], logit[:, :, :], for_all(bias[:, :]), ALU.add))
            for c in range(TOPK):
                step(dve.tensor_reduce(top[:, c, :], logit[:, :, :], AX.X, ALU.max))
                step(dve.tensor_tensor(eq[:, :, :], logit[:, :, :], over_e(top[:, c, :]), ALU.is_equal))
                step(dve.tensor_tensor(eq[:, :, :], eq[:, :, :], for_all(prio[:, :]), ALU.mult))
                step(dve.tensor_reduce(best[:, :], eq[:, :, :], AX.X, ALU.max))
                step(dve.tensor_tensor(hit[:, c, :, :], eq[:, :, :], over_e(best[:, :]), ALU.is_equal))
                if c == 0:
                    step(dve.scalar_tensor_tensor(out=logit[:, :, :], in0=hit[:, 0, :, :], scalar=NEG, in1=logit[:, :, :],
                                                  op0=ALU.mult, op1=ALU.add))
            dve.tensor_tensor(gap[:, :], top[:, 1, :], top[:, 0, :], ALU.subtract).then_inc(gap_ready, 1)
            dve.sem_inc(hit_ready, 1)
            dve.wait_ge(prefix_ready, 1)
            within = ps[:, 0, :].rearrange("p (n e) -> p n e", e=E)
            step(dve.tensor_copy(total[:, :, :], ps[:, 1, :].rearrange("p (n e) -> p n e", e=E)))
            for e in range(E):
                m = dve.tensor_tensor_scan(view(upto[:, :, :], e, [[E, KT]]), k.ones[:, 0:KT],
                                           view(total[:, :, :], e, [[E, KT]]), 0.0, ALU.mult, ALU.add)
                step(m)
            step(dve.tensor_tensor(rank[:, :, :], upto[:, :, :], total[:, :, :], ALU.subtract))
            step(dve.tensor_tensor(rank[:, :, :], rank[:, :, :], within, ALU.add))
            step(dve.tensor_tensor(more[:, :, :], view(upto[:, KT - 1, :], 0, [[1, E], [0, MAXT]]), steps[:, :, :], ALU.is_gt))
            step(dve.tensor_reduce(need[:, :], more[:, :, :], AX.X, ALU.add))
            step(dve.tensor_tensor_scan(past[:, :], k.ones[:, 0:E], need[:, :], 0.0, ALU.mult, ALU.add))
            step(dve.tensor_tensor(start[:, :], past[:, :], need[:, :], ALU.subtract))
            step(dve.tensor_scalar(start[:, :], start[:, :], float(XS), None, ALU.mult))
            hits = hit[:, :, :, :].rearrange("p c t e -> p (c t) e")
            if capacity is not None:
                step(dve.tensor_tensor(ranked[:, :, :], rank[:, :, :], hits, ALU.mult))
                step(dve.tensor_reduce(keep[:, :], ranked[:, :, :], AX.X, ALU.add))
            step(dve.tensor_tensor(rank[:, :, :], rank[:, :, :], for_all(start[:, :], KT), ALU.add))
            step(dve.tensor_tensor(ranked[:, :, :], rank[:, :, :], hits, ALU.mult))
            step(dve.tensor_reduce(slot[:, :], ranked[:, :, :], AX.X, ALU.add))
            step(dve.tensor_copy(slot_i[:, :], slot[:, :]))
            step(dve.tensor_scalar(part_i[:, 0, :], slot_i[:, :], P.bit_length() - 1, None, ALU.logical_shift_right))
            step(dve.tensor_scalar(part_i[:, 1, :], slot_i[:, :], P - 1, None, ALU.bitwise_and))
            step(dve.tensor_copy(part_f[:, :, :], part_i[:, :, :]))
            dve.sem_inc(slot_ready, 1)
            for n in range(KT):
                wait(dve, placed, n - 7)
                if n % 2 == 1:
                    dve.tensor_scalar(column_hit[:, n % 8, :], column[:, :], part_f[:, 0, n:n + 1], choice_id[:, n:n + 1],
                                      ALU.is_equal, ALU.mult)
                dve.tensor_scalar(lane_hit[:, n % 8, :], lane[:, :], part_f[:, 1, n:n + 1], None,
                                  ALU.is_equal).then_inc(lane_ready, 1)
            step(dve.tensor_tensor(tile_no[:, :, :], tile_no[:, :, :], for_all(past[:, :], XTILES), ALU.is_ge))
            step(dve.tensor_reduce(tile_e[:, :], tile_no[:, :, :], AX.X, ALU.add))
            step(dve.tensor_scalar(r.expert[:, :], tile_e[:, :], float(E - 1), None, ALU.min))
            dve.wait_ge(exp_ready, 1)
            step(dve.tensor_scalar(best[:, :], gap[:, :], 1.0, None, ALU.add))
            step(dve.reciprocal(r.weight[:, 0:NT], best[:, :]))
            step(dve.tensor_tensor(r.weight[:, NT:KT], r.weight[:, 0:NT], gap[:, :], ALU.mult))
            if capacity is not None:
                step(dve.scalar_tensor_tensor(out=r.weight[:, :], in0=keep[:, :], scalar=float(capacity), in1=r.weight[:, :],
                                              op0=ALU.is_lt, op1=ALU.mult))
            dve.wait_ge(placed, KT)
            step(dve.tensor_copy(owner[:, :], ps[:, 2, 0:SC]))
            step(dve.tensor_scalar(second[:, :], owner[:, :], float(NTOK), float(-NTOK), ALU.is_gt, ALU.mult))
            step(dve.scalar_tensor_tensor(out=token_f[:, :], in0=owner[:, :], scalar=-1.0, in1=second[:, :],
                                          op0=ALU.add, op1=ALU.add))
            step(dve.tensor_scalar(r.token[:, :], token_f[:, :], 0.0, None, ALU.max))
            step(dve.scalar_tensor_tensor(out=free[:, :], in0=owner[:, :], scalar=0.0, in1=slot_id[:, :],
                                          op0=ALU.is_equal, op1=ALU.mult))
            step(dve.scalar_tensor_tensor(out=r.dest[:, :], in0=owner[:, :], scalar=-1.0, in1=free[:, :],
                                          op0=ALU.add, op1=ALU.add))


UNROLL = 4
LOOP_END = XTILES // UNROLL - 1


def expert_phase(nc, k, r, name, weights, gated):
    nf = len(weights.fc)
    nr = len(weights.rows)
    nw = nf + 2
    with ExitStack() as ctx:
        def sb(n, s, dt=F32):
            return ctx.enter_context(nc.sbuf_tensor(n + name, s, dt))

        def sem(n):
            return phase_semaphore(nc, k, n + name)

        fc = sb("fc", [P, UNROLL, nf, FF])
        proj = sb("proj", [P, UNROLL, FK, C])
        fc_bias = sb("fc_bias", [P, UNROLL, nf * FK])
        fc_biases, out_rows, tables_in = r.fc_biases, r.out_rows, r.tables_in
        x_rows = sb("x_rows", [P, UNROLL, 2, C])
        x_T = sb("x_T", [P, 2, XS])
        act1 = sb("act1", [P, 2, FK, XS])
        act2 = sb("act2", [P, 2, FK, XS]) if gated else None
        y = sb("y", [P, UNROLL, 2, C])
        token_now, dest_now = sb("token_now", [P, UNROLL, 2], I32), sb("dest_now", [P, UNROLL, 2], I32)
        ps_x = ctx.enter_context(nc.psum_tensor("ps_x" + name, [P, CH], F32))
        ps_h = ctx.enter_context(nc.psum_tensor("ps_h" + name, [P, nf, 2, 2, XS], F32))
        ps_o = ctx.enter_context(nc.psum_tensor("ps_o" + name, [P, 2, CH], F32))
        if gated:
            cen = sb("cen", [P, 2, 2, C])
            stats = sb("stats", [P, 2, 6])
            moments = sb("moments", [P, 2, 2, 2])
            inv_std = sb("inv_std", [P, 2, 2])
            exponent = sb("exponent", [P, 2])
            exponent_ready, var_ready, inv_ready = sem("exponent_ready"), sem("var_ready"), sem("inv_ready")
            biased, scaled = sem("biased"), sem("scaled")
            stats_ready = sem("stats_ready")
        halved = sem("halved")
        w_in = [sem(f"w_in{i}_") for i in range(UNROLL)]
        x_in = [sem(f"x_in{i}_") for i in range(UNROLL)]
        x_turned, x_copied, fc_ready, act_ready = sem("x_turned"), sem("x_copied"), sem("fc_ready"), sem("act_ready")
        g_ready, out_ready, out_read, y_ready = sem("g_ready"), sem("out_ready"), sem("out_read"), sem("y_ready")
        token_ready = sem("token_ready")
        stored = [sem(f"stored{i}_") for i in range(UNROLL)]
        block = ctx.enter_context(nc.Block())

        def exists(j):
            return not isinstance(j, int) or 0 <= j < XTILES

        def tiles(eng, step, first=0, last=XTILES):
            for j in range(first, UNROLL):
                step(j // UNROLL, j % UNROLL)
            with eng.Fori(1, LOOP_END) as i:
                for s in range(UNROLL):
                    step(i, s)
            for j in range(UNROLL * LOOP_END, last):
                step(j // UNROLL, j % UNROLL)

        def ring(i, s, n):
            return (s + n) % UNROLL, i + (s + n) // UNROLL + 1

        @block.sync
        def _(sp):
            if gated:
                sp.wait_ge(halved, 1)
            else:
                sp.wait_ge(tables_in, 16 * (nf + nr))

            def step(i, s):
                j = UNROLL * i + s
                wait(sp, out_ready, j - UNROLL + 1)
                e = sp.value_load(r.expert[0:1, bass.ds(j, 1)], min_val=0, max_val=E - 1)
                for f, (w, _) in enumerate(weights.fc):
                    sp.dma_start(fc[:, s, f, :], w[bass.ds(e, 1), :, :].rearrange("o p f -> (o p) f")).then_inc(w_in[s], 16)
                sp.dma_start(proj[:, s, :, :], weights.proj[bass.ds(e, 1), :, :].rearrange("o (p f) c -> (o p) f c", p=P)).then_inc(w_in[s], 16)
                sp.dma_start(fc_bias[:, s, :], fc_biases[:, bass.ds(e, 1), :, :]).then_inc(w_in[s], 16)

            tiles(sp, step)

        @block.tensor
        def _(pe):
            def first_layer(i, s):
                n = UNROLL * i + s + 1
                slot, count = ring(i, s, 1)
                pe.wait_ge(w_in[slot], 16 * nw * count)
                pe.wait_ge(x_copied, n + 1)
                for g in range(2):
                    for l in range(nf):
                        wait(pe, act_ready, 2 * nf * (n - 1) + g * nf + l + 1)
                        for f in (2 * g, 2 * g + 1):
                            m = pe.matmul(ps_h[:, l, g, f % 2, :], fc[:, slot, l, f:FF:FK], x_T[:, slot % 2, :],
                                          start=True, stop=True)
                        m.then_inc(fc_ready, 1)

            def turn(i, s):
                n = UNROLL * i + s + 2
                slot, count = ring(i, s, 2)
                pe.wait_ge(x_in[slot], 32 * count)
                wait(pe, x_copied, n)
                for h in range(2):
                    m = pe.transpose(ps_x[:, h * P:(h + 1) * P], x_rows[:, slot, h, :], k.ident[:, :])
                m.then_inc(x_turned, 1)

            def second_layer(j, s):
                pe.wait_ge(g_ready if gated else act_ready, 2 * j + 2)
                wait(pe, out_read if gated else y_ready, j - 1)
                for h in range(2):
                    for f in range(FK):
                        m = pe.matmul(ps_o[:, s % 2, h * P:(h + 1) * P], act1[:, s % 2, f, h * P:(h + 1) * P],
                                      proj[:, s, f, :], start=f == 0, stop=f == FK - 1)
                m.then_inc(out_ready, 1)

            def step(i, s):
                j = UNROLL * i + s
                if exists(j + 1):
                    first_layer(i, s)
                if exists(j + 2):
                    turn(i, s)
                if exists(j):
                    second_layer(j, s)

            tiles(pe, step, first=-2)

        @block.scalar
        def _(act):
            def step(i, s):
                n = UNROLL * i + s + 1
                if exists(n):
                    slot, _ = ring(i, s, 1)
                    for g in range(2):
                        for l in range(nf):
                            act.wait_ge(fc_ready, 2 * nf * n + g * nf + l + 1)
                            wait(act, out_ready, n - 1)
                            out = (act1, act2)[l]
                            for f in (2 * g, 2 * g + 1):
                                m = act.activation(out[:, slot % 2, f, :], ps_h[:, l, g, f % 2, :],
                                                   ACT.Tanh if l else ACT.Gelu, scale=0.5 if l else 1.0,
                                                   bias=fc_bias[:, slot, l * FK + f:l * FK + f + 1])
                            m.then_inc(act_ready, 1)
                n = n + 1
                if exists(n):
                    act.wait_ge(x_turned, n + 1)
                    wait(act, fc_ready, 2 * nf * (n - 1))
                    act.activation(x_T[:, s % 2, :], ps_x[:, 0:XS], ACT.Copy).then_inc(x_copied, 1)

            tiles(act, step, first=-2)

        @block.vector
        def _(dve):
            dve.tensor_copy(token_now[:, :, :], r.token[:, 0:2 * UNROLL].rearrange("p (s h) -> p s h", h=2)).then_inc(token_ready, 1)
            dve.wait_ge(tables_in, 16 * (nf + nr))
            if gated:
                dve.tensor_scalar(fc_biases[:, :, 1, :], fc_biases[:, :, 1, :], 0.5, None, ALU.mult).then_inc(halved, 1)

            def gate(n, slot, g):
                dve.wait_ge(act_ready, 4 * n + 2 * g + 2)
                a1 = act1[:, slot, 2 * g:2 * g + 2, :]
                dve.scalar_tensor_tensor(out=a1, in0=act2[:, slot, 2 * g:2 * g + 2, :], scalar=1.0, in1=a1,
                                         op0=ALU.add, op1=ALU.mult).then_inc(g_ready, 1)

            def rows(j):
                e = dve.value_load(r.expert[0:1, bass.ds(j, 1)], min_val=0, max_val=E - 1)
                return [view(out_rows[:, i, bass.ds(e, 1), :], 0, [[1, C]]) for i in range(nr)]

            def both(row):
                return view(row, 0, [[0, 2], [1, C]])

            def y_free(i, s):
                wait(dve, stored[s], 32 * i)
                dve.nop(nofuse=True)
                dve.tensor_copy(dest_now[:, s, :], r.dest[:, bass.ds(2 * (UNROLL * i + s), 2)])

            def next_tokens(j, s):
                dve.wait_ge(x_turned, j + 1)
                dve.nop(nofuse=True)
                dve.tensor_copy(token_now[:, s, :], r.token[:, bass.ds(2 * (j + UNROLL), 2)]).then_inc(token_ready, 1)

            def finish(i, s):
                j = UNROLL * i + s
                out_b, = rows(j)
                dve.wait_ge(out_ready, j + 1)
                y_free(i, s)
                dve.nop(nofuse=True)
                dve.tensor_tensor(y[:, s, :, :], ps_o[:, s % 2, 0:XS].rearrange("p (h c) -> p h c", h=2),
                                  both(out_b), ALU.add).then_inc(y_ready, 1)

            def residual(j, s, out_b):
                c = cen[:, s % 2, :, :]
                dve.wait_ge(out_ready, j + 1)
                dve.scalar_tensor_tensor(out=c, in0=ps_o[:, s % 2, 0:XS].rearrange("p (h c) -> p h c", h=2), scalar=0.5,
                                         in1=x_rows[:, s, :, :], op0=ALU.mult, op1=ALU.add).then_inc(out_read, 1)
                dve.wait_ge(out_read, j + 1)
                dve.nop(nofuse=True)
                dve.tensor_tensor(c, c, both(out_b), ALU.add).then_inc(biased, 1)
                dve.wait_ge(biased, j + 1)
                for h in range(2):
                    m = dve.bn_stats(stats[:, h, :], cen[:, s % 2, h, :])
                m.then_inc(stats_ready, 1)
                dve.wait_ge(stats_ready, j + 1)
                dve.nop(nofuse=True)
                for h in range(2):
                    m = dve.bn_aggr(moments[:, s % 2, h, :], stats[:, h, :])
                m.then_inc(var_ready, 1)

            def normalize(i, s, gamma, beta):
                j = UNROLL * i + s
                dve.wait_ge(inv_ready, j + 1)
                y_free(i, s)
                for h in range(2):
                    m = dve.scalar_tensor_tensor(out=y[:, s, h, :], in0=cen[:, s % 2, h, :], scalar=moments[:, s % 2, h, 0:1],
                                                 in1=gamma, op0=ALU.subtract, op1=ALU.mult)
                m.then_inc(scaled, 1)
                dve.wait_ge(scaled, j + 1)
                for h in range(2):
                    m = dve.scalar_tensor_tensor(out=y[:, s, h, :], in0=y[:, s, h, :], scalar=inv_std[:, s % 2, h:h + 1],
                                                 in1=beta, op0=ALU.mult, op1=ALU.add)
                m.then_inc(y_ready, 1)

            def step(i, s):
                j = UNROLL * i + s
                if gated:
                    if exists(j):
                        out_b, gamma, beta = rows(j)
                    if exists(j + 1):
                        gate(j + 1, (s + 1) % 2, 0)
                    if exists(j):
                        residual(j, s, out_b)
                    if exists(j + 1):
                        gate(j + 1, (s + 1) % 2, 1)
                    if exists(j):
                        if exists(j + UNROLL):
                            next_tokens(j, s)
                        normalize(i, s, gamma, beta)
                elif exists(j):
                    if exists(j + UNROLL):
                        next_tokens(j, s)
                    finish(i, s)

            tiles(dve, step, first=-1)

        @block.gpsimd
        def _(pool):
            if gated:
                pool.memset(exponent[:, :], -0.5).then_inc(exponent_ready, 1)
                pool.wait_ge(exponent_ready, 1)

            def gather(j, slot):
                pool.wait_ge(token_ready, 1 if isinstance(j, int) and j < UNROLL else j - UNROLL + 2)
                pool.nop(nofuse=True)
                for h in range(2):
                    pool.indirect_dma_start(out=x_rows[:, slot, h, :], out_offset=None, in_=k.h_dram,
                                            in_offset=bass.IndirectOffsetOnAxis(ap=token_now[:, slot, h:h + 1], axis=0)).then_inc(x_in[slot], 16)

            def scatter(j, slot):
                pool.wait_ge(y_ready, j + 1)
                pool.nop(nofuse=True)
                for h in range(2):
                    pool.indirect_dma_start(out=k.y_dram, out_offset=bass.IndirectOffsetOnAxis(ap=dest_now[:, slot, h:h + 1], axis=0),
                                            in_=y[:, slot, h, :], in_offset=None).then_inc(stored[slot], 16)

            for j in range(UNROLL):
                gather(j, j)

            def step(i, s):
                j = UNROLL * i + s
                if exists(j - 1):
                    scatter(j - 1, (s - 1) % UNROLL)
                if gated and exists(j):
                    pool.wait_ge(var_ready, j + 1)
                    pool.tensor_tensor(inv_std[:, s % 2, :], moments[:, s % 2, :, 1], exponent[:, :], ALU.pow).then_inc(inv_ready, 1)
                if exists(j + UNROLL) and exists(j):
                    pool.wait_ge(x_turned, j + 1)
                    if gated:
                        pool.wait_ge(out_read, j + 1)
                    pool.nop(nofuse=True)
                    gather(j + UNROLL, s)

            tiles(pool, step, last=XTILES + 1)
            for s in range(UNROLL):
                pool.wait_ge(stored[s], 32 * ((XTILES + UNROLL - 1 - s) // UNROLL))


def combine_phase(nc, k, r, name, layer):
    with ExitStack() as ctx:
        def sb(n, s, dt=F32):
            return ctx.enter_context(nc.sbuf_tensor(n + name, s, dt))

        def sem(n):
            return phase_semaphore(nc, k, n + name)

        got = sb("got", [P, TOPK, NT, C])
        part = sb("part", [P, 2, 4, C])
        both = sb("both", [P, 2, 4, C])
        ps = ctx.enter_context(nc.psum_tensor("ps_comb" + name, [P, 2, CH], F32))
        rows_in = [sem(f"rows_in{n}_") for n in range(NCH)]
        part_ready, both_ready, turned, added = sem("part_ready"), sem("both_ready"), sem("turned"), sem("added")
        block = ctx.enter_context(nc.Block())

        def rows(choice, n):
            first = choice * NT + 4 * n
            return k.y_dram.rearrange("(n p) c -> p n c", p=P)[:, first:first + 4, :]

        @block.sync
        def _(sp):
            for n in range(NCH):
                for c in range(TOPK):
                    sp.dma_start(got[:, c, 4 * n:4 * n + 4, :], rows(c, n)).then_inc(rows_in[n], 16)

        @block.tensor
        def _(pe):
            for n in range(NCH):
                pe.wait_ge(both_ready, 4 * (n + 1))
                wait(pe, added, 2 * (n - 1))
                for j in range(4):
                    m = pe.transpose(ps[:, n % 2, j * P:(j + 1) * P], both[:, n % 2, j, :], k.ident[:, :])
                m.then_inc(turned, 1)

        @block.scalar
        def _(act):
            for n in range(NCH):
                act.wait_ge(rows_in[n], 16 * TOPK)
                wait(act, both_ready, 4 * (n - 1))
                for j in range(4):
                    t = 4 * n + j
                    act.activation(part[:, n % 2, j, :], got[:, 0, t, :], ACT.Copy, scale=r.weight[:, t:t + 1]).then_inc(part_ready, 1)

        @block.vector
        def _(dve):
            for n in range(NCH + 1):
                if n < NCH:
                    wait(dve, turned, n - 1)
                    for j in range(4):
                        t = 4 * n + j
                        dve.wait_ge(part_ready, t + 1)
                        dve.scalar_tensor_tensor(out=both[:, n % 2, j, :], in0=got[:, 1, t, :], scalar=r.weight[:, NT + t:NT + t + 1],
                                                 in1=part[:, n % 2, j, :], op0=ALU.mult, op1=ALU.add).then_inc(both_ready, 1)
                if n >= 1:
                    m = n - 1
                    dve.wait_ge(turned, m + 1)
                    for s in range(2):
                        b = 2 * m + s
                        xs = k.xT[:, b * T:(b + 1) * T]
                        dve.scalar_tensor_tensor(out=xs, in0=ps[:, m % 2, s * T:(s + 1) * T], scalar=k.mod[:, layer, 5, b:b + 1],
                                                 in1=xs, op0=ALU.mult, op1=ALU.add).then_inc(added, 1)


def experts(nc, d, k, name, layer, gate_w, gate_b, capacity, weights, gated):
    with ExitStack() as ctx:
        def sb(n, s, dt=F32):
            return ctx.enter_context(nc.sbuf_tensor(n + name, s, dt))

        r = Place()
        r.weight, r.expert = sb("weight", [P, KT]), sb("expert", [P, XTILES], I32)
        r.token, r.dest = sb("token", [P, SC], I32), sb("dest", [P, SC], I32)
        r.fc_biases, r.out_rows = sb("fc_biases", [P, E, len(weights.fc), FK]), sb("out_rows", [P, len(weights.rows), E, C])
        with ExitStack() as early:
            def tb(n, s):
                return early.enter_context(nc.sbuf_tensor(n + name, s, F32))

            k.hT = tb("hT", [P, NTOK])
            r.w, r.bias, r.prio, r.earlier = tb("gate_w", [P, E]), tb("gate_b", [P, E]), tb("prio", [P, E]), tb("earlier", [P, P])
            r.steps, r.tile_no = tb("steps", [P, E, MAXT]), tb("tile_no", [P, XTILES, E])
            r.lane, r.column = tb("lane", [P, P]), tb("column", [P, SC])
            r.choice_id = tb("choice_id", [P, KT])
            r.slot_id = tb("slot_id", [P, SC])
            r.rows, r.logits = tb("h_rows", [P, NT, C]), tb("logit", [P, NT, E])
            norm_phase(nc, k, "_n" + name, layer, 1, route_tables(nc, k, r, name, gate_w, gate_b, weights), r)
            route_phase(nc, k, r, name, gate_b is not None, capacity)
        expert_phase(nc, k, r, "_x" + name, weights, gated)
        combine_phase(nc, k, r, "_c" + name, layer)


def layer0_experts(nc, d, k):
    w = Place()
    w.fc = [(d["L0_ffn_c_fc"], d["L0_ffn_fc_bias"].rearrange("e o f -> (e o) f"))]
    w.proj = d["L0_ffn_c_proj"]
    w.rows = [d["L0_ffn_proj_bias"]]
    experts(nc, d, k, "_m0", 0, d["L0_ffn_gate_w"], None, CAPACITY, w, False)


def layer1_experts(nc, d, k):
    w = Place()
    w.fc = [(d["L1_ffn_Wi"], d["L1_ffn_bi"]), (d["L1_ffn_Wg"], d["L1_ffn_bg"])]
    w.proj = d["L1_ffn_Wo"]
    w.rows = [d["L1_ffn_bo"], d["L1_ffn_gamma"], d["L1_ffn_beta"]]
    experts(nc, d, k, "_m1", 1, d["L1_ffn_Wr"], d["L1_ffn_br"], None, w, True)


class Place:
    pass


def output_phase(nc, d, k):
    with ExitStack() as ctx:
        rows = ctx.enter_context(nc.sbuf_tensor("out_rows", [P, NCH, CH], F32))
        ps = ctx.enter_context(nc.psum_tensor("ps_out", [P, 4, CH], F32))
        turned, copied_dve, copied_act, stored = (phase_semaphore(nc, k, n) for n in ("out_turned", "copied_dve", "copied_act", "out_stored"))
        block = ctx.enter_context(nc.Block())

        @block.tensor
        def _(pe):
            for n in range(NCH):
                wait(pe, copied_dve, (n - 2) // 2)
                wait(pe, copied_act, (n - 3) // 2)
                for j in range(4):
                    m = pe.transpose(ps[:, n % 4, j * P:(j + 1) * P], k.xT[:, (4 * n + j) * P:(4 * n + j + 1) * P], k.ident[:, :])
                m.then_inc(turned, 1)

        @block.vector
        def _(dve):
            for n in range(0, NCH, 2):
                dve.wait_ge(turned, n + 1)
                dve.tensor_copy(rows[:, n, :], ps[:, n % 4, :]).then_inc(copied_dve, 1)

        @block.scalar
        def _(act):
            for n in range(1, NCH, 2):
                act.wait_ge(turned, n + 1)
                act.activation(rows[:, n, :], ps[:, n % 4, :], ACT.Copy).then_inc(copied_act, 1)

        @block.sync
        def _(sp):
            out = d["out"].rearrange("(n p) c -> p n c", p=P)
            for n in range(NCH):
                sp.wait_ge(copied_act if n % 2 else copied_dve, n // 2 + 1)
                sp.dma_start(out[:, 4 * n:4 * n + 4, :], rows[:, n, :].rearrange("p (j c) -> p j c", j=4)).then_inc(stored, 16)
            sp.wait_ge(stored, 16 * NCH)


def build(nc, d):
    with ExitStack() as ctx:
        def sb(n, s, dt=F32):
            return ctx.enter_context(nc.sbuf_tensor(n, s, dt))

        k = Place()
        k.semaphores = []
        k.ident, k.ones, k.eps = sb("ident", [P, P]), sb("ones", [P, P]), sb("eps", [P, 1])
        k.mod = sb("mod", [P, 2, 6, B])
        k.xT = sb("xT", [P, NTOK])
        k.h_dram = nc.dram_tensor("h_dram", (NTOK, C), F32, kind="Internal").ap()
        k.y_dram = nc.dram_tensor("y_dram", (TOPK * NTOK + XTILES * XS, C), F32, kind="Internal").ap()
        setup_phase(nc, d, k)
        layer0_attention(nc, d, k)
        layer0_experts(nc, d, k)
        clear_semaphores(nc, k)
        layer1_attention(nc, d, k)
        layer1_experts(nc, d, k)
        output_phase(nc, d, k)


def layer0_attention(nc, d, k):
    with ExitStack() as ctx:
        def sb(n, s, dt=F32):
            return ctx.enter_context(nc.sbuf_tensor(n, s, dt))

        a = Place()
        a.ek_line = nc.dram_tensor("ek_line", (REL_W, HD), F32, kind="Internal").ap()
        a.ev_line = nc.dram_tensor("ev_line", (REL_W, HD), F32, kind="Internal").ap()
        a.ek_skew = nc.dram_tensor("ek_skew", (P, SKEW_W + HD), F32, kind="Internal").ap()
        a.ev_skew = nc.dram_tensor("ev_skew", (P, SKEW_W + HD), F32, kind="Internal").ap()
        a.qT, a.kT, a.v = sb("qT0", [P, NTOK]), sb("kT0", [P, NTOK]), sb("v0", [P, NT * C])
        a.ve = sb("ve", [P, VE_BLOCKS * VE_W])
        a.e_rel = sb("e_rel", [P, 3 * P])
        a.wproj, a.wproj_rel = sb("wproj0", [P, C]), sb("wproj_rel", [P, 8, C])
        a.bproj, a.gate_bias = sb("bproj0", [P, 1]), sb("gate_bias0", [P, B])
        a.head_mask, a.y_mask, a.t_mask = sb("head_mask", [P, H]), sb("y_mask", [P, 2, 64]), sb("t_mask", [P, TB])
        a.spread = sb("spread", [P, H * TB * HD])
        a.q_rel = sb("q_rel", [P, 2, HALF_TILES * P])
        with ExitStack() as early:
            def tb(n, s):
                return early.enter_context(nc.sbuf_tensor(n, s, F32))

            k.hT = tb("hT0", [P, NTOK])
            a.wqkv, a.bqk, a.bv, a.ek_wide = tb("wqkv0", [P, 3 * C]), tb("bqk0", [P, 2]), tb("bv0", [P, C]), tb("ek_wide", [P, (T + TB) * HD])
            norm_phase(nc, k, "_n00", 0, 0, rel_tables(nc, d, k, a))
            rel_project_phase(nc, k, a)
        a.q_diag = sb("q_diag", [P, 2, HALF_TILES * P])
        rel_attention_phase(nc, k, a)


INPUTS = [
    "L0_attn_x", "L0_attn_Wattn", "L0_attn_battn", "L0_attn_Wproj", "L0_attn_bproj", "L0_attn_embk", "L0_attn_embv",
    "L0_ffn_gate_w", "L0_ffn_c_fc", "L0_ffn_fc_bias", "L0_ffn_c_proj", "L0_ffn_proj_bias", "L0_c", "L0_wmod",
    "L1_attn_wq", "L1_attn_bq", "L1_attn_wk", "L1_attn_bk", "L1_attn_wv", "L1_attn_bv", "L1_attn_wo", "L1_attn_bo",
    "L1_attn_wi1", "L1_attn_bi1", "L1_attn_wi2", "L1_attn_bi2", "L1_ffn_Wr", "L1_ffn_br", "L1_ffn_Wi", "L1_ffn_bi",
    "L1_ffn_Wg", "L1_ffn_bg", "L1_ffn_Wo", "L1_ffn_bo", "L1_ffn_gamma", "L1_ffn_beta", "L1_c", "L1_wmod",
]


def kernel(**inputs):
    import numpy as np
    import concourse.bacc as bacc
    from concourse.bass_utils import run_bass_kernel_spmd

    nc = bacc.Bacc("TRN2", target_bir_lowering=False, num_devices=1)
    arrays, d = {}, {}
    for name in INPUTS:
        arrays[name] = np.ascontiguousarray(inputs[name])
        d[name] = nc.dram_tensor(name, arrays[name].shape, F32, kind="ExternalInput").ap()
    d["x"] = d["L0_attn_x"].rearrange("b t c -> (b t) c")
    out = nc.dram_tensor("out", (B, T, C), F32, kind="ExternalOutput").ap()
    d["out"] = out.rearrange("b t c -> (b t) c")
    build(nc, d)
    return run_bass_kernel_spmd(nc, [arrays], core_ids=[0]).results[0]["out"]
```
